# Optimizing a Trainium2 kernel written in Bass

```python
import numpy as np
import jax
import jax.numpy as jnp

def _softmax(x, axis=-1):
    return jax.nn.softmax(x, axis=axis)

def _gelu(x):
    return jax.nn.gelu(x, approximate=True)

def _silu(x):
    return jax.nn.silu(x)

def _sigmoid(x):
    return jax.nn.sigmoid(x)

def _layernorm(x, axis=-1, eps=1e-05):
    m = jnp.mean(x, axis=axis, keepdims=True)
    v = jnp.var(x, axis=axis, keepdims=True)
    return (x - m) / jnp.sqrt(v + eps)

def _scatter_add(tgt, idx, src, axis=0):
    return tgt.at[idx].add(src)

def _segment_sum(src, seg, n):
    return jax.ops.segment_sum(src, seg, n)
kernel_name = 'mk_gnn_preln_d2_gnn_r8_21e7b8'

def setup_inputs(seed: int=0):
    np.random.seed(seed)
    _w = jnp.asarray

    def _rec_inputs():
        import jax
        import jax.numpy as jnp
        _gk = jax.random.key(seed)
        x = -0.0002117 + 1 * jax.random.normal(jax.random.fold_in(_gk, 1), (12500, 256), jnp.float32)
        src = jax.random.randint(jax.random.fold_in(_gk, 2), (200000,), 0, 12500, jnp.int32)
        dst = jnp.minimum((12500 * jax.random.uniform(jax.random.fold_in(_gk, 3), (200000,)) ** 2.0).astype(jnp.int32), 99999)
        _o = jnp.argsort(dst, stable=True)
        src = src[_o]
        dst = dst[_o]
        edge_weight = jax.random.uniform(jax.random.fold_in(_gk, 13), (200000,), jnp.float32, 0.0, 1)
        edge_weight1 = jax.random.uniform(jax.random.fold_in(_gk, 14), (200000, 1), jnp.float32, 0.0, 1)
        return (x, src, dst, edge_weight, edge_weight1)
    x, src, dst, edge_weight, edge_weight1 = _rec_inputs()

    def _L0_gnn_setup():
        import jax, jax.numpy as jnp
        import numpy as np
        N_NODES = 12500
        N_EDGES = 400000
        IN_DIM = 256
        OUT_DIM = 256
        key = jax.random.key(seed)
        k1, k2, k3, k4, k5 = jax.random.split(key, 5)
        x = jax.random.normal(k1, (N_NODES, IN_DIM), dtype=jnp.float32)
        limit = np.sqrt(6.0 / (IN_DIM + OUT_DIM)).astype(np.float32)
        weight = jax.random.uniform(k2, (IN_DIM, OUT_DIM), dtype=jnp.float32, minval=-limit, maxval=limit)
        values = jax.random.uniform(k3, (N_EDGES,), dtype=jnp.float32)
        row = jnp.sort(jax.random.randint(k4, (N_EDGES,), 0, N_NODES, dtype=jnp.int32))
        col = jax.random.randint(k5, (N_EDGES,), 0, N_NODES, dtype=jnp.int32)
        return {'x': x, 'weight': weight, 'values': values, 'row': row, 'col': col}
    _L0_gnn_all = _L0_gnn_setup()
    _L0_gnn_in = {k: v for k, v in _L0_gnn_all.items() if k in ('weight',)}
    del _L0_gnn_all

    def _L1_gnn_setup():
        import jax, jax.numpy as jnp
        import numpy as np
        BS = 512
        EMBED = 256
        NHEAD = 8
        HDIM = EMBED // NHEAD
        E = BS * BS

        def _xavier(key, shape):
            lim = float(np.sqrt(6.0 / (shape[0] + shape[1])))
            return jax.random.uniform(key, shape, jnp.float32, -lim, lim)
        key = jax.random.key(seed)
        ks = jax.random.split(key, 6)
        feats = jax.random.normal(ks[0], (BS, EMBED), jnp.float32)
        dst = jnp.repeat(jnp.arange(BS), BS)
        src = jnp.tile(jnp.arange(BS), BS)
        edge_index = jnp.stack([src, dst], axis=1).astype(jnp.int32)
        edge_attr = jnp.zeros((E, 1), jnp.float32)
        return {'feats': feats, 'edge_index': edge_index, 'edge_attr': edge_attr, 'Wq': _xavier(ks[1], (EMBED, EMBED)), 'bq': jnp.zeros((EMBED,), jnp.float32), 'Wk': _xavier(ks[2], (EMBED, EMBED)), 'bk': jnp.zeros((EMBED,), jnp.float32), 'Wv': _xavier(ks[3], (EMBED, EMBED)), 'bv': jnp.zeros((EMBED,), jnp.float32), 'Wo': _xavier(ks[4], (EMBED, EMBED)), 'bo': jnp.zeros((EMBED,), jnp.float32)}
    _L1_gnn_all = _L1_gnn_setup()
    _L1_gnn_in = {k: v for k, v in _L1_gnn_all.items() if k in ('Wq', 'bq', 'Wk', 'bk', 'Wv', 'bv', 'Wo', 'bo')}
    del _L1_gnn_all
    return {'x': x, 'src': src, 'dst': dst, 'edge_weight': edge_weight, 'edge_weight1': edge_weight1, 'L0_gnn_weight': _L0_gnn_in['weight'], 'L1_gnn_Wq': _L1_gnn_in['Wq'], 'L1_gnn_bq': _L1_gnn_in['bq'], 'L1_gnn_Wk': _L1_gnn_in['Wk'], 'L1_gnn_bk': _L1_gnn_in['bk'], 'L1_gnn_Wv': _L1_gnn_in['Wv'], 'L1_gnn_bv': _L1_gnn_in['bv'], 'L1_gnn_Wo': _L1_gnn_in['Wo'], 'L1_gnn_bo': _L1_gnn_in['bo']}

def reference(x, src, dst, edge_weight, edge_weight1, L0_gnn_weight, L1_gnn_Wq, L1_gnn_bq, L1_gnn_Wk, L1_gnn_bk, L1_gnn_Wv, L1_gnn_bv, L1_gnn_Wo, L1_gnn_bo):
    import jax
    import jax.numpy as jnp

    def _L0_gnn_ref(x, weight, values, row, col):
        import jax, jax.numpy as jnp
        import numpy as np
        N_NODES = 12500
        N_EDGES = 400000
        IN_DIM = 256
        OUT_DIM = 256
        h = x @ weight
        msgs = values[:, None] * h[col]
        out = jax.ops.segment_sum(msgs, row, num_segments=N_NODES)
        return out

    def _L1_gnn_ref(feats, edge_index, edge_attr, Wq, bq, Wk, bk, Wv, bv, Wo, bo):
        import jax, jax.numpy as jnp
        import numpy as np
        BS = 512
        EMBED = 256
        NHEAD = 8
        HDIM = EMBED // NHEAD
        E = BS * BS

        def _xavier(key, shape):
            lim = float(np.sqrt(6.0 / (shape[0] + shape[1])))
            return jax.random.uniform(key, shape, jnp.float32, -lim, lim)
        bs = feats.shape[0]
        scale = 1.0 / np.sqrt(HDIM)
        q = (feats @ Wq.T + bq).reshape(bs, NHEAD, HDIM).transpose(1, 0, 2)
        k = (feats @ Wk.T + bk).reshape(bs, NHEAD, HDIM).transpose(1, 0, 2)
        v = (feats @ Wv.T + bv).reshape(bs, NHEAD, HDIM).transpose(1, 0, 2)
        r, c = (edge_index[:, 0], edge_index[:, 1])
        qe = q[:, c, :]
        ke = k[:, r, :]
        ve = v[:, r, :]
        sim = jnp.einsum('hed,hed->eh', qe, ke) * scale
        m = jax.ops.segment_max(sim, c, num_segments=bs)
        p = jnp.exp(sim - m[c])
        s = jax.ops.segment_sum(p, c, num_segments=bs)
        attn = p / s[c]
        out_e = attn.T[..., None] * ve
        out_e = out_e.transpose(1, 0, 2).reshape(-1, NHEAD * HDIM)
        agg = jax.ops.segment_sum(out_e, c, num_segments=bs)
        return agg @ Wo.T + bo
    edge_index_t = jnp.stack([src, dst], axis=1)
    h = jnp.maximum(_layernorm(x, axis=-1), 0.0)
    x = x + _L0_gnn_ref(h, L0_gnn_weight, edge_weight, src, dst)
    h = jnp.maximum(_layernorm(x, axis=-1), 0.0)
    x = x + _L1_gnn_ref(h, edge_index_t, edge_weight1, L1_gnn_Wq, L1_gnn_bq, L1_gnn_Wk, L1_gnn_bk, L1_gnn_Wv, L1_gnn_bv, L1_gnn_Wo, L1_gnn_bo)
    return x

_drawn_inputs = setup_inputs


def setup_inputs(seed=0):
    import zlib

    import numpy as np

    out = dict(_drawn_inputs(seed))
    spreads = {'L1_gnn_bq': (0.0, 2.0),
     'L1_gnn_bk': (0.0, 2.0),
     'L1_gnn_bv': (0.0, 0.316),
     'L1_gnn_bo': (0.0, 0.316)}
    factors = {'L1_gnn_Wq': 8.0, 'L1_gnn_Wk': 8.0}
    for name, (base, spread) in spreads.items():
        noise = np.random.default_rng([zlib.crc32(name.encode()), seed]).standard_normal(out[name].shape)
        drawn = base * np.exp(spread * noise) if base else spread * noise
        out[name] = jnp.asarray(drawn.astype(out[name].dtype))
    for name, factor in factors.items():
        out[name] = (out[name] * factor).astype(out[name].dtype)
    return out
```

```python
from contextlib import ExitStack

import numpy as np

import concourse.bass as bass
from concourse import mybir

P = 128
N = 12500
E = 200000
D = 256
NH = 8
NB = 98
NLAST = N - (NB - 1) * P
T = 1563
J = T + NB - 1
JP = 13 * P
W = 8
NW = -(-J // W)
KVW = 256 + NH * 33
ROW = 257
BIG = 1.0e30
SCALE = float(np.float32(1.0) / np.sqrt(np.float32(32.0)))

F32 = mybir.dt.float32
I32 = mybir.dt.int32
BF16 = mybir.dt.bfloat16
ALU = mybir.AluOpType
ACT = mybir.ActivationFunctionType
AX = mybir.AxisListType


class Engine:

    def __init__(self, sem):
        self.sem = sem
        self.count = 0
        self.todo = []
        self.seen = {}

    def waits(self, tokens):
        for t in tokens:
            if t is None:
                continue
            sem, value = t
            if self.seen.get(id(sem), 0) < value:
                self.seen[id(sem)] = value
                self.todo.append(lambda e, sem=sem, value=value: e.wait_ge(sem, value))

    def op(self, fn, *tokens):
        self.waits(tokens)
        self.count += 1
        sem = self.sem
        self.todo.append(lambda e: fn(e).then_inc(sem, 1))
        return (sem, self.count)

    def do(self, fn, *tokens):
        self.waits(tokens)
        self.todo.append(fn)


class Slot:

    def __init__(self, sem):
        self.sem = sem
        self.count = 0

    def dma(self, eng, fn, *tokens):
        eng.waits(tokens)
        self.count += 16
        sem = self.sem
        eng.todo.append(lambda e: fn(e).then_inc(sem, 16))
        return (sem, self.count)

    @property
    def token(self):
        return (self.sem, self.count)


def build(nc, x, src, dst, edge_weight, weight, Wq, bq, Wk, bk, Wv, bv, Wo, bo, out, dump=None):
    def dram(name, shape, dt=F32):
        return nc.dram_tensor(name, shape, dt, kind="Internal").ap()

    fields = dram("fields", (JP, 5 * P))
    posrows = dram("posrows", (JP, P))
    dvec = dram("dvec", (8, JP))
    ivec = dram("ivec", (8, JP), I32)
    bvec = dram("bvec", (1, P))
    msgs = dram("msgs", (T * P, ROW))
    srcs = dram("srcs", (E,), I32)
    dsts = dram("dsts", (E,), I32)
    ws = dram("ws", (E,))
    recs = [dram(f"recs{k}", (T * P, 4)) for k in range(2)]
    kvt = dram("kvt", (NB * P, KVW))
    qt = dram("qt", (NB * P, D))
    x1t = dram("x1t", (NB * P, D))

    with ExitStack() as top:
        top.enter_context(nc.allow_non_contiguous_dma(reason="vectors of one element per partition"))

        def mksem(name):
            return top.enter_context(nc.semaphore(name))

        def sb(stack, name, shape, dt=F32):
            return stack.enter_context(nc.sbuf_tensor(name, shape, dt))

        psum = [top.enter_context(nc.psum_tensor(f"ps{i}", [P, 512], F32)) for i in range(8)]
        iota = sb(top, "iota", [P, P])
        ident = sb(top, "ident", [P, P])
        tri = sb(top, "tri", [P, P])
        trib = sb(top, "trib", [P, P], BF16)
        onesb = sb(top, "onesb", [P, 2], BF16)
        unsorted = sb(top, "unsorted", [1, 1], I32)

        def phase(name, program, slots):
            with ExitStack() as stack:
                sems = {k: stack.enter_context(nc.semaphore(f"{name}_{k}")) for k in ("pe", "dve", "act", "pool", "sp")}
                eng = {k: Engine(s) for k, s in sems.items()}
                slot = {}
                for k, n in slots.items():
                    slot[k] = [Slot(stack.enter_context(nc.semaphore(f"{name}_{k}{i}"))) for i in range(n)]
                program(stack, eng, slot)
                block = stack.enter_context(nc.Block())
                for key, deco in (("pe", block.tensor), ("dve", block.vector), ("act", block.scalar),
                                  ("pool", block.gpsimd), ("sp", block.sync)):
                    def run(e, todo=eng[key].todo):
                        for fn in todo:
                            fn(e)
                    deco(run)

        def four(kept, e, name):
            if "regs" not in kept:
                kept["regs"] = [e.alloc_register(f"{name}{i}") for i in range(4)]
            return kept["regs"]

        def ranks(stack, en, keyT, ready, name):
            pe, dve = en["pe"], en["dve"]
            onehot = sb(stack, f"onehot{name}", [P, 4, P], BF16)
            scr = sb(stack, f"scr{name}", [P, 2, P])
            C = sb(stack, f"C{name}", [P, T])
            Cs = sb(stack, f"Cs{name}", [P, T])
            base = sb(stack, f"base{name}", [P, 1])
            pos = sb(stack, f"pos{name}", [P, JP])
            free = [None] * 4

            def digits(t):
                return dve.op(lambda e: e.tensor_scalar(onehot[:, t % 4, :], iota[:, :], keyT[:, t:t + 1], None,
                                                        ALU.is_equal), free[t % 4])

            t_one = dve.op(lambda e: e.memset(C[:, :], 1.0))
            dve.waits(ready)
            hist = None
            for t in range(T):
                o = digits(t)
                hist = free[t % 4] = pe.op(
                    lambda e, t=t: e.matmul(psum[2 + t // 512][:, t % 512:t % 512 + 1], lhsT=onehot[:, t % 4, :],
                                            rhs=onesb[:, 0:1], start=True, stop=True), o)
            scan = None
            for k in range(4):
                n = min(512, T - 512 * k)
                first = scan is None
                scan = dve.op(lambda e, k=k, n=n, first=first: e.tensor_tensor_scan(
                    Cs[:, 512 * k:512 * k + n], C[:, 512 * k:512 * k + n], psum[2 + k][:, 0:n],
                    0.0 if first else Cs[:, 512 * k - 1:512 * k], ALU.mult, ALU.add), hist, t_one, scan)
            a = pe.op(lambda e: e.matmul(psum[6][:, 0:1], lhsT=tri[:, :], rhs=Cs[:, T - 1:T], start=True, stop=True),
                      scan)
            t_base = dve.op(lambda e: e.tensor_copy(base[:, :], psum[6][:, 0:1]), a)
            for k in range(4):
                n = min(512, T - 512 * k)
                a = dve.op(lambda e, k=k, n=n: e.tensor_tensor(
                    C[:, 512 * k:512 * k + n], Cs[:, 512 * k:512 * k + n], psum[2 + k][:, 0:n], ALU.subtract), scan)
            t_B = dve.op(lambda e: e.tensor_scalar(C[:, :], C[:, :], base[:, 0:1], None, ALU.add), a, t_base)

            ps_free = [None] * 2
            held = []
            r = None

            def reduce(t, m):
                return dve.op(lambda e: e.tensor_tensor_reduce(
                    scr[:, t % 2, :], onehot[:, t % 4, :], psum[t % 2][:, 0:P], 1.0, 0.0, ALU.mult, ALU.add,
                    pos[:, t:t + 1]), m)

            pe.waits(ready)
            for t in range(T):
                o = digits(t)
                pe.op(lambda e, t=t: e.matmul(psum[t % 2][:, 0:P], lhsT=trib[:, :], rhs=onehot[:, t % 4, :],
                                              start=True, stop=False), o, ps_free[t % 2])
                m = pe.op(lambda e, t=t: e.matmul(psum[t % 2][:, 0:P], lhsT=C[:, t:t + 1].to_broadcast([P, P]),
                                                  rhs=ident[:, :], start=False, stop=True), t_B)
                held.append((t, m))
                if len(held) == 2 or t == T - 1:
                    tt, mm = held.pop(0)
                    r = ps_free[tt % 2] = free[tt % 4] = reduce(tt, mm)
            for tt, mm in held:
                r = reduce(tt, mm)
            t_pos = dve.op(lambda e: e.memset(pos[:, T:JP], float(E)))
            return pos, base, t_base, t_pos, r

        def start(stack, en, sl):
            pe, dve, act, pool, sp = (en[k] for k in ("pe", "dve", "act", "pool", "sp"))
            inti = sb(stack, "inti", [P, P], I32)
            da = sb(stack, "da", [125, 1600], I32)
            db = sb(stack, "db", [125, 1600], I32)
            df = sb(stack, "df", [125, 1600])
            ds = sb(stack, "ds", [P, 1])
            a = pool.op(lambda e: e.iota(inti[:, :], pattern=[[1, P]], base=0, channel_multiplier=0))
            t_iota = dve.op(lambda e: e.tensor_copy(iota[:, :], inti[:, :]), a)
            a = pool.op(lambda e: e.iota(inti[:, :], pattern=[[1, P]], base=0, channel_multiplier=-1), t_iota)
            t1 = dve.op(lambda e: e.tensor_scalar(ident[:, :], inti[:, :], 0.0, None, ALU.is_equal), a)
            t2 = dve.op(lambda e: e.tensor_scalar(tri[:, :], inti[:, :], 0.0, None, ALU.is_gt), a)
            t_tri = dve.op(lambda e: e.tensor_copy(trib[:, :], tri[:, :]), t2)
            t_onesb = dve.op(lambda e: e.memset(onesb[:, :], 1.0))

            for i, (to, vec) in enumerate(((srcs, src), (dsts, dst), (ws, edge_weight))):
                sl["cp"][i].dma(sp, lambda e, to=to, vec=vec: e.dma_start(
                    to.rearrange("(p e) -> p e", e=3125), vec.rearrange("(p e) -> p e", e=3125)))
            z = dve.op(lambda e: e.memset(db[:, :], 1 << 20))
            z2 = dve.op(lambda e: e.memset(ds[:, :], 0.0))
            la = sl["ld"][0].dma(sp, lambda e: e.dma_start(da[:, :], dst.rearrange("(p e) -> p e", e=1600)))
            lb = sl["ld"][1].dma(sp, lambda e: e.dma_start(db[0:124, :],
                                                           dst[1:1 + 124 * 1600].rearrange("(p e) -> p e", e=1600)), z)
            lc = sl["ld"][2].dma(sp, lambda e: e.dma_start(db[124:125, 0:1599],
                                                           dst[1 + 124 * 1600:E].rearrange("(p e) -> p e", e=1599)))
            a = dve.op(lambda e: e.tensor_tensor(df[:, :], da[:, :], db[:, :], ALU.is_gt), la, lb, lc)
            a = dve.op(lambda e: e.tensor_reduce(ds[0:125, :], df[:, :], AX.X, ALU.add), a, z2)
            onef = sb(stack, "onef", [P, 1])
            o = dve.op(lambda e: e.memset(onef[:, :], 1.0))
            a = pe.op(lambda e: e.matmul(psum[0][0:1, 0:1], lhsT=ds[:, :], rhs=onef[:, :], start=True, stop=True), a, o)
            dve.op(lambda e: e.tensor_copy(unsorted[:, :], psum[0][0:1, 0:1]), a)
            sp.waits([c.token for c in sl["cp"]])

        phase("start", start, {"cp": 3, "ld": 3})

        def sort_pass(k):
            def program(stack, en, sl):
                pe, dve, act, pool, sp = (en[x] for x in ("pe", "dve", "act", "pool", "sp"))
                (ld,) = sl["ld"]
                rec = sb(stack, f"rec{k}", [P, T, 4])
                ri = sb(stack, f"ri{k}", [P, 2, T], I32)
                keyT = sb(stack, f"keyT{k}", [P, JP])
                posI = sb(stack, f"posI{k}", [P, T], I32)
                z = dve.op(lambda e: e.memset(ri[:, :, :], 16383))
                z1 = dve.op(lambda e: e.memset(rec[:, :, :], 0.0))
                full = (T - 1) * P
                if k == 0:
                    for i, vec in enumerate((srcs, dsts)):
                        l = ld.dma(sp, lambda e, i=i, vec=vec: e.dma_start(
                            ri[:, i, 0:T - 1], vec[0:full].rearrange("(t p) -> p t", p=P)), z, ld.token)
                        l = ld.dma(sp, lambda e, i=i, vec=vec: e.dma_start(
                            ri[0:64, i, T - 1:T], vec[full:E].rearrange("(t p) -> p t", p=64)), l)
                    l = ld.dma(sp, lambda e: e.dma_start(
                        rec[:, 0:T - 1, 2], ws[0:full].rearrange("(t p) -> p t", p=P)), z1, l)
                    l = ld.dma(sp, lambda e: e.dma_start(
                        rec[0:64, T - 1, 2:3], ws[full:E].rearrange("(t p) -> p t", p=64)), l)
                    for i in range(2):
                        l = dve.op(lambda e, i=i: e.tensor_copy(rec[:, :, i], ri[:, i, :]), ld.token)
                else:
                    l = ld.dma(sp, lambda e: e.dma_start(rec[:, :, :], recs[0].rearrange("(t p) f -> p t f", p=P)),
                               z1)
                    l = dve.op(lambda e: e.tensor_copy(ri[:, 1, :], rec[:, :, 1]), l, z)
                if k == 0:
                    a = dve.op(lambda e: e.tensor_scalar(ri[:, 0, :], ri[:, 1, :], 127, None, ALU.bitwise_and), l)
                else:
                    a = dve.op(lambda e: e.tensor_scalar(ri[:, 0, :], ri[:, 1, :], 7, None,
                                                         ALU.logical_shift_right), l)
                a = dve.op(lambda e: e.tensor_copy(keyT[:, 0:T], ri[:, 0, :]), a)
                pos, _, _, _, r = ranks(stack, en, keyT, [a], f"s{k}")
                a = dve.op(lambda e: e.tensor_copy(posI[:, :], pos[:, 0:T]), r)
                for t in range(T):
                    s = sl["sc"][t % 8]
                    s.dma(pool, lambda e, t=t: e.indirect_dma_start(
                        recs[k], bass.IndirectOffsetOnAxis(ap=posI[:, t:t + 1], axis=0), rec[:, t, :], None),
                        a, s.token)
                done = [s.token for s in sl["sc"]]
                if k == 1:
                    l = ld.dma(sp, lambda e: e.dma_start(rec[:, :, :], recs[1].rearrange("(t p) f -> p t f", p=P)),
                               *done)
                    for i in range(2):
                        a = dve.op(lambda e, i=i: e.tensor_copy(ri[:, i, :], rec[:, :, i]), l)
                    dve_done = a
                    for i, (vec, t) in enumerate(((srcs, ri[:, 0, :]), (dsts, ri[:, 1, :]), (ws, rec[:, :, 2]))):
                        l = ld.dma(sp, lambda e, vec=vec, t=t: e.dma_start(
                            vec[0:full].rearrange("(t p) -> p t", p=P), t[:, 0:T - 1]), dve_done, l)
                        l = ld.dma(sp, lambda e, vec=vec, t=t: e.dma_start(
                            vec[full:E].rearrange("(t p) -> p t", p=64), t[0:64, T - 1:T]), l)
                    done.append(l)
                sp.waits(done)
            return program

        with nc.If(nc.values_load(unsorted[0:1, 0:1], min_val=0, max_val=E) > 0):
            phase("sort0", sort_pass(0), {"ld": 1, "sc": 8})
            phase("sort1", sort_pass(1), {"ld": 1, "sc": 8})

        def prep(stack, en, sl):
            pe, dve, act, pool, sp = (en[k] for k in ("pe", "dve", "act", "pool", "sp"))
            (gen,) = sl["gen"]
            (ld0,), (ld1,), (ld2,) = sl["ld0"], sl["ld1"], sl["ld2"]
            (st,) = sl["st"]
            ints = sb(stack, "ints", [P, 2, 13, P], I32)
            blk = sb(stack, "blk", [P, 13, P], I32)
            fr = sb(stack, "fr", [P, 13, 5, P])
            sblkf = sb(stack, "sblkf", [P, 13, P])
            sbT = sb(stack, "sbT", [P, JP])
            ones = sb(stack, "onesrow", [P, JP])
            basebc = sb(stack, "basebc", [P, P])
            posr = sb(stack, "posr", [P, 13, P])
            scr = sb(stack, "scr", [P, 2, P])
            cvec = sb(stack, "cvec", [P, 2, 13])
            cbc = sb(stack, "cbc", [P, JP])
            jcol = sb(stack, "jcol", [P, 13])
            jcoli = sb(stack, "jcoli", [P, 13], I32)
            cnt = sb(stack, "cnt", [P, 2, 13])
            tj = sb(stack, "tj", [P, 2, 2, 13])
            tji = sb(stack, "tji", [P, 2, 2, 13], I32)
            zrow = sb(stack, "zrow", [64, ROW])

            t_ones = dve.op(lambda e: e.memset(ones[:, :], 1.0))
            a = pool.op(lambda e: e.iota(jcoli[:, :], pattern=[[P, 13]], base=0, channel_multiplier=1))
            t_j = dve.op(lambda e: e.tensor_copy(jcol[:, :], jcoli[:, :]), a)

            m0 = dve.op(lambda e: e.memset(ints[:, :, :, :], 16383))
            m1 = dve.op(lambda e: e.memset(fr[:, 12, 2, :], 0.0))
            full = 12 * P * P
            rest = full + 26 * P

            def load_rows(slot, dst_ap, vec, *tok):
                slot.dma(sp, lambda e: e.dma_start(dst_ap(slice(0, P), slice(0, 12), P),
                                                   vec[0:full].rearrange("(c p e) -> p c e", p=P, e=P)), *tok)
                slot.dma(sp, lambda e: e.dma_start(dst_ap(slice(0, 26), 12, P),
                                                   vec[full:rest].rearrange("(p e) -> p e", e=P)))
                slot.dma(sp, lambda e: e.dma_start(dst_ap(slice(26, 27), 12, 64),
                                                   vec[rest:E].rearrange("(p e) -> p e", e=64)))
            load_rows(ld0, lambda p, c, n: ints[p, 0, c, 0:n], srcs, m0)
            load_rows(ld1, lambda p, c, n: ints[p, 1, c, 0:n], dsts, m0)
            load_rows(ld2, lambda p, c, n: fr[p, c, 2, 0:n], ws, m1)

            a = dve.op(lambda e: e.tensor_scalar(blk[:, :, :], ints[:, 0, :, :], 7, None, ALU.logical_shift_right),
                       ld0.token)
            t_sblk = dve.op(lambda e: e.tensor_copy(sblkf[:, :, :], blk[:, :, :]), a)
            f_src = dve.op(lambda e: e.tensor_copy(fr[:, :, 0, :], ints[:, 0, :, :]))
            f_dst = dve.op(lambda e: e.tensor_copy(fr[:, :, 1, :], ints[:, 1, :, :]), ld1.token)
            a = dve.op(lambda e: e.tensor_scalar(blk[:, :, 0], ints[:, 1, :, 0], 7, None, ALU.logical_shift_right),
                       t_sblk)
            a = dve.op(lambda e: e.tensor_copy(cnt[:, 0, :], blk[:, :, 0]), a)
            t_cd = dve.op(lambda e: e.tensor_tensor(cvec[:, 0, :], cnt[:, 0, :], jcol[:, :], ALU.add), a, t_j)
            k1 = dve.op(lambda e: e.memset(fr[:, :, 3, 0:1], 1.0))
            k2 = dve.op(lambda e: e.memset(fr[:, :, 4, P - 1:P], 1.0))
            k3 = dve.op(lambda e: e.tensor_tensor(fr[:, :, 3, 1:P], fr[:, :, 1, 1:P], fr[:, :, 1, 0:P - 1],
                                                  ALU.not_equal), f_dst)
            k4 = dve.op(lambda e: e.tensor_copy(fr[:, :, 4, 0:P - 1], fr[:, :, 3, 1:P]), k3)
            t_fields = gen.dma(sp, lambda e: e.dma_start(
                fields.rearrange("(c p) f -> p c f", p=P), fr[:, :, :, :].rearrange("p c a b -> p c (a b)")),
                k1, k2, k4, f_src, ld2.token)

            prev = [None, None]
            for c in range(13):
                b = psum[c % 2]
                a = pe.op(lambda e, c=c, b=b: e.transpose(b[:, 0:P], sblkf[:, c, :], ident[:, :]),
                          t_sblk, prev[c % 2])
                prev[c % 2] = act.op(lambda e, c=c, b=b: e.copy(sbT[:, c * P:(c + 1) * P], b[:, 0:P]), a)

            pos, base, t_base, t_pos, sl_ = ranks(stack, en, sbT, prev, "a")
            a = gen.dma(sp, lambda e: e.dma_start(bvec.rearrange("a b -> b a"), base[:, :]), t_base, t_fields)
            t_bbc = gen.dma(sp, lambda e: e.dma_start(basebc[:, :], bvec.to_broadcast([P, P])), a)
            prev = [sl_, sl_]
            for c in range(13):
                b = psum[c % 2]
                a = pe.op(lambda e, c=c, b=b: e.transpose(b[:, 0:P], pos[:, c * P:(c + 1) * P], ident[:, :]),
                          t_pos, prev[c % 2])
                prev[c % 2] = act.op(lambda e, c=c, b=b: e.copy(posr[:, c, :], b[:, 0:P]), a)
            gen.dma(sp, lambda e: e.dma_start(posrows.rearrange("(c p) e -> p c e", p=P), posr[:, :, :]),
                    prev[0], prev[1], t_bbc)

            a = dve.op(lambda e: e.tensor_scalar(cnt[:, 1, :], jcol[:, :], float(P), None, ALU.mult), t_cd)
            last = None
            for c in range(13):
                last = dve.op(lambda e, c=c: e.tensor_scalar(scr[:, c % 2, 1:P], basebc[:, 1:P],
                                                             cnt[:, 1, c:c + 1], 0.0, ALU.is_le, ALU.add,
                                                             accum_out=cvec[:, 1, c:c + 1]), t_bbc, a, last)
            t_cs = dve.op(lambda e: e.tensor_tensor(cvec[:, 1, :], cvec[:, 1, :], jcol[:, :], ALU.add), last)

            tok = t_cs
            dtok = (gen.sem, gen.count)
            for k in range(2):
                dtok = gen.dma(sp, lambda e, k=k: e.dma_start(dvec[k:k + 1, :].rearrange("a (c p) -> p (a c)", p=P),
                                                              cvec[:, k, :]), tok, dtok)
                dtok = gen.dma(sp, lambda e, k=k: e.dma_start(cbc[:, :], dvec[k:k + 1, :].to_broadcast([P, JP])),
                               dtok)
                for c in range(13):
                    tok = dve.op(lambda e, c=c, k=k: e.tensor_scalar(
                        ones[:, 0:T], cbc[:, 0:T], jcol[:, c:c + 1], 0.0, ALU.is_le, ALU.add,
                        accum_out=cnt[:, k, c:c + 1]), dtok, tok)
                tok = dve.op(lambda e, k=k: e.tensor_scalar(tj[:, k, 0, :], cnt[:, k, :], -1.0, 0.0, ALU.add,
                                                            ALU.max), tok)
                tok = dve.op(lambda e, k=k: e.tensor_tensor(tj[:, k, 1, :], jcol[:, :], tj[:, k, 0, :],
                                                            ALU.subtract), tok)
                tok = dve.op(lambda e, k=k: e.tensor_copy(tji[:, k, :, :], tj[:, k, :, :]), tok)
                for i in range(2):
                    dtok = gen.dma(sp, lambda e, k=k, i=i: e.dma_start(
                        dvec[2 + 2 * k + i:3 + 2 * k + i, :].rearrange("a (c p) -> p (a c)", p=P),
                        tj[:, k, i, :]), tok, dtok)
                    dtok = gen.dma(sp, lambda e, k=k, i=i: e.dma_start(
                        ivec[2 * k + i:1 + 2 * k + i, :].rearrange("a (c p) -> p (a c)", p=P),
                        tji[:, k, i, :]), tok, dtok)
            z = dve.op(lambda e: e.memset(zrow[:, :], 0.0))
            z = dve.op(lambda e: e.memset(zrow[:, D:D + 1], 16383.0), z)
            dtok = gen.dma(sp, lambda e: e.dma_start(msgs[E:T * P, :], zrow[:, :]), z, dtok)
            sp.waits([dtok])

        phase("prep", prep, {"gen": 1, "ld0": 1, "ld1": 1, "ld2": 1, "st": 1})

        def norm_relu(dve, act, xt, ht, stt, mv, sc, eps, *tok):
            a = dve.op(lambda e: e.bn_stats(stt, xt), *tok)
            a = dve.op(lambda e: e.bn_aggr(mv, stt), a)
            a = act.op(lambda e: e.activation(sc[:, 0:1], mv[:, 1:2], ACT.Sqrt, bias=eps, scale=1.0), a)
            a = dve.op(lambda e: e.reciprocal(sc[:, 1:2], sc[:, 0:1]), a)
            a = dve.op(lambda e: e.tensor_scalar(sc[:, 2:3], mv[:, 0:1], sc[:, 1:2], -1.0, ALU.mult, ALU.mult), a)
            return act.op(lambda e: e.activation(ht, xt, ACT.Relu, bias=sc[:, 2:3], scale=sc[:, 1:2]), a)

        def l0a(stack, en, sl):
            pe, dve, act, pool, sp = (en[k] for k in ("pe", "dve", "act", "pool", "sp"))
            (gen,) = sl["gen"]
            h = sb(stack, "h", [P, NB, D])
            xt = sb(stack, "xt", [P, 4, D])
            stt = sb(stack, "stt", [P, 4, 6])
            mv = sb(stack, "mv", [P, 4, 2])
            sc = sb(stack, "sc", [P, 4, 4])
            epst = sb(stack, "epst", [P, 1])
            tidx = sb(stack, "tidx", [P, 13], I32)
            bbc = sb(stack, "bbc", [P, JP])
            brow = sb(stack, "brow", [1, JP], I32)
            fg = sb(stack, "fg", [P, 2, 5 * P])
            pg = sb(stack, "pg", [P, 2, P])
            dloc = sb(stack, "dloc", [P, JP])
            wT = sb(stack, "wT", [P, JP])
            sT = sb(stack, "sT", [P, JP])
            pT = sb(stack, "pT", [P, JP])
            pI = sb(stack, "pI", [P, JP], I32)
            msk = sb(stack, "msk", [P, JP])
            NO = 4
            NM = 8
            O = sb(stack, "O0", [P, NO, P])
            OT = sb(stack, "OT0", [P, NO, P])
            mt = sb(stack, "mt", [P, NM, ROW])

            t_eps = dve.op(lambda e: e.memset(epst[:, :], 1e-5))
            g = gen.dma(sp, lambda e: e.dma_start(tidx[:, :], ivec[0:1, :].rearrange("a (c p) -> p (a c)", p=P)))
            g = gen.dma(sp, lambda e: e.dma_start(brow[:, :], ivec[1:2, :]))
            g = gen.dma(sp, lambda e: e.dma_start(bbc[:, :], dvec[3:4, :].to_broadcast([P, JP])))
            xfree = [None] * 4
            z = dve.op(lambda e: e.memset(xt[:, (NB - 1) % 4, :], 0.0))
            h_done = None
            for b in range(NB):
                s = b % 4
                n = P if b < NB - 1 else NLAST
                if b == NB - 1:
                    z = dve.op(lambda e, s=s: e.memset(xt[:, s, :], 0.0), xfree[s])
                l = sl["x"][s].dma(sp, lambda e, b=b, s=s, n=n: e.dma_start(xt[0:n, s, :], x[b * P:b * P + n, :]),
                                   xfree[s], z)
                xfree[s] = h_done = norm_relu(dve, act, xt[:, s, :], h[:, b, :], stt[:, s, :], mv[:, s, :],
                                              sc[:, s, :], epst[:, :], l, t_eps, xfree[s])
            fgfree = [None] * 2
            psfree = [None] * 2
            last = None
            for c in range(13):
                s = c % 2
                lf = sl["fg"][s].dma(pool, lambda e, c=c, s=s: e.indirect_dma_start(
                    fg[:, s, :], None, fields, bass.IndirectOffsetOnAxis(ap=tidx[:, c:c + 1], axis=0)), g, fgfree[s])
                lp = sl["pg"][s].dma(pool, lambda e, c=c, s=s: e.indirect_dma_start(
                    pg[:, s, :], None, posrows, bass.IndirectOffsetOnAxis(ap=tidx[:, c:c + 1], axis=0)))
                for i, (dstt, view) in enumerate(((dloc, fg[:, s, P:2 * P]), (wT, fg[:, s, 2 * P:3 * P]),
                                                  (sT, fg[:, s, 0:P]), (pT, pg[:, s, :]))):
                    a = pe.op(lambda e, i=i, view=view: e.transpose(psum[i % 2][:, 0:P], view, ident[:, :]),
                              lf, lp, psfree[i % 2])
                    psfree[i % 2] = act.op(lambda e, i=i, c=c, dstt=dstt: e.copy(dstt[:, c * P:(c + 1) * P],
                                                                                 psum[i % 2][:, 0:P]), a)
                fgfree[s] = a
                last = psfree[1]
            a = dve.op(lambda e: e.scalar_tensor_tensor(out=dloc[:, :], in0=bbc[:, :], scalar=-float(P),
                                                        in1=dloc[:, :], op0=ALU.mult, op1=ALU.add), last, psfree[0], g)
            b1 = dve.op(lambda e: e.tensor_scalar(msk[:, :], dloc[:, :], 0.0, 1.0e6, ALU.is_lt, ALU.mult), a)
            b2 = dve.op(lambda e: e.tensor_scalar(bbc[:, :], dloc[:, :], 127.0, 1.0e6, ALU.is_gt, ALU.mult), a)
            b3 = dve.op(lambda e: e.tensor_tensor(msk[:, :], msk[:, :], bbc[:, :], ALU.add), b1, b2)
            b4 = dve.op(lambda e: e.tensor_tensor(msk[:, :], msk[:, :], pT[:, :], ALU.add), b3)
            t_pI = dve.op(lambda e: e.tensor_copy(pI[:, :], msk[:, :]), b4)

            vals = {}
            ofree = [None] * NO
            otfree = [None] * NO
            mfree = [None] * NM
            tr_free = [None] * 2
            he_free = [None] * 2
            stage = {}
            pe.waits([h_done])

            def s1(j):
                o = dve.op(lambda e, j=j: e.tensor_scalar(O[:, j % NO, :], iota[:, :], dloc[:, j:j + 1], None,
                                                          ALU.is_equal), ofree[j % NO], t_pI)
                t = pe.op(lambda e, j=j: e.transpose(psum[j % 2][:, 0:P], O[:, j % NO, :], ident[:, :]),
                          o, tr_free[j % 2], psfree[0], psfree[1])
                ofree[j % NO] = t
                c = act.op(lambda e, j=j: e.copy(OT[:, j % NO, :], psum[j % 2][:, 0:P]), t, otfree[j % NO])
                tr_free[j % 2] = c
                stage[j] = c

            def s2(j):
                if j % 4 == 0:
                    m = min(4, J - j)

                    def ld(e, j=j, m=m):
                        regs = four(vals, e, "l0a")
                        e.load(regs[:m], brow[0:1, j:j + m])
                        vals["v"] = [e.snap(r, min_val=0, max_val=NB - 1) for r in regs[:m]]
                    pe.do(ld, g)
                m = pe.op(lambda e, j=j: e.matmul(
                    psum[2 + j % 2][:, 0:D], lhsT=OT[:, j % NO, :],
                    rhs=h[:, bass.ds(vals["v"][j % 4], 1), :].rearrange("p a b -> p (a b)"), start=True, stop=True),
                    stage.pop(j), he_free[j % 2])
                otfree[j % NO] = m
                c = act.op(lambda e, j=j: e.activation(mt[:, j % NM, 0:D], psum[2 + j % 2][:, 0:D], ACT.Copy,
                                                       scale=wT[:, j:j + 1]), m, mfree[j % NM])
                he_free[j % 2] = c
                c2 = dve.op(lambda e, j=j: e.tensor_copy(mt[:, j % NM, D:D + 1], sT[:, j:j + 1]), mfree[j % NM])
                mfree[j % NM] = sl["m"][j % NM].dma(pool, lambda e, j=j: e.indirect_dma_start(
                    msgs, bass.IndirectOffsetOnAxis(ap=pI[:, j:j + 1], axis=0), mt[:, j % NM, :], None,
                    bounds_check=E - 1, oob_is_err=False), c, c2, t_pI)

            for j in range(J + 1):
                if j < J:
                    s1(j)
                if j >= 1:
                    s2(j - 1)
            pool.waits(mfree)

        phase("l0a", l0a, {"gen": 1, "x": 4, "fg": 2, "pg": 2, "m": 8})

        def l0b(stack, en, sl):
            pe, dve, act, pool, sp = (en[k] for k in ("pe", "dve", "act", "pool", "sp"))
            (gen,) = sl["gen"]
            acc = sb(stack, "acc0", [P, NB, D])
            bbc = sb(stack, "bbc1", [P, JP])
            rows = sb(stack, "rows1", [1, 2, JP], I32)
            NM = 8
            NO = 4
            mt = sb(stack, "mt1", [P, NM, ROW])
            O = sb(stack, "O1", [P, NO, P])
            g = gen.dma(sp, lambda e: e.dma_start(rows[:, 0, :], ivec[2:3, :]))
            g = gen.dma(sp, lambda e: e.dma_start(rows[:, 1, :], ivec[3:4, :]))
            g = gen.dma(sp, lambda e: e.dma_start(bbc[:, :], dvec[5:6, :].to_broadcast([P, JP])))
            k = dve.op(lambda e: e.tensor_scalar(bbc[:, :], bbc[:, :], float(P), None, ALU.mult), g)
            az = pool.op(lambda e: e.memset(acc[:, :, :], 0.0))
            mfree = [None] * NM
            ofree = [None] * NO
            pfree = [None] * 2
            vs, vd = {}, {}
            pend = []
            sp.waits([g])
            dve.waits([az, k])
            last = None

            def add(j, m):
                if j % 4 == 0:
                    n = min(4, J - j)

                    def ld(e, j=j, n=n):
                        regs = four(vd, e, "l0d")
                        e.load(regs[:n], rows[0:1, 1, j:j + n])
                        vd["v"] = [e.snap(r, min_val=0, max_val=NB - 1) for r in regs[:n]]
                    dve.do(ld)

                def fn(e, j=j):
                    t = acc[:, bass.ds(vd["v"][j % 4], 1), :].rearrange("p a b -> p (a b)")
                    return e.tensor_tensor(t, t, psum[j % 2][:, 0:D], ALU.add)
                return dve.op(fn, m, (dve.sem, dve.count))

            for j in range(J):
                if j % 4 == 0:
                    n = min(4, J - j)

                    def lds(e, j=j, n=n):
                        regs = four(vs, e, "l0s")
                        e.load(regs[:n], rows[0:1, 0, j:j + n])
                        vs["v"] = [e.snap(r, min_val=0, max_val=T - 1) for r in regs[:n]]
                    sp.do(lds)
                l = sl["m"][j % NM].dma(sp, lambda e, j=j: e.dma_start(
                    mt[:, j % NM, :], msgs[bass.ds(vs["v"][j % 4] * P, P), :]), mfree[j % NM])
                o = dve.op(lambda e, j=j: e.tensor_scalar(O[:, j % NO, :], iota[:, :], bbc[:, j:j + 1],
                                                          mt[:, j % NM, D:D + 1], ALU.add, ALU.is_equal),
                           l, ofree[j % NO])
                if pend:
                    jj, m = pend.pop()
                    pfree[jj % 2] = last = add(jj, m)
                for f in range(2):
                    m = pe.op(lambda e, j=j, f=f: e.matmul(
                        psum[j % 2][:, f * P:(f + 1) * P], lhsT=mt[:, j % NM, f * P:(f + 1) * P],
                        rhs=O[:, j % NO, :], start=True, stop=True), l, o, pfree[j % 2])
                mfree[j % NM] = ofree[j % NO] = m
                pend.append((j, m))
            jj, m = pend.pop()
            last = add(jj, m)

            wts = sb(stack, "wts", [P, 2, D])
            wraw = sb(stack, "wraw", [P, 2, D])
            wt = sb(stack, "wt", [P, 2, 3, D])
            bias = sb(stack, "bias", [P, 3, D])
            w = sl["w"]
            t_w = w[0].dma(sp, lambda e: e.dma_start(wts[:, :, :], weight.rearrange("(a p) d -> p a d", p=P)))
            bt = None
            for i, bb in enumerate((bq, bk, bv)):
                bt = w[1].dma(sp, lambda e, i=i, bb=bb: e.dma_start(
                    bias[:, i, :], bb.rearrange("(a d) -> a d", a=1).to_broadcast([P, D])))
            free = None
            c = None
            for i, ww in enumerate((Wq, Wk, Wv)):
                l = w[2].dma(sp, lambda e, ww=ww: e.dma_start(wraw[:, :, :], ww.rearrange("(a p) d -> p a d", p=P)),
                             free)
                for a in range(2):
                    for b in range(2):
                        t = pe.op(lambda e, a=a, b=b: e.transpose(psum[2][:, 0:P], wraw[:, a, b * P:(b + 1) * P],
                                                                  ident[:, :]), l, c)
                        c = act.op(lambda e, a=a, b=b, i=i: e.copy(wt[:, b, i, a * P:(a + 1) * P],
                                                                   psum[2][:, 0:P]), t)
                free = t
            t_wt = c

            NX = 3
            xt = sb(stack, "xt1", [P, NX, D])
            ht = sb(stack, "ht1", [P, NX, D])
            hT = sb(stack, "hT1", [P, NX, 2, P])
            stt = sb(stack, "stt1", [P, NX, 6])
            mv = sb(stack, "mv1", [P, NX, 2])
            sc = sb(stack, "sc1", [P, NX, 4])
            epst = sb(stack, "epst1", [P, 1])
            qo = sb(stack, "qo", [P, NX, D])
            kvo = sb(stack, "kvo", [P, NX, KVW])
            t_eps = dve.op(lambda e: e.memset(epst[:, :], 1e-5))
            t_one = dve.op(lambda e: e.memset(kvo[:, :, :], 1.0))
            xfree = [None] * NX
            hfree = [None] * NX
            qfree = [None] * NX
            st = sl["st"]
            p3 = p45 = p6 = None
            z = None
            for b in range(NB):
                s = b % NX
                n = P if b < NB - 1 else NLAST
                if b == NB - 1:
                    z = dve.op(lambda e, s=s: e.memset(xt[:, s, :], 0.0), xfree[s], st[s].token)
                l = sl["x"][s].dma(sp, lambda e, b=b, s=s, n=n: e.dma_start(xt[0:n, s, :], x[b * P:b * P + n, :]),
                                   xfree[s], st[s].token, z)
                for f in range(2):
                    m = pe.op(lambda e, b=b, f=f: e.matmul(psum[3][:, 0:D], lhsT=acc[:, b, f * P:(f + 1) * P],
                                                           rhs=wts[:, f, :], start=(f == 0), stop=(f == 1)),
                              t_w, p3, last)
                a = dve.op(lambda e, s=s: e.tensor_tensor(xt[:, s, :], xt[:, s, :], psum[3][:, 0:D], ALU.add), m, l)
                p3 = a
                s1 = st[s].dma(sp, lambda e, b=b, s=s: e.dma_start(x1t[b * P:(b + 1) * P, :], xt[:, s, :]), a)
                hd = norm_relu(dve, act, xt[:, s, :], ht[:, s, :], stt[:, s, :], mv[:, s, :], sc[:, s, :],
                               epst[:, :], a, t_eps, hfree[s])
                xfree[s] = hd
                for f in range(2):
                    m = pe.op(lambda e, s=s, f=f: e.transpose(psum[4][:, f * P:(f + 1) * P],
                                                              ht[:, s, f * P:(f + 1) * P], ident[:, :]), hd, p45)
                p45 = act.op(lambda e, s=s: e.copy(hT[:, s, :, :].rearrange("p a b -> p (a b)"), psum[4][:, 0:D]), m)
                for f in range(2):
                    pe.op(lambda e, s=s, f=f: e.matmul(psum[5][:, 0:D], lhsT=hT[:, s, f, :], rhs=wt[:, f, 0, :],
                                                       start=(f == 0), stop=(f == 1)), p45, t_wt, p6)
                for f in range(2):
                    m = pe.op(lambda e, s=s, f=f: e.matmul(
                        psum[6][:, :], lhsT=hT[:, s, f, :], rhs=wt[:, f, 1:3, :].rearrange("p a b -> p (a b)"),
                        start=(f == 0), stop=(f == 1)))
                hfree[s] = m
                qtok = qfree[s]
                a1 = dve.op(lambda e, s=s: e.tensor_tensor(qo[:, s, :], psum[5][:, 0:D], bias[:, 0, :], ALU.add),
                            m, bt, qtok, t_one)
                a2 = dve.op(lambda e, s=s: e.tensor_tensor(kvo[:, s, 0:D], psum[6][:, 0:D], bias[:, 1, :], ALU.add))
                a3 = dve.op(lambda e, s=s: e.tensor_tensor(
                    kvo[:, s, D:KVW].rearrange("p (h d) -> p h d", h=NH)[:, :, 0:32],
                    psum[6][:, D:2 * D].rearrange("p (h d) -> p h d", h=NH),
                    bias[:, 2, :].rearrange("p (h d) -> p h d", h=NH), ALU.add))
                p6 = a3
                o = sl["qo"][s]
                o.dma(sp, lambda e, b=b, s=s: e.dma_start(qt[b * P:(b + 1) * P, :], qo[:, s, :]), a1)
                qfree[s] = o.dma(sp, lambda e, b=b, s=s: e.dma_start(kvt[b * P:(b + 1) * P, :], kvo[:, s, :]), a3)
            sp.waits(qfree + [q.token for q in st])

        phase("l0b", l0b, {"gen": 1, "m": 8, "w": 3, "x": 3, "st": 3, "qo": 3})

        def l1(stack, en, sl):
            pe, dve, act, pool, sp = (en[k] for k in ("pe", "dve", "act", "pool", "sp"))
            (gen,) = sl["gen"]
            acc = sb(stack, "acc2", [P, NB, NH, 33])
            brow = sb(stack, "brow2", [1, JP], I32)
            sI = sb(stack, "sI", [P, JP], I32)
            dloc = sb(stack, "dloc2", [P, JP])
            FT = sb(stack, "FT", [P, JP], BF16)
            LT = sb(stack, "LT", [P, JP], BF16)
            link = sb(stack, "link", [P, JP])

            with ExitStack() as pre:
                tidx = sb(pre, "tidx2", [P, 13], I32)
                same = sb(pre, "same", [P, JP + 1])
                fg = sb(pre, "fg2", [P, 2, 5 * P])
                g = gen.dma(sp, lambda e: e.dma_start(tidx[:, :], ivec[0:1, :].rearrange("a (c p) -> p (a c)", p=P)))
                g = gen.dma(sp, lambda e: e.dma_start(brow[:, :], ivec[1:2, :]))
                g = gen.dma(sp, lambda e: e.dma_start(same[:, 1:JP + 1], dvec[3:4, :].to_broadcast([P, JP])))
                fgfree = [None] * 2
                psfree = [None] * 2
                for c in range(13):
                    s = c % 2
                    lf = sl["fg"][s].dma(pool, lambda e, c=c, s=s: e.indirect_dma_start(
                        fg[:, s, :], None, fields, bass.IndirectOffsetOnAxis(ap=tidx[:, c:c + 1], axis=0)),
                        g, fgfree[s])
                    for i, (dstt, k) in enumerate(((dloc, 1), (sI, 0), (FT, 3), (LT, 4))):
                        a = pe.op(lambda e, i=i, s=s, k=k: e.transpose(psum[i % 2][:, 0:P],
                                                                       fg[:, s, k * P:(k + 1) * P], ident[:, :]),
                                  lf, psfree[i % 2])
                        if k == 0:
                            psfree[i % 2] = dve.op(lambda e, i=i, c=c, dstt=dstt: e.tensor_scalar(
                                dstt[:, c * P:(c + 1) * P], psum[i % 2][:, 0:P], float(N - 1), None, ALU.min), a)
                        elif k == 3:
                            psfree[i % 2] = act.op(lambda e, i=i, c=c, dstt=dstt: e.activation(
                                dstt[:, c * P:(c + 1) * P], psum[i % 2][:, 0:P], ACT.Copy, scale=-BIG), a)
                        else:
                            psfree[i % 2] = act.op(lambda e, i=i, c=c, dstt=dstt: e.copy(
                                dstt[:, c * P:(c + 1) * P], psum[i % 2][:, 0:P]), a)
                    fgfree[s] = a
                a = dve.op(lambda e: e.scalar_tensor_tensor(
                    out=dloc[:, :], in0=same[:, 1:JP + 1], scalar=-float(P), in1=dloc[:, :], op0=ALU.mult,
                    op1=ALU.add), psfree[0], psfree[1], g)
                pre_done = dve.op(lambda e: e.memset(same[:, 0:1], -1.0), g)
                t_link = dve.op(lambda e: e.tensor_tensor(link[:, :], same[:, 1:JP + 1], same[:, 0:JP],
                                                          ALU.not_equal), pre_done, a)
                t_link = dve.op(lambda e: e.tensor_scalar(link[:, :], link[:, :], -BIG, None, ALU.mult), t_link)
            for q in (pe, dve, act, pool, sp):
                q.waits([t_link, fgfree[0], fgfree[1]])
            NK = 20
            NQ = 4
            NO = 18
            NT = 13
            kv = sb(stack, "kv", [P, NK, KVW], F32)
            qb = sb(stack, "qb", [P, NQ, D])
            O = sb(stack, "O2", [P, NO, P])
            OT = sb(stack, "OT2", [P, NT, P])
            prod = sb(stack, "prod", [P, 2, D])
            sims = sb(stack, "sims", [P, 2, NH, W])
            FB = sb(stack, "FB", [P, NH, W])
            FS = sb(stack, "FS", [64, P])
            PM = sb(stack, "PM", [64, P])
            PL = sb(stack, "PL", [P, W, 9])
            absent = sb(stack, "absent", [P, W])
            val = sb(stack, "val", [P, NH, W])
            D0 = sb(stack, "D0", [P, 2, NH, W])
            fw = sb(stack, "fw", [P, NH, W])
            ref = sb(stack, "ref", [P, NH, W])
            carry = sb(stack, "carry", [P, NH])
            alpha = sb(stack, "alpha", [P, 2, NH])
            dd = sb(stack, "dd", [P, NH, W])
            pp = sb(stack, "pp", [P, 2, NH, W])
            pv = sb(stack, "pv", [P, 2, NH * 33])

            az = pool.op(lambda e: e.memset(acc[:, :, :, :], 0.0))
            t_carry = dve.op(lambda e: e.memset(carry[:, :], -BIG))
            dve.waits([az])
            kvfree = [None] * NK
            qfree = [None] * NQ
            ofree = [None] * NO
            otfree = [None] * NT
            trfree = [None] * 2
            qefree = [None] * 2
            ufree = [None] * 2
            prodfree = [None] * 2
            kvtok = {}
            simtok = [None] * 2
            simfree = [None] * 2
            vs, vd = {}, {}
            b4 = b5 = None
            S = {"b4": None, "b5": None, "carry": t_carry}
            sp.waits([g])

            def stage_a(w):
                n = min(W, J - w * W)
                for i in range(n):
                    if i:
                        yield
                    j = w * W + i
                    if j % 4 == 0:
                        m = min(4, J - j)

                        def lds(e, j=j, m=m):
                            regs = four(vs, e, "l1s")
                            e.load(regs[:m], brow[0:1, j:j + m])
                            vs["v"] = [e.snap(r, min_val=0, max_val=NB - 1) for r in regs[:m]]
                        sp.do(lds)
                    lk = kvtok[j] = sl["kv"][j % NK].dma(pool, lambda e, j=j: e.indirect_dma_start(
                        kv[:, j % NK, :], None, kvt, bass.IndirectOffsetOnAxis(ap=sI[:, j:j + 1], axis=0)),
                        kvfree[j % NK], a0)
                    lq = sl["q"][j % NQ].dma(sp, lambda e, j=j: e.dma_start(
                        qb[:, j % NQ, :], qt[bass.ds(vs["v"][j % 4] * P, P), :]), qfree[j % NQ])
                    o = dve.op(lambda e, j=j: e.tensor_scalar(O[:, j % NO, :], iota[:, :], dloc[:, j:j + 1], None,
                                                              ALU.is_equal), ofree[j % NO])
                    t = pe.op(lambda e, j=j: e.transpose(psum[j % 2][:, 0:P], O[:, j % NO, :], ident[:, :]),
                              o, trfree[j % 2])
                    c = trfree[j % 2] = act.op(lambda e, j=j: e.copy(OT[:, j % NT, :], psum[j % 2][:, 0:P]), t,
                                               otfree[j % NT])
                    q = pe.op(lambda e, j=j: e.matmul(psum[2 + j % 2][:, 0:D], lhsT=OT[:, j % NT, :],
                                                      rhs=qb[:, j % NQ, :], start=True, stop=True),
                              c, lq, qefree[j % 2])
                    qfree[j % NQ] = q
                    pr = dve.op(lambda e, j=j: e.tensor_tensor(prod[:, j % 2, :], psum[2 + j % 2][:, 0:D],
                                                               kv[:, j % NK, 0:D], ALU.mult), q, lk, prodfree[j % 2])
                    qefree[j % 2] = pr
                    r = dve.op(lambda e, j=j, w=w, i=i: e.tensor_reduce(
                        sims[:, w % 2, :, i], prod[:, j % 2, :].rearrange("p (h d) -> p h d", h=NH), AX.X,
                        ALU.add), pr, simfree[w % 2])
                    prodfree[j % 2] = r
                if n < W:
                    r = dve.op(lambda e, w=w, n=n: e.memset(sims[:, w % 2, :, n:W], 0.0), r)
                simtok[w % 2] = r

            def stage_b(w):
                n = min(W, J - w * W)
                j0 = w * W
                fb = act.op(lambda e: e.copy(FB[:, :, :], FT[:, j0:j0 + W].rearrange("p (a b) -> p a b", a=1)
                                             .to_broadcast([P, NH, W])), S.get("tf"), a0)
                d1 = act.op(lambda e: e.copy(D0[:, 0, :, :], link[:, j0:j0 + W].rearrange("p (a b) -> p a b", a=1)
                                             .to_broadcast([P, NH, W])), S.get("scan"), t_link)
                d1 = act.op(lambda e: e.copy(D0[:, 1, :, 0:W - 1],
                                             link[:, j0 + 1:j0 + W].rearrange("p (a b) -> p a b", a=1)
                                             .to_broadcast([P, NH, W - 1])))
                ts = pe.op(lambda e: e.transpose(psum[4][0:64, 0:P],
                                                 sims[:, w % 2, :, :].rearrange("p a b -> p (a b)"), ident[:, :]),
                           simtok[w % 2], S["b4"])
                tf = S["tf"] = pe.op(lambda e: e.transpose(psum[4][0:64, P:2 * P],
                                                           FB[:, :, :].rearrange("p a b -> p (a b)"), ident[:, :]), fb)
                fs = act.op(lambda e: e.copy(FS[:, :], psum[4][0:64, P:2 * P]), tf, S.get("pm"))
                pm = S["pm"] = dve.op(lambda e: e.tensor_tensor_scan(PM[:, :], FS[:, :], psum[4][0:64, 0:P], 0.0,
                                                                     ALU.add, ALU.max), fs, ts, S.get("tb"))
                tb = S["tb"] = pe.op(lambda e: e.transpose(psum[4][:, 2 * P:2 * P + 64], PM[:, :],
                                                           ident[0:64, 0:64]), pm)
                yield
                l1_ = dve.op(lambda e: e.tensor_tensor(
                    PL[:, :, 0:NH].rearrange("p j h -> p h j"),
                    psum[4][:, 2 * P:2 * P + 64].rearrange("p (h j) -> p h j", h=NH),
                    LT[:, j0:j0 + W].rearrange("p (a b) -> p a b", a=1).to_broadcast([P, NH, W]), ALU.mult),
                    tb, S.get("m9"))
                S["b4"] = l1_
                l2 = act.op(lambda e: e.copy(PL[:, :, NH], LT[:, j0:j0 + W]), S.get("m9"))
                for i in range(n):
                    j = j0 + i
                    m9 = pe.op(lambda e, i=i, j=j: e.matmul(psum[5][:, i * 9:(i + 1) * 9], lhsT=O[:, j % NO, :],
                                                            rhs=PL[:, i, :], start=True, stop=True),
                               l1_, l2, S["b5"])
                S["m9"] = m9
                yield
                v9 = psum[5][:, 0:W * 9].rearrange("p (j k) -> p j k", k=9)
                ab = dve.op(lambda e: e.tensor_scalar(absent[:, 0:n], v9[:, 0:n, NH], BIG, -BIG, ALU.mult, ALU.add),
                            m9)
                if n < W:
                    vt = dve.op(lambda e: e.memset(val[:, :, :], 0.0), S.get("scan"))
                else:
                    vt = None
                v = dve.op(lambda e: e.tensor_tensor(
                    val[:, :, 0:n], v9[:, 0:n, 0:NH].rearrange("p j h -> p h j"),
                    absent[:, 0:n].rearrange("p (a b) -> p a b", a=1).to_broadcast([P, NH, n]), ALU.add),
                    ab, vt, S.get("scan"))
                v = dve.op(lambda e: e.scalar_tensor_tensor(
                    out=val[:, :, 0], in0=carry[:, :], scalar=link[:, j0:j0 + 1], in1=val[:, :, 0], op0=ALU.add,
                    op1=ALU.max), v, S["carry"])
                z = dve.op(lambda e: e.memset(D0[:, 0, :, 0:1], -BIG), d1)
                z = dve.op(lambda e: e.memset(D0[:, 1, :, W - 1:W], -BIG), d1)
                f = dve.op(lambda e: e.tensor_tensor_scan(
                    fw[:, :, :].rearrange("p a b -> p (a b)"), D0[:, 0, :, :].rearrange("p a b -> p (a b)"),
                    val[:, :, :].rearrange("p a b -> p (a b)"), 0.0, ALU.add, ALU.max), v, z)
                r = dve.op(lambda e: e.tensor_tensor_scan(
                    ref[:, :, :].rearrange("p a b -> p (a b)")[:, ::-1],
                    D0[:, 1, :, :].rearrange("p a b -> p (a b)")[:, ::-1],
                    fw[:, :, :].rearrange("p a b -> p (a b)")[:, ::-1], 0.0, ALU.add, ALU.max), f, S.get("me"))
                S["scan"] = r
                al = dve.op(lambda e: e.scalar_tensor_tensor(
                    out=alpha[:, 0, :], in0=carry[:, :], scalar=link[:, j0:j0 + 1], in1=ref[:, :, 0], op0=ALU.add,
                    op1=ALU.subtract), r, S.get("al"))
                ex = act.op(lambda e: e.activation(alpha[:, 1, :], alpha[:, 0, :], ACT.Exp, scale=SCALE), al,
                            S.get("resc"))
                S["al"] = ex
                S["carry"] = dve.op(lambda e: e.tensor_copy(carry[:, :], ref[:, :, n - 1]), al)
                for i in range(n):
                    j = j0 + i
                    me = pe.op(lambda e, i=i, j=j: e.matmul(psum[5][:, 128 + i * NH:128 + (i + 1) * NH],
                                                            lhsT=OT[:, j % NT, :], rhs=ref[:, :, i], start=True,
                                                            stop=True), r)
                    otfree[j % NT] = me
                S["me"] = me
                yield
                d = dve.op(lambda e: e.tensor_tensor(
                    dd[:, :, 0:n], sims[:, w % 2, :, 0:n],
                    psum[5][:, 128:128 + n * NH].rearrange("p (j h) -> p h j", h=NH), ALU.subtract), me,
                    S.get("dd"))
                S["b5"] = d
                simfree[w % 2] = d
                S["dd"] = S["pp"] = act.op(lambda e: e.activation(pp[:, w % 2, :, 0:n], dd[:, :, 0:n], ACT.Exp,
                                                                  scale=SCALE), d, S.get(f"ppf{w % 2}"))

                def ldd(e, j0=j0):
                    regs = four(vd, e, "l1d")
                    e.load(regs[:1], brow[0:1, j0:j0 + 1])
                    vd["a"] = e.snap(regs[0], min_val=0, max_val=NB - 1)
                    t = acc[:, bass.ds(vd["a"], 1), :, :].rearrange("p a h d -> p (a h) d")
                    return e.tensor_tensor(t, t, alpha[:, 1, :].rearrange("p (h a) -> p h a", a=1)
                                           .to_broadcast([P, NH, 33]), ALU.mult)
                S["acc"] = S["resc"] = dve.op(ldd, ex, S.get("acc"))

            def stage_c(w):
                n = min(W, J - w * W)
                pend = None

                def add(j, u):
                    if j % 4 == 0:
                        m = min(4, J - j)

                        def ld(e, j=j, m=m):
                            regs = four(vd, e, "l1d")
                            e.load(regs[:m], brow[0:1, j:j + m])
                            vd["v"] = [e.snap(r, min_val=0, max_val=NB - 1) for r in regs[:m]]
                        dve.do(ld)

                    def fn(e, j=j):
                        t = acc[:, bass.ds(vd["v"][j % 4], 1), :, :].rearrange("p a h d -> p (a h d)")
                        return e.tensor_tensor(t, t, psum[6 + j % 2][:, 0:NH * 33], ALU.add)
                    S["acc"] = ufree[j % 2] = dve.op(fn, u, S["acc"])

                for i in range(n):
                    if i:
                        yield
                    j = w * W + i
                    p = dve.op(lambda e, j=j, i=i: e.tensor_tensor(
                        pv[:, j % 2, :].rearrange("p (h d) -> p h d", h=NH),
                        kv[:, j % NK, D:KVW].rearrange("p (h d) -> p h d", h=NH),
                        pp[:, w % 2, :, i:i + 1].to_broadcast([P, NH, 33]), ALU.mult),
                        S["pp"], S.get(f"pv{j % 2}"), kvtok.pop(j))
                    kvfree[j % NK] = p
                    u = pe.op(lambda e, j=j: e.matmul(psum[6 + j % 2][:, 0:NH * 33], lhsT=O[:, j % NO, :],
                                                      rhs=pv[:, j % 2, :], start=True, stop=True), p, ufree[j % 2])
                    S[f"pv{j % 2}"] = u
                    ofree[j % NO] = u
                    if pend:
                        add(*pend)
                    pend = (j, u)
                S[f"ppf{w % 2}"] = p
                add(*pend)

            a0 = a
            def chain(*gens):
                for g_ in gens:
                    yield from g_
                    yield

            for w in range(NW + 1):
                one = stage_a(w) if w < NW else iter(())
                two = chain(stage_b(w - 1), stage_c(w - 1)) if w >= 1 else iter(())
                k = 0
                live = True
                while live:
                    live = False
                    for g_ in ((one, two) if k < 4 else (one, two, two)):
                        for _ in g_:
                            live = True
                            break
                    k += 1
            S_acc = S["acc"]

            w = sl["w"]
            wraw = kv[:, 0:1, 0:2 * D].rearrange("p a (b d) -> p (a b) d", b=2)
            wot = kv[:, 1:2, 0:2 * D].rearrange("p a (b d) -> p (a b) d", b=2)
            bias = kv[:, 2, 0:D]
            l = w[0].dma(sp, lambda e: e.dma_start(wraw, Wo.rearrange("(a p) d -> p a d", p=P)), *kvfree)
            bt = w[1].dma(sp, lambda e: e.dma_start(
                bias, bo.rearrange("(a d) -> a d", a=1).to_broadcast([P, D])))
            c = None
            for a in range(2):
                for b in range(2):
                    t = pe.op(lambda e, a=a, b=b: e.transpose(psum[0][:, 0:P], wraw[:, a, b * P:(b + 1) * P],
                                                              ident[:, :]), l, c, trfree[0])
                    c = act.op(lambda e, a=a, b=b: e.copy(wot[:, b, a * P:(a + 1) * P], psum[0][:, 0:P]), t,
                               *kvfree)
            t_wo = c
            rs = sb(stack, "rs", [P, 2, NH])
            ofr = [None] * 2
            xf = [None] * 2
            p1 = p2 = None
            dve.waits([S_acc])
            for b in range(NB):
                s = b % 2
                n = P if b < NB - 1 else NLAST
                ot = kv[:, 4 + s, 0:D]
                oT = kv[:, 6 + s, 0:D]
                xt = kv[:, 8 + s, 0:D]
                l = sl["x"][s].dma(sp, lambda e, b=b, xt=xt: e.dma_start(xt, x1t[b * P:(b + 1) * P, :]), xf[s])
                a = dve.op(lambda e, b=b, s=s: e.tensor_scalar(rs[:, s, :], acc[:, b, :, 32], 1e-30, None, ALU.max))
                a = dve.op(lambda e, s=s: e.reciprocal(rs[:, s, :], rs[:, s, :]), a)
                a = dve.op(lambda e, b=b, s=s, ot=ot: e.tensor_tensor(
                    ot.rearrange("p (h d) -> p h d", h=NH), acc[:, b, :, 0:32],
                    rs[:, s, :].rearrange("p (h a) -> p h a", a=1).to_broadcast([P, NH, 32]), ALU.mult),
                    a, ofr[s], *kvfree)
                for f in range(2):
                    t = pe.op(lambda e, f=f, ot=ot, s=s: e.transpose(psum[1][:, f * P:(f + 1) * P],
                                                                     ot[:, f * P:(f + 1) * P], ident[:, :]),
                              a, p1, trfree[1])
                ofr[s] = t
                p1 = act.op(lambda e, oT=oT: e.copy(oT, psum[1][:, 0:D]), t, *kvfree)
                for f in range(2):
                    m = pe.op(lambda e, f=f, oT=oT: e.matmul(psum[2][:, 0:D], lhsT=oT[:, f * P:(f + 1) * P],
                                                             rhs=wot[:, f, :], start=(f == 0), stop=(f == 1)),
                              p1, t_wo, p2, qefree[0])
                a = dve.op(lambda e, xt=xt: e.tensor_tensor(xt, xt, bias, ALU.add), l, bt)
                a = p2 = dve.op(lambda e, xt=xt: e.tensor_tensor(xt, xt, psum[2][:, 0:D], ALU.add), a, m)
                xf[s] = sl["o"][s].dma(sp, lambda e, b=b, n=n, xt=xt: e.dma_start(out[b * P:b * P + n, :],
                                                                                  xt[0:n, :]), a)
            sp.waits(xf)

        phase("l1", l1, {"gen": 1, "fg": 2, "kv": 20, "q": 4, "w": 2, "x": 2, "o": 2})


_INS = ["x", "src", "dst", "edge_weight", "L0_gnn_weight", "L1_gnn_Wq", "L1_gnn_bq", "L1_gnn_Wk", "L1_gnn_bk",
        "L1_gnn_Wv", "L1_gnn_bv", "L1_gnn_Wo", "L1_gnn_bo"]


def kernel(**inputs):
    import numpy as _np
    import concourse.bacc as _bacc
    from concourse import mybir as _mybir
    from concourse.bass_utils import run_bass_kernel_spmd as _run

    nc = _bacc.Bacc("TRN2", target_bir_lowering=False, num_devices=1)
    arrays, args = {}, []
    for name in _INS:
        a = _np.ascontiguousarray(inputs[name])
        arrays[f"in_{name}"] = a
        args.append(nc.dram_tensor(f"in_{name}", a.shape, _mybir.dt.from_np(a.dtype), kind="ExternalInput").ap())
    out = nc.dram_tensor("out_0", (N, D), F32, kind="ExternalOutput").ap()
    build(nc, *args, out)
    r = _run(nc, [arrays], core_ids=[0])
    return r.results[0]["out_0"]
```

```python
from contextlib import ExitStack

import numpy as np

import concourse.bass as bass
from concourse import mybir

P = 128
N = 12500
E = 200000
D = 256
NH = 8
NB = 98
NLAST = N - (NB - 1) * P
T = 1563
J = T + NB - 1
JP = 13 * P
W = 8
NW = -(-J // W)
KVW = 256 + NH * 33
ROW = 257
BIG = 1.0e30
SCALE = float(np.float32(1.0) / np.sqrt(np.float32(32.0)))

F32 = mybir.dt.float32
I32 = mybir.dt.int32
BF16 = mybir.dt.bfloat16
ALU = mybir.AluOpType
ACT = mybir.ActivationFunctionType
AX = mybir.AxisListType


class Engine:

    def __init__(self, sem):
        self.sem = sem
        self.count = 0
        self.todo = []
        self.seen = {}

    def waits(self, tokens):
        for t in tokens:
            if t is None:
                continue
            sem, value = t
            if self.seen.get(id(sem), 0) < value:
                self.seen[id(sem)] = value
                self.todo.append(lambda e, sem=sem, value=value: e.wait_ge(sem, value))

    def op(self, fn, *tokens):
        self.waits(tokens)
        self.count += 1
        sem = self.sem
        self.todo.append(lambda e: fn(e).then_inc(sem, 1))
        return (sem, self.count)

    def do(self, fn, *tokens):
        self.waits(tokens)
        self.todo.append(fn)


class Slot:

    def __init__(self, sem):
        self.sem = sem
        self.count = 0

    def dma(self, eng, fn, *tokens):
        eng.waits(tokens)
        self.count += 16
        sem = self.sem
        eng.todo.append(lambda e: fn(e).then_inc(sem, 16))
        return (sem, self.count)

    @property
    def token(self):
        return (self.sem, self.count)


def build(nc, x, src, dst, edge_weight, weight, Wq, bq, Wk, bk, Wv, bv, Wo, bo, out, dump=None):
    def dram(name, shape, dt=F32):
        return nc.dram_tensor(name, shape, dt, kind="Internal").ap()

    fields = dram("fields", (JP, 5 * P))
    starts = dram("starts", (JP, P))
    dvec = dram("dvec", (8, JP))
    ivec = dram("ivec", (8, JP), I32)
    bvec = dram("bvec", (1, P))
    msgs = dram("msgs", (T * P, ROW))
    srcs = dram("srcs", (E,), I32)
    dsts = dram("dsts", (E,), I32)
    ws = dram("ws", (E,))
    recs = [dram(f"recs{k}", (T * P, 4)) for k in range(2)]
    kvt = dram("kvt", (NB * P, KVW))
    qt = dram("qt", (NB * P, D))
    x1t = dram("x1t", (NB * P, D))

    with ExitStack() as top:
        top.enter_context(nc.allow_non_contiguous_dma(reason="vectors of one element per partition"))

        def mksem(name):
            return top.enter_context(nc.semaphore(name))

        def sb(stack, name, shape, dt=F32):
            return stack.enter_context(nc.sbuf_tensor(name, shape, dt))

        psum = [top.enter_context(nc.psum_tensor(f"ps{i}", [P, 512], F32)) for i in range(8)]
        iota = sb(top, "iota", [P, P])
        ident = sb(top, "ident", [P, P])
        tri = sb(top, "tri", [P, P])
        trib = sb(top, "trib", [P, P], BF16)
        onesb = sb(top, "onesb", [P, 2], BF16)
        iotab = sb(top, "iotab", [P, P], BF16)
        identb = sb(top, "identb", [P, P], BF16)
        unsorted = sb(top, "unsorted", [1, 1], I32)

        always, unless_sorted = ([], []), ([], [])
        by_pool = ("fg", "cg", "kv", "ms", "sc")

        def phase(name, program, slots, kept=always):
            with ExitStack() as stack:
                eng = {k: Engine(mksem(f"{name}_{k}")) for k in ("pe", "dve", "act", "pool", "sp")}
                slot = {}
                used = [0, 0]
                for k, n in slots.items():
                    q = k in by_pool
                    while len(kept[q]) < used[q] + n:
                        kept[q].append(Slot(mksem(f"{name}_dma{int(q)}_{len(kept[q])}")))
                    slot[k] = kept[q][used[q]:used[q] + n]
                    used[q] += n
                program(stack, eng, slot)
                block = stack.enter_context(nc.Block())
                for key, deco in (("pe", block.tensor), ("dve", block.vector), ("act", block.scalar),
                                  ("pool", block.gpsimd), ("sp", block.sync)):
                    def run(e, todo=eng[key].todo):
                        for fn in todo:
                            fn(e)
                    deco(run)

        def four(kept, e, name):
            if "regs" not in kept:
                kept["regs"] = [e.alloc_register(f"{name}{i}") for i in range(4)]
            return kept["regs"]

        def bcast(ap, n):
            return ap.rearrange("p (a b) -> p a b", a=1).to_broadcast([P, n, ap.shape[-1]])

        def rows_of(ap, n=P):
            return ap.rearrange("p (j a) -> p j a", a=1).to_broadcast([P, ap.shape[-1], n])

        def pipeline(stages, n):
            for t in range(n + len(stages) - 1):
                for k in reversed(range(len(stages))):
                    if 0 <= t - k < n:
                        stages[k](t - k)

        def histogram(stack, en, keyT, ready, name, more=None):
            pe, dve = en["pe"], en["dve"]
            hot = sb(stack, f"hot{name}", [P, 3, W, P], BF16)
            C = sb(stack, f"C{name}", [P, JP])
            Cs = sb(stack, f"Cs{name}", [P, T])
            base = sb(stack, f"base{name}", [P, 1])
            free = [None] * 3
            t_one = dve.op(lambda e: e.memset(C[:, :], 1.0))
            hist = None
            for k, t0 in enumerate(range(0, T, W)):
                n = min(W, T - t0)
                o = dve.op(lambda e, k=k, t0=t0, n=n: e.tensor_tensor(
                    hot[:, k % 3, 0:n, :], bcast(iotab[:, :], n), rows_of(keyT[:, t0:t0 + n]), ALU.is_equal),
                    free[k % 3], *ready)
                for t in range(t0, t0 + n):
                    hist = free[k % 3] = pe.op(
                        lambda e, t=t, k=k, t0=t0: e.matmul(
                            psum[2 + t // 512][:, t % 512:t % 512 + 1], lhsT=hot[:, k % 3, t - t0, :],
                            rhs=onesb[:, 0:1], start=True, stop=True), o)
            if more:
                more()
            scan = None
            for k in range(4):
                n = min(512, T - 512 * k)
                first = scan is None
                scan = dve.op(lambda e, k=k, n=n, first=first: e.tensor_tensor_scan(
                    Cs[:, 512 * k:512 * k + n], C[:, 512 * k:512 * k + n], psum[2 + k][:, 0:n],
                    0.0 if first else Cs[:, 512 * k - 1:512 * k], ALU.mult, ALU.add), hist, t_one, scan)
            a = pe.op(lambda e: e.matmul(psum[6][:, 0:1], lhsT=tri[:, :], rhs=Cs[:, T - 1:T], start=True, stop=True),
                      scan)
            t_base = dve.op(lambda e: e.tensor_copy(base[:, :], psum[6][:, 0:1]), a)
            for k in range(4):
                n = min(512, T - 512 * k)
                a = dve.op(lambda e, k=k, n=n: e.tensor_tensor(
                    C[:, 512 * k:512 * k + n], Cs[:, 512 * k:512 * k + n], psum[2 + k][:, 0:n], ALU.subtract), scan)
            t_C = dve.op(lambda e: e.tensor_scalar(C[:, :], C[:, :], base[:, 0:1], None, ALU.add), a, t_base)
            return C, base, t_base, t_C

        def rank(en, hot, C, t, bank, *tokens):
            pe = en["pe"]
            pe.op(lambda e: e.matmul(psum[bank][:, 0:P], lhsT=trib[:, :], rhs=hot, start=True, stop=False), *tokens)
            return pe.op(lambda e: e.matmul(psum[bank][:, 0:P], lhsT=C[:, t:t + 1].to_broadcast([P, P]),
                                            rhs=ident[:, :], start=False, stop=True))

        def ranks(stack, en, keyT, ready, name):
            dve = en["dve"]
            C, _, _, t_C = histogram(stack, en, keyT, ready, name)
            hot = sb(stack, f"hot1{name}", [P, 4, P], BF16)
            keyf = sb(stack, f"keyf{name}", [P, T])
            scr = sb(stack, f"scr{name}", [P, 2, P])
            pos = sb(stack, f"pos{name}", [P, T])
            kf = dve.op(lambda e: e.tensor_copy(keyf[:, :], keyT[:, 0:T]), *ready)
            free = [None] * 4
            bank = [None] * 2
            r = None

            def one(t):
                o = dve.op(lambda e: e.tensor_scalar(hot[:, t % 4, :], iota[:, :], keyf[:, t:t + 1], None,
                                                     ALU.is_equal), free[t % 4], kf)
                held[t] = rank(en, hot[:, t % 4, :], C, t, t % 2, o, bank[t % 2], t_C)

            def two(t):
                nonlocal r
                r = bank[t % 2] = free[t % 4] = dve.op(lambda e: e.tensor_tensor_reduce(
                    scr[:, t % 2, :], hot[:, t % 4, :], psum[t % 2][:, 0:P], 1.0, 0.0, ALU.mult, ALU.add,
                    pos[:, t:t + 1]), held.pop(t))
            held = {}
            pipeline([one, two], T)
            return pos, r

        def pairs(stack, en, slot, k, cv, ready):
            dve, pool, sp = en["dve"], en["pool"], en["sp"]
            ji = sb(stack, f"ji{k}", [P, 13], I32)
            jcol = sb(stack, f"jcol{k}", [P, 13])
            cbc = sb(stack, f"cbc{k}", [P, JP])
            junk = sb(stack, f"junk{k}", [P, T], BF16)
            cnt = sb(stack, f"cnt{k}", [P, 13])
            tj = sb(stack, f"tj{k}", [P, 2, 13])
            tji = sb(stack, f"tji{k}", [P, 2, 13], I32)
            a = pool.op(lambda e: e.iota(ji[:, :], pattern=[[P, 13]], base=0, channel_multiplier=1))
            t_j = dve.op(lambda e: e.tensor_copy(jcol[:, :], ji[:, :]), a)
            a = dve.op(lambda e: e.tensor_tensor(cv, cv, jcol[:, :], ALU.add), t_j, *ready)
            d = slot.dma(sp, lambda e: e.dma_start(dvec[k:k + 1, :].rearrange("a (c p) -> p (a c)", p=P), cv), a,
                         slot.token)
            d = slot.dma(sp, lambda e: e.dma_start(cbc[:, :], dvec[k:k + 1, :].to_broadcast([P, JP])), d)

            def rest():
                tok = None
                for c in range(13):
                    tok = dve.op(lambda e, c=c: e.tensor_scalar(junk[:, :], cbc[:, 0:T], jcol[:, c:c + 1], 0.0,
                                                                ALU.is_le, ALU.add, accum_out=cnt[:, c:c + 1]),
                                 d, tok)
                tok = dve.op(lambda e: e.tensor_scalar(tj[:, 0, :], cnt[:, :], -1.0, 0.0, ALU.add, ALU.max), tok)
                tok = dve.op(lambda e: e.tensor_tensor(tj[:, 1, :], jcol[:, :], tj[:, 0, :], ALU.subtract), tok)
                tok = dve.op(lambda e: e.tensor_copy(tji[:, :, :], tj[:, :, :]), tok)
                dt = d
                for i in range(2):
                    dt = slot.dma(sp, lambda e, i=i: e.dma_start(
                        dvec[2 + 2 * k + i:3 + 2 * k + i, :].rearrange("a (c p) -> p (a c)", p=P), tj[:, i, :]),
                        tok, dt)
                    dt = slot.dma(sp, lambda e, i=i: e.dma_start(
                        ivec[2 * k + i:1 + 2 * k + i, :].rearrange("a (c p) -> p (a c)", p=P), tji[:, i, :]),
                        tok, dt)
                return dt
            return rest

        def start(stack, en, sl):
            pe, dve, act, pool, sp = (en[k] for k in ("pe", "dve", "act", "pool", "sp"))
            inti = sb(stack, "inti", [P, P], I32)
            da = sb(stack, "da", [125, 1600], I32)
            db = sb(stack, "db", [125, 1600], I32)
            df = sb(stack, "df", [125, 1600])
            ds = sb(stack, "ds", [P, 1])
            a = pool.op(lambda e: e.iota(inti[:, :], pattern=[[1, P]], base=0, channel_multiplier=0))
            t_iota = dve.op(lambda e: e.tensor_copy(iota[:, :], inti[:, :]), a)
            a = pool.op(lambda e: e.iota(inti[:, :], pattern=[[1, P]], base=0, channel_multiplier=-1), t_iota)
            t1 = dve.op(lambda e: e.tensor_scalar(ident[:, :], inti[:, :], 0.0, None, ALU.is_equal), a)
            t2 = dve.op(lambda e: e.tensor_scalar(tri[:, :], inti[:, :], 0.0, None, ALU.is_gt), a)
            t_tri = dve.op(lambda e: e.tensor_copy(trib[:, :], tri[:, :]), t2)
            t_onesb = dve.op(lambda e: e.memset(onesb[:, :], 1.0))

            dve.op(lambda e: e.tensor_copy(iotab[:, :], iota[:, :]), t_iota)
            dve.op(lambda e: e.tensor_copy(identb[:, :], ident[:, :]), t1)
            for i, (to, vec) in enumerate(((srcs, src), (dsts, dst), (ws, edge_weight))):
                sl["cp"][i].dma(sp, lambda e, to=to, vec=vec: e.dma_start(
                    to.rearrange("(p e) -> p e", e=3125), vec.rearrange("(p e) -> p e", e=3125)))
            z = dve.op(lambda e: e.memset(db[:, :], 1 << 20))
            z2 = dve.op(lambda e: e.memset(ds[:, :], 0.0))
            la = sl["ld"][0].dma(sp, lambda e: e.dma_start(da[:, :], dst.rearrange("(p e) -> p e", e=1600)))
            lb = sl["ld"][1].dma(sp, lambda e: e.dma_start(db[0:124, :],
                                                           dst[1:1 + 124 * 1600].rearrange("(p e) -> p e", e=1600)), z)
            lc = sl["ld"][2].dma(sp, lambda e: e.dma_start(db[124:125, 0:1599],
                                                           dst[1 + 124 * 1600:E].rearrange("(p e) -> p e", e=1599)))
            a = dve.op(lambda e: e.tensor_tensor(df[:, :], da[:, :], db[:, :], ALU.is_gt), la, lb, lc)
            a = dve.op(lambda e: e.tensor_reduce(ds[0:125, :], df[:, :], AX.X, ALU.add), a, z2)
            onef = sb(stack, "onef", [P, 1])
            o = dve.op(lambda e: e.memset(onef[:, :], 1.0))
            a = pe.op(lambda e: e.matmul(psum[0][0:1, 0:1], lhsT=ds[:, :], rhs=onef[:, :], start=True, stop=True), a, o)
            dve.op(lambda e: e.tensor_copy(unsorted[:, :], psum[0][0:1, 0:1]), a)
            sp.waits([c.token for c in sl["cp"]])

        phase("start", start, {"cp": 3, "ld": 3})

        def sort_pass(k):
            def program(stack, en, sl):
                pe, dve, act, pool, sp = (en[x] for x in ("pe", "dve", "act", "pool", "sp"))
                (ld,) = sl["ld"]
                rec = sb(stack, f"rec{k}", [P, T, 4])
                ri = sb(stack, f"ri{k}", [P, 2, T], I32)
                keyT = sb(stack, f"keyT{k}", [P, T], BF16)
                posI = sb(stack, f"posI{k}", [P, T], I32)
                z = dve.op(lambda e: e.memset(ri[:, :, :], 16383))
                z1 = dve.op(lambda e: e.memset(rec[:, :, :], 0.0))
                full = (T - 1) * P
                if k == 0:
                    for i, vec in enumerate((srcs, dsts)):
                        l = ld.dma(sp, lambda e, i=i, vec=vec: e.dma_start(
                            ri[:, i, 0:T - 1], vec[0:full].rearrange("(t p) -> p t", p=P)), z, ld.token)
                        l = ld.dma(sp, lambda e, i=i, vec=vec: e.dma_start(
                            ri[0:64, i, T - 1:T], vec[full:E].rearrange("(t p) -> p t", p=64)), l)
                    l = ld.dma(sp, lambda e: e.dma_start(
                        rec[:, 0:T - 1, 2], ws[0:full].rearrange("(t p) -> p t", p=P)), z1, l)
                    l = ld.dma(sp, lambda e: e.dma_start(
                        rec[0:64, T - 1, 2:3], ws[full:E].rearrange("(t p) -> p t", p=64)), l)
                    for i in range(2):
                        l = dve.op(lambda e, i=i: e.tensor_copy(rec[:, :, i], ri[:, i, :]), ld.token)
                else:
                    l = ld.dma(sp, lambda e: e.dma_start(rec[:, :, :], recs[0].rearrange("(t p) f -> p t f", p=P)),
                               z1)
                    l = dve.op(lambda e: e.tensor_copy(ri[:, 1, :], rec[:, :, 1]), l, z)
                if k == 0:
                    a = dve.op(lambda e: e.tensor_scalar(ri[:, 0, :], ri[:, 1, :], 127, None, ALU.bitwise_and), l)
                else:
                    a = dve.op(lambda e: e.tensor_scalar(ri[:, 0, :], ri[:, 1, :], 7, None,
                                                         ALU.logical_shift_right), l)
                a = dve.op(lambda e: e.tensor_copy(keyT[:, 0:T], ri[:, 0, :]), a)
                pos, r = ranks(stack, en, keyT, [a], f"s{k}")
                a = dve.op(lambda e: e.tensor_copy(posI[:, :], pos[:, 0:T]), r)
                for t in range(T):
                    s = sl["sc"][t % 8]
                    s.dma(pool, lambda e, t=t: e.indirect_dma_start(
                        recs[k], bass.IndirectOffsetOnAxis(ap=posI[:, t:t + 1], axis=0), rec[:, t, :], None),
                        a, s.token)
                done = [s.token for s in sl["sc"]]
                if k == 1:
                    l = ld.dma(sp, lambda e: e.dma_start(rec[:, :, :], recs[1].rearrange("(t p) f -> p t f", p=P)),
                               *done)
                    for i in range(2):
                        a = dve.op(lambda e, i=i: e.tensor_copy(ri[:, i, :], rec[:, :, i]), l)
                    dve_done = a
                    for i, (vec, t) in enumerate(((srcs, ri[:, 0, :]), (dsts, ri[:, 1, :]), (ws, rec[:, :, 2]))):
                        l = ld.dma(sp, lambda e, vec=vec, t=t: e.dma_start(
                            vec[0:full].rearrange("(t p) -> p t", p=P), t[:, 0:T - 1]), dve_done, l)
                        l = ld.dma(sp, lambda e, vec=vec, t=t: e.dma_start(
                            vec[full:E].rearrange("(t p) -> p t", p=64), t[0:64, T - 1:T]), l)
                    done.append(l)
                sp.waits(done)
            return program

        with nc.If(nc.values_load(unsorted[0:1, 0:1], min_val=0, max_val=E) > 0):
            phase("sort0", sort_pass(0), {"ld": 1, "sc": 8}, unless_sorted)
            phase("sort1", sort_pass(1), {"ld": 1, "sc": 8}, unless_sorted)

        def prep(stack, en, sl):
            pe, dve, act, pool, sp = (en[k] for k in ("pe", "dve", "act", "pool", "sp"))
            (gen,), (gen2,) = sl["gen"], sl["gen2"]
            (ld0,), (ld1,), (ld2,) = sl["ld0"], sl["ld1"], sl["ld2"]
            sbT = sb(stack, "sbT", [P, T], BF16)
            cvec = sb(stack, "cvec", [P, 13])
            epst = sb(stack, "epst", [P, 1])
            stt = sb(stack, "stt", [P, 4, 6])
            mv = sb(stack, "mv", [P, NB, 2])
            sc = sb(stack, "sc", [P, 3, NB])
            first = stack.enter_context(ExitStack())
            ints = sb(first, "ints", [P, 2, 13, P], I32)
            blk = sb(first, "blk", [P, 13, P], I32)
            fr = sb(first, "fr", [P, 13, 5, P])
            sblkf = sb(first, "sblkf", [P, 13, P])
            cblk = sb(first, "cblk", [P, 13])

            m0 = dve.op(lambda e: e.memset(ints[:, :, :, :], 16383))
            m1 = dve.op(lambda e: e.memset(fr[:, 12, 2, :], 0.0))
            mh = dve.op(lambda e: e.memset(h[:, NB - 1, :], 0.0))
            t_eps = dve.op(lambda e: e.memset(epst[:, :], 1e-5))
            full = 12 * P * P
            rest = full + 26 * P

            def load_rows(slot, dst_ap, vec, *tok):
                slot.dma(sp, lambda e: e.dma_start(dst_ap(slice(0, P), slice(0, 12), P),
                                                   vec[0:full].rearrange("(c p e) -> p c e", p=P, e=P)), *tok)
                slot.dma(sp, lambda e: e.dma_start(dst_ap(slice(0, 26), 12, P),
                                                   vec[full:rest].rearrange("(p e) -> p e", e=P)))
                slot.dma(sp, lambda e: e.dma_start(dst_ap(slice(26, 27), 12, 64),
                                                   vec[rest:E].rearrange("(p e) -> p e", e=64)))
            load_rows(ld0, lambda p, c, n: ints[p, 0, c, 0:n], srcs, m0)
            load_rows(ld1, lambda p, c, n: ints[p, 1, c, 0:n], dsts, m0)
            load_rows(ld2, lambda p, c, n: fr[p, c, 2, 0:n], ws, m1)
            xl = []
            for i, (b0, b1) in enumerate(((0, 25), (25, 50), (50, 75), (75, NB - 1))):
                xl += [sl["x"][i].dma(act, lambda e, b0=b0, b1=b1: e.dma_start(
                    h[:, b0:b1, :], x[b0 * P:b1 * P, :].rearrange("(b p) d -> p b d", p=P)))] * (b1 - b0)
            xl.append(sl["x"][4].dma(act, lambda e: e.dma_start(h[0:NLAST, NB - 1, :], x[(NB - 1) * P:N, :]), mh))

            a = dve.op(lambda e: e.tensor_scalar(blk[:, :, :], ints[:, 0, :, :], 7, None, ALU.logical_shift_right),
                       ld0.token)
            t_sblk = dve.op(lambda e: e.tensor_copy(sblkf[:, :, :], blk[:, :, :]), a)
            f_src = dve.op(lambda e: e.tensor_copy(fr[:, :, 0, :], ints[:, 0, :, :]))
            f_dst = dve.op(lambda e: e.tensor_copy(fr[:, :, 1, :], ints[:, 1, :, :]), ld1.token)
            a = dve.op(lambda e: e.tensor_scalar(blk[:, :, 0], ints[:, 1, :, 0], 7, None, ALU.logical_shift_right),
                       t_sblk)
            a = dve.op(lambda e: e.tensor_copy(cvec[:, :], blk[:, :, 0]), a)
            finish_pairs = pairs(first, en, gen, 0, cvec[:, :], [a])
            k1 = dve.op(lambda e: e.memset(fr[:, :, 3, 0:1], 1.0))
            k2 = dve.op(lambda e: e.memset(fr[:, :, 4, P - 1:P], 1.0))
            k3 = dve.op(lambda e: e.tensor_tensor(fr[:, :, 3, 1:P], fr[:, :, 1, 1:P], fr[:, :, 1, 0:P - 1],
                                                  ALU.not_equal), f_dst)
            k4 = dve.op(lambda e: e.tensor_copy(fr[:, :, 4, 0:P - 1], fr[:, :, 3, 1:P]), k3)
            t_fields = gen2.dma(sp, lambda e: e.dma_start(
                fields.rearrange("(c p) f -> p c f", p=P), fr[:, :, :, :].rearrange("p c a b -> p c (a b)")),
                k1, k2, k4, f_src, ld2.token)

            prev = [None, None]
            for c in range(13):
                b = psum[c % 2]
                a = pe.op(lambda e, c=c, b=b: e.transpose(b[:, 0:P], sblkf[:, c, :], ident[:, :]),
                          t_sblk, prev[c % 2])
                n = min(P, T - c * P)
                prev[c % 2] = act.op(lambda e, c=c, b=b, n=n: e.copy(sbT[:, c * P:c * P + n], b[:, 0:n]), a)

            dt = finish_pairs()
            for q in (pe, dve, act, pool, sp):
                q.waits([dt, t_fields, prev[0], prev[1]])
            first.close()
            crow = sb(stack, "crow", [P, 13, P])

            def stats():
                free = [None] * 4
                last = None
                for b in range(NB):
                    a = dve.op(lambda e, b=b: e.bn_stats(stt[:, b % 4, :], h[:, b, :]), xl[b], free[b % 4])
                    last = free[b % 4] = dve.op(lambda e, b=b: e.bn_aggr(mv[:, b, :], stt[:, b % 4, :]), a)
                norm_all(dve, act, mv, sc, epst, last, t_eps)
                for b in range(NB):
                    act.op(lambda e, b=b: e.activation(h[:, b, :], h[:, b, :], ACT.Relu, bias=sc[:, 2, b:b + 1],
                                                       scale=sc[:, 1, b:b + 1]), (dve.sem, dve.count))

            C, base, t_base, t_C = histogram(stack, en, sbT, [prev[0], prev[1]], "a", stats)
            gen.dma(sp, lambda e: e.dma_start(bvec.rearrange("a b -> b a"), base[:, :]), t_base, dt)
            z = dve.op(lambda e: e.memset(C[:, T:JP], 0.0), t_C)
            prev = [None] * 2
            for c in range(13):
                b = psum[c % 2]
                a = pe.op(lambda e, c=c, b=b: e.transpose(b[:, 0:P], C[:, c * P:(c + 1) * P], ident[:, :]),
                          z, prev[c % 2])
                prev[c % 2] = dve.op(lambda e, c=c, b=b: e.tensor_copy(crow[:, c, :], b[:, 0:P]), a)
            dt = gen2.dma(sp, lambda e: e.dma_start(starts.rearrange("(c p) e -> p c e", p=P), crow[:, :, :]),
                          prev[0], prev[1], t_fields)
            sp.waits([dt, gen.token])

        def norm_all(dve, act, mv, sc, epst, *tok):
            a = act.op(lambda e: e.activation(sc[:, 0, :], mv[:, :, 1], ACT.Sqrt, bias=epst[:, :], scale=1.0), *tok)
            a = dve.op(lambda e: e.reciprocal(sc[:, 1, :], sc[:, 0, :]), a)
            return dve.op(lambda e: e.scalar_tensor_tensor(out=sc[:, 2, :], in0=mv[:, :, 0], scalar=-1.0,
                                                           in1=sc[:, 1, :], op0=ALU.mult, op1=ALU.mult), a)

        hstack = top.enter_context(ExitStack())
        h = sb(hstack, "h", [P, NB, D])
        phase("prep", prep, {"gen": 1, "gen2": 1, "ld0": 1, "ld1": 1, "ld2": 1, "x": 5})

        def l0a(stack, en, sl):
            pe, dve, act, pool, sp = (en[k] for k in ("pe", "dve", "act", "pool", "sp"))
            (gen,), (gen2,) = sl["gen"], sl["gen2"]
            NM = 3 * W
            NT = 20
            brow = sb(stack, "brow", [1, JP], I32)
            dloc = sb(stack, "dloc", [P, JP], BF16)
            sdig = sb(stack, "sdig", [P, JP], BF16)
            wT = sb(stack, "wT", [P, JP])
            sT = sb(stack, "sT", [P, JP])
            msk = sb(stack, "msk", [P, JP])
            Cp = sb(stack, "Cp", [P, JP])
            with ExitStack() as pre:
                tidx = sb(pre, "tidx", [P, 13], I32)
                bbc = sb(pre, "bbc", [P, JP])
                dl = sb(pre, "dl0", [P, JP])
                si = sb(pre, "si", [P, JP], I32)
                fg = sb(pre, "fg", [P, 2, 5 * P])
                cg = sb(pre, "cg", [P, 2, P])
                g = gen.dma(sp, lambda e: e.dma_start(tidx[:, :], ivec[0:1, :].rearrange("a (c p) -> p (a c)", p=P)))
                g = gen.dma(sp, lambda e: e.dma_start(brow[:, :], ivec[1:2, :]))
                g = gen.dma(sp, lambda e: e.dma_start(bbc[:, :], dvec[3:4, :].to_broadcast([P, JP])))
                fgfree = [None] * 2
                psfree = [None] * 4
                for c in range(13):
                    s = c % 2
                    lf = sl["fg"][s].dma(pool, lambda e, c=c, s=s: e.indirect_dma_start(
                        fg[:, s, :], None, fields, bass.IndirectOffsetOnAxis(ap=tidx[:, c:c + 1], axis=0)),
                        g, fgfree[s])
                    lc = sl["cg"][s].dma(pool, lambda e, c=c, s=s: e.indirect_dma_start(
                        cg[:, s, :], None, starts, bass.IndirectOffsetOnAxis(ap=tidx[:, c:c + 1], axis=0)))
                    for i, (dstt, view) in enumerate(((dl, fg[:, s, P:2 * P]), (wT, fg[:, s, 2 * P:3 * P]),
                                                      (sT, fg[:, s, 0:P]), (Cp, cg[:, s, :]))):
                        a = pe.op(lambda e, i=i, view=view: e.transpose(psum[i][:, 0:P], view, ident[:, :]),
                                  lf, lc, psfree[i])
                        if i % 2:
                            psfree[i] = act.op(lambda e, i=i, c=c, dstt=dstt: e.copy(
                                dstt[:, c * P:(c + 1) * P], psum[i][:, 0:P]), a)
                        else:
                            psfree[i] = dve.op(lambda e, i=i, c=c, dstt=dstt: e.tensor_copy(
                                dstt[:, c * P:(c + 1) * P], psum[i][:, 0:P]), a)
                    fgfree[s] = a
                a = dve.op(lambda e: e.scalar_tensor_tensor(out=dl[:, :], in0=bbc[:, :], scalar=-float(P),
                                                            in1=dl[:, :], op0=ALU.mult, op1=ALU.add), *psfree, g)
                b0 = dve.op(lambda e: e.tensor_copy(dloc[:, :], dl[:, :]), a)
                b1 = dve.op(lambda e: e.tensor_scalar(msk[:, :], dl[:, :], 0.0, 1.0e6, ALU.is_lt, ALU.mult), a)
                b2 = dve.op(lambda e: e.tensor_scalar(dl[:, :], dl[:, :], 127.0, 1.0e6, ALU.is_gt, ALU.mult), a, b0, b1)
                b3 = dve.op(lambda e: e.tensor_tensor(msk[:, :], msk[:, :], dl[:, :], ALU.add), b1, b2)
                b4 = dve.op(lambda e: e.tensor_copy(si[:, :], sT[:, :]), psfree[2])
                b4 = dve.op(lambda e: e.tensor_scalar(si[:, :], si[:, :], 7, None, ALU.logical_shift_right), b4)
                b5 = dve.op(lambda e: e.tensor_copy(sdig[:, :], si[:, :]), b4)
            for q in (pe, dve, act, pool, sp):
                q.waits([b3, b5, *psfree, *fgfree, g])
            Ob = sb(stack, "Ob0", [P, 2, W, P], BF16)
            Os = sb(stack, "Os0", [P, 2, W, P], BF16)
            OT = sb(stack, "OT0", [P, NT, P])
            mt = sb(stack, "mtw", [P, NM, ROW])
            scr = sb(stack, "scr0", [P, 2, P])
            pos = sb(stack, "pos0", [P, 2, W])
            posI = sb(stack, "posIw", [P, 3, W], I32)
            zrow = sb(stack, "zrow", [64, ROW])
            basebc = sb(stack, "basebc", [P, P])
            cv = sb(stack, "cv", [P, 13])
            cr = sb(stack, "cr", [P, 13])
            cri = sb(stack, "cri", [P, 13], I32)

            z = dve.op(lambda e: e.memset(zrow[:, :], 0.0))
            z = dve.op(lambda e: e.memset(zrow[:, D:D + 1], 16383.0), z)
            t_z = gen2.dma(sp, lambda e: e.dma_start(msgs[E:T * P, :], zrow[:, :]), z)

            tb = gen.dma(sp, lambda e: e.dma_start(basebc[:, :], bvec.to_broadcast([P, P])), g)
            a = pool.op(lambda e: e.iota(cri[:, :], pattern=[[P * P, 13]], base=0, channel_multiplier=P))
            a = dve.op(lambda e: e.tensor_copy(cr[:, :], cri[:, :]), a)
            last = None
            for c in range(13):
                last = dve.op(lambda e, c=c: e.tensor_scalar(scr[:, c % 2, 1:P], basebc[:, 1:P], cr[:, c:c + 1], 0.0,
                                                             ALU.is_le, ALU.add, accum_out=cv[:, c:c + 1]),
                              tb, a, last)
            finish_pairs = pairs(stack, en, gen, 1, cv[:, :], [last])

            vals = {}
            obtok, ostok, otok, hetok, hedone, rktok, scaled, ranked = ({} for _ in range(8))
            bank = {k: None for k in range(8)}
            mfree = [None] * NM
            pos_free = [None] * 2
            scrfree = [last, last]

            def onehots(w):
                n = min(W, J - w * W)
                j0 = w * W
                obtok[w] = dve.op(lambda e: e.tensor_tensor(
                    Ob[:, w % 2, 0:n, :], bcast(iotab[:, :], n), rows_of(dloc[:, j0:j0 + n]), ALU.is_equal),
                    otok.get((j0 - W) // 4 - 1))
                ostok[w] = dve.op(lambda e: e.tensor_tensor(
                    Os[:, w % 2, 0:n, :], bcast(iotab[:, :], n), rows_of(sdig[:, j0:j0 + n]), ALU.is_equal),
                    ranked.get(j0 - W - 1))

            def columns(j):
                if j >= J:
                    return
                psb = psum[0][:, :].bitcast(BF16)
                w = j // W
                for i in range(4):
                    t = pe.op(lambda e, i=i: e.transpose(psb[:, i * P:(i + 1) * P], Ob[:, w % 2, j % W + i, :],
                                                         identb[:, :]), obtok[w], bank[0])
                bank[0] = otok[j // 4] = act.op(lambda e: e.copy(
                    OT[:, j % NT:j % NT + 4, :], psb[:, 0:4 * P].rearrange("p (j n) -> p j n", n=P)), t,
                    hedone.get(j - NT + 3))

            def products(j):
                if j % 4 == 0:
                    m = min(4, J - j)

                    def ld(e):
                        r = four(vals, e, "l0a")
                        e.load(r[:m], brow[0:1, j:j + m])
                        vals["v"] = [e.snap(x, min_val=0, max_val=NB - 1) for x in r[:m]]
                    pe.do(ld)
                k = 1 + j % 3
                hetok[j] = hedone[j] = pe.op(lambda e: e.matmul(
                    psum[k][:, 0:D], lhsT=OT[:, j % NT, :],
                    rhs=h[:, bass.ds(vals["v"][j % 4], 1), :].rearrange("p a b -> p (a b)"), start=True, stop=True),
                    otok[j // 4], bank[k])
                k2 = 4 + j % 3
                rktok[j] = rank(en, Os[:, j // W % 2, j % W, :], Cp, j, k2, ostok[j // W], bank[k2])

            def weigh(j):
                k = 1 + j % 3
                scaled[j] = bank[k] = act.op(lambda e: e.activation(mt[:, j % NM, 0:D], psum[k][:, 0:D], ACT.Copy,
                                                                    scale=wT[:, j:j + 1]),
                                             hetok.pop(j), mfree[j % NM])
                k2 = 4 + j % 3
                r = ranked[j] = bank[k2] = scrfree[j % 2] = dve.op(lambda e: e.tensor_tensor_reduce(
                    scr[:, j % 2, :], Os[:, j // W % 2, j % W, :], psum[k2][:, 0:P], 1.0, 0.0, ALU.mult, ALU.add,
                    pos[:, j // W % 2, j % W:j % W + 1]), rktok.pop(j), pos_free[j // W % 2], scrfree[j % 2])
                if j % W == W - 1 or j == J - 1:
                    w = j // W
                    n = j % W + 1
                    j0 = w * W
                    s0 = j0 % NM
                    c = dve.op(lambda e: e.tensor_copy(mt[:, s0:s0 + n, D], sT[:, j0:j0 + n]), *mfree[s0:s0 + n])
                    a = pos_free[w % 2] = dve.op(lambda e: e.tensor_tensor(
                        posI[:, w % 3, 0:n], pos[:, w % 2, 0:n], msk[:, j0:j0 + n], ALU.add), r, *mfree[s0:s0 + n])
                    for i in range(n):
                        mfree[s0 + i] = sl["ms"][s0 + i].dma(pool, lambda e, i=i: e.indirect_dma_start(
                            msgs, bass.IndirectOffsetOnAxis(ap=posI[:, w % 3, i:i + 1], axis=0),
                            mt[:, s0 + i, :], None, bounds_check=E - 1, oob_is_err=False), scaled[j0 + i], c, a)

            onehots(0)
            columns(0)
            columns(4)

            def step(j):
                if j % W == 2 and j // W + 1 < NW:
                    onehots(j // W + 1)
                    columns(j + 6)
                if j % W == 5:
                    columns(j + 7)
                products(j)
            pipeline([step, lambda j: None, weigh], J)
            dt = finish_pairs()
            pool.waits(mfree)
            sp.waits([dt, t_z])

        phase("l0a", l0a, {"gen": 1, "gen2": 1, "fg": 2, "cg": 2, "ms": 3 * W})
        hstack.close()

        def l0b(stack, en, sl):
            pe, dve, act, pool, sp = (en[k] for k in ("pe", "dve", "act", "pool", "sp"))
            (gen,) = sl["gen"]
            acc = sb(stack, "acc0", [P, NB, D])
            az = pool.op(lambda e: e.memset(acc[:, :, :], 0.0))
            wts = sb(stack, "wts", [P, 2, D])
            wt = sb(stack, "wt", [P, 2, 3, D])
            bias = sb(stack, "bias", [P, 3, D])
            epst = sb(stack, "epst1", [P, 1])
            t_eps = dve.op(lambda e: e.memset(epst[:, :], 1e-5))
            w = sl["w"]
            t_w = w[0].dma(act, lambda e: e.dma_start(wts[:, :, :], weight.rearrange("(a p) d -> p a d", p=P)))
            for i, bb in enumerate((bq, bk, bv)):
                bt = w[1].dma(act, lambda e, i=i, bb=bb: e.dma_start(
                    bias[:, i, :], bb.rearrange("(a d) -> a d", a=1).to_broadcast([P, D])))
            part = stack.enter_context(ExitStack())
            NM = 3 * W
            wraw = sb(part, "wraw", [P, 3, 2, D])
            bbc = sb(part, "bbc1", [P, JP])
            rows = sb(part, "rows1", [1, 2, JP], I32)
            mt = sb(part, "mt1", [P, NM, ROW])
            O = sb(part, "O1", [P, 2, W, P])
            sl8 = sb(part, "sl8", [P, 2, W])
            for i, ww in enumerate((Wq, Wk, Wv)):
                lw = w[2].dma(act, lambda e, ww=ww, i=i: e.dma_start(wraw[:, i, :, :],
                                                                     ww.rearrange("(a p) d -> p a d", p=P)))
            g = gen.dma(sp, lambda e: e.dma_start(rows[:, 0, :], ivec[2:3, :]))
            g = gen.dma(sp, lambda e: e.dma_start(rows[:, 1, :], ivec[3:4, :]))
            g = gen.dma(sp, lambda e: e.dma_start(bbc[:, :], dvec[5:6, :].to_broadcast([P, JP])))
            k = dve.op(lambda e: e.tensor_scalar(bbc[:, :], bbc[:, :], float(P), None, ALU.mult), g)
            c = [None] * 2
            for i in range(3):
                for a in range(2):
                    for b in range(2):
                        q = (a + b) % 2
                        t = pe.op(lambda e, a=a, b=b, i=i, q=q: e.transpose(
                            psum[6 + q][:, 0:P], wraw[:, i, a, b * P:(b + 1) * P], ident[:, :]), lw, c[q])
                        c[q] = act.op(lambda e, a=a, b=b, i=i, q=q: e.copy(
                            wt[:, b, i, a * P:(a + 1) * P], psum[6 + q][:, 0:P]), t)
            t_wt = c

            mfree = [None] * NM
            bank = [None] * 4
            ofree = [None] * 2
            vs, vd = {}, {}
            mtok, otok, ptok = {}, {}, {}
            S = {"acc": None}
            sp.waits([g])
            dve.waits([az, k])

            def load(w):
                for j in range(w * W, min(J, (w + 1) * W)):
                    if j % 4 == 0:
                        n = min(4, J - j)

                        def lds(e, j=j, n=n):
                            r = four(vs, e, "l0s")
                            e.load(r[:n], rows[0:1, 0, j:j + n])
                            vs["v"] = [e.snap(x, min_val=0, max_val=T - 1) for x in r[:n]]
                        sp.do(lds)
                    mtok[j] = sl["m"][j % NM].dma(sp, lambda e, j=j: e.dma_start(
                        mt[:, j % NM, :], msgs[bass.ds(vs["v"][j % 4] * P, P), :]), mfree[j % NM])

            def onehots(w):
                if w >= NW:
                    return
                j0 = w * W
                n = min(W, J - j0)
                s0 = j0 % NM
                a = dve.op(lambda e: e.tensor_tensor(sl8[:, w % 2, 0:n], mt[:, s0:s0 + n, D], bbc[:, j0:j0 + n],
                                                     ALU.subtract), *[mtok[j] for j in range(j0, j0 + n)])
                otok[w] = dve.op(lambda e: e.tensor_tensor(
                    O[:, w % 2, 0:n, :], bcast(iota[:, :], n), rows_of(sl8[:, w % 2, 0:n]), ALU.is_equal),
                    a, ofree[w % 2])

            def product(j):
                w = j // W
                for f in range(2):
                    m = pe.op(lambda e, f=f: e.matmul(
                        psum[j % 4][:, f * P:(f + 1) * P], lhsT=mt[:, j % NM, f * P:(f + 1) * P],
                        rhs=O[:, w % 2, j % W, :], start=True, stop=True), mtok[j], otok[w], bank[j % 4])
                ptok[j] = mfree[j % NM] = ofree[w % 2] = m

            def add(j):
                if j % 4 == 0:
                    n = min(4, J - j)

                    def ld(e):
                        r = four(vd, e, "l0d")
                        e.load(r[:n], rows[0:1, 1, j:j + n])
                        vd["v"] = [e.snap(x, min_val=0, max_val=NB - 1) for x in r[:n]]
                    dve.do(ld)

                def fn(e):
                    t = acc[:, bass.ds(vd["v"][j % 4], 1), :].rearrange("p a b -> p (a b)")
                    return e.tensor_tensor(t, t, psum[j % 4][:, 0:D], ALU.add)
                S["acc"] = bank[j % 4] = dve.op(fn, ptok.pop(j), S["acc"])

            load(0)
            load(1)
            onehots(0)

            def step(j):
                if j % W == 0 and j // W + 2 < NW:
                    load(j // W + 2)
                if j % W == 4:
                    onehots(j // W + 1)
                product(j)
            pipeline([step, lambda j: None, add], J)
            last = S["acc"]
            for q in (pe, dve, act, pool, sp):
                q.waits([last, t_w, bt, *t_wt, *mfree])
            part.close()

            NX = 6
            xt = sb(stack, "xt1", [P, NX, D])
            stt = sb(stack, "stt1", [P, 4, 6])
            mv = sb(stack, "mv1", [P, NB, 2])
            sc = sb(stack, "sc1", [P, 3, NB])
            z = dve.op(lambda e: e.memset(xt[:, (NB - 1) % NX, :], 0.0))
            xfree = [None] * NX
            bank = [last] * 4
            sfree = [None] * 4
            l, m, a = {}, {}, {}

            def x_load(b):
                s = b % NX
                n = P if b < NB - 1 else NLAST
                zz = dve.op(lambda e: e.memset(xt[:, s, :], 0.0), xfree[s]) if b == NB - 1 else None
                l[b] = sl["x"][s].dma(sp, lambda e: e.dma_start(xt[0:n, s, :], x[b * P:b * P + n, :]), xfree[s], zz, z)

            def x_product(b):
                for f in range(2):
                    m[b] = pe.op(lambda e, f=f: e.matmul(psum[b % 4][:, 0:D], lhsT=acc[:, b, f * P:(f + 1) * P],
                                                         rhs=wts[:, f, :], start=(f == 0), stop=(f == 1)), bank[b % 4])

            def x_add(b):
                a[b] = bank[b % 4] = xfree[b % NX] = dve.op(lambda e: e.tensor_tensor(
                    acc[:, b, :], xt[:, b % NX, :], psum[b % 4][:, 0:D], ALU.add), m[b], l[b])

            def x_stats(b):
                sfree[b % 4] = dve.op(lambda e: e.bn_stats(stt[:, b % 4, :], acc[:, b, :]), a[b], sfree[b % 4])
                sl["st"][b % 4].dma(sp, lambda e: e.dma_start(x1t[b * P:(b + 1) * P, :], acc[:, b, :]), a[b],
                                    sl["st"][b % 4].token)

            def x_aggr(b):
                sfree[b % 4] = dve.op(lambda e: e.bn_aggr(mv[:, b, :], stt[:, b % 4, :]), sfree[b % 4])
            pipeline([x_load, lambda b: None, lambda b: None, x_product, x_add, x_stats, x_aggr], NB)
            nrm = norm_all(dve, act, mv, sc, epst, *sfree, t_eps)

            NY = 3
            ht = sb(stack, "ht1", [P, NY, D])
            hT = sb(stack, "hT1", [P, NY, D])
            qo = sb(stack, "qo", [P, NY, D])
            kvo = sb(stack, "kvo", [P, NY, KVW])
            t_one = dve.op(lambda e: e.memset(kvo[:, :, :], 1.0))
            hd, tr, cp, qm, km = {}, {}, {}, {}, {}
            bank = [None] * 8
            hfree = [None] * NY
            hTfree = [None] * NY
            ofree = [None] * NY

            def h_norm(b):
                s = b % NY
                hd[b] = act.op(lambda e: e.activation(ht[:, s, :], acc[:, b, :], ACT.Relu, bias=sc[:, 2, b:b + 1],
                                                      scale=sc[:, 1, b:b + 1]), nrm, hfree[s])

            def h_turn(b):
                k = b % 2
                for f in range(2):
                    tr[b] = pe.op(lambda e, f=f: e.transpose(psum[k][:, f * P:(f + 1) * P],
                                                             ht[:, b % NY, f * P:(f + 1) * P], ident[:, :]),
                                  hd[b], bank[k])
                hfree[b % NY] = tr[b]
                cp[b] = bank[k] = act.op(lambda e: e.copy(hT[:, b % NY, :], psum[k][:, 0:D]), tr[b], hTfree[b % NY])

            def h_products(b):
                k = 2 + b % 2
                for f in range(2):
                    qm[b] = pe.op(lambda e, f=f: e.matmul(psum[k][:, 0:D], lhsT=hT[:, b % NY, f * P:(f + 1) * P],
                                                          rhs=wt[:, f, 0, :], start=(f == 0), stop=(f == 1)),
                                  cp[b], bank[k])
                k2 = 4 + b % 3
                for f in range(2):
                    km[b] = pe.op(lambda e, f=f: e.matmul(
                        psum[k2][:, :], lhsT=hT[:, b % NY, f * P:(f + 1) * P],
                        rhs=wt[:, f, 1:3, :].rearrange("p a b -> p (a b)"), start=(f == 0), stop=(f == 1)), bank[k2])
                hTfree[b % NY] = km[b]

            def h_out(b):
                s = b % NY
                k, k2 = 2 + b % 2, 4 + b % 3
                a1 = bank[k] = dve.op(lambda e: e.tensor_tensor(qo[:, s, :], psum[k][:, 0:D], bias[:, 0, :], ALU.add),
                                      qm[b], ofree[s])
                dve.op(lambda e: e.tensor_tensor(kvo[:, s, 0:D], psum[k2][:, 0:D], bias[:, 1, :], ALU.add),
                       km[b], t_one)
                a3 = bank[k2] = dve.op(lambda e: e.tensor_tensor(
                    kvo[:, s, D:KVW].rearrange("p (h d) -> p h d", h=NH)[:, :, 0:32],
                    psum[k2][:, D:2 * D].rearrange("p (h d) -> p h d", h=NH),
                    bias[:, 2, :].rearrange("p (h d) -> p h d", h=NH), ALU.add))
                o = sl["qo"][s]
                o.dma(sp, lambda e: e.dma_start(qt[b * P:(b + 1) * P, :], qo[:, s, :]), a1)
                ofree[s] = o.dma(sp, lambda e: e.dma_start(kvt[b * P:(b + 1) * P, :], kvo[:, s, :]), a3)
            pipeline([h_norm, h_turn, h_products, h_out], NB)
            sp.waits(ofree + [q.token for q in sl["st"]])

        phase("l0b", l0b, {"gen": 1, "m": 3 * W, "w": 3, "x": 6, "st": 4, "qo": 3})

        def l1(stack, en, sl):
            pe, dve, act, pool, sp = (en[k] for k in ("pe", "dve", "act", "pool", "sp"))
            (gen,) = sl["gen"]
            acc = sb(stack, "acc2", [P, NB, NH, 33])
            irow = sb(stack, "irow", [P, JP], I32)
            sI = sb(stack, "sI", [P, JP], I32)
            dloc = sb(stack, "dloc2", [P, JP], BF16)
            FT = sb(stack, "FT", [P, JP], BF16)
            LT = sb(stack, "LT", [P, JP], BF16)
            link = sb(stack, "link", [P, JP], BF16)
            link0 = sb(stack, "link0", [P, NW])
            NK = 20
            NQ = 4
            NOF = 12
            NT = 20

            az = pool.op(lambda e: e.memset(acc[:, :, :, :], 0.0))
            with ExitStack() as pre:
                tidx = sb(pre, "tidx2", [P, 13], I32)
                same = sb(pre, "same", [P, JP + 1])
                tmp = sb(pre, "tmpI", [P, JP], I32)
                dl = sb(pre, "dl", [P, JP])
                fg = sb(pre, "fg2", [P, 2, 5 * P])
                g = gen.dma(sp, lambda e: e.dma_start(tidx[:, :], ivec[0:1, :].rearrange("a (c p) -> p (a c)", p=P)))
                g = gen.dma(sp, lambda e: e.dma_start(same[:, 1:JP + 1], dvec[3:4, :].to_broadcast([P, JP])))
                fgfree = [None] * 2
                psfree = [None] * 2
                for c in range(13):
                    s = c % 2
                    lf = sl["fg"][s].dma(pool, lambda e, c=c, s=s: e.indirect_dma_start(
                        fg[:, s, :], None, fields, bass.IndirectOffsetOnAxis(ap=tidx[:, c:c + 1], axis=0)),
                        g, fgfree[s])
                    for i, (dstt, k) in enumerate(((dl, 1), (sI, 0), (FT, 3), (LT, 4))):
                        a = pe.op(lambda e, i=i, s=s, k=k: e.transpose(psum[i % 2][:, 0:P],
                                                                       fg[:, s, k * P:(k + 1) * P], ident[:, :]),
                                  lf, psfree[i % 2])
                        if k == 0:
                            psfree[i % 2] = dve.op(lambda e, i=i, c=c, dstt=dstt: e.tensor_scalar(
                                dstt[:, c * P:(c + 1) * P], psum[i % 2][:, 0:P], float(N - 1), None, ALU.min), a)
                        elif k == 3:
                            psfree[i % 2] = act.op(lambda e, i=i, c=c, dstt=dstt: e.activation(
                                dstt[:, c * P:(c + 1) * P], psum[i % 2][:, 0:P], ACT.Copy, scale=-BIG), a)
                        else:
                            psfree[i % 2] = act.op(lambda e, i=i, c=c, dstt=dstt: e.copy(
                                dstt[:, c * P:(c + 1) * P], psum[i % 2][:, 0:P]), a)
                    fgfree[s] = a
                a = dve.op(lambda e: e.scalar_tensor_tensor(
                    out=dloc[:, :], in0=same[:, 1:JP + 1], scalar=-float(P), in1=dl[:, :], op0=ALU.mult,
                    op1=ALU.add), psfree[0], psfree[1], g)
                m = dve.op(lambda e: e.memset(same[:, 0:1], -1.0), g)
                t = dve.op(lambda e: e.tensor_copy(tmp[:, :], same[:, 1:JP + 1]), g)
                r0 = dve.op(lambda e: e.tensor_copy(irow[0:1, :], tmp[0:1, :]), t)
                r1 = dve.op(lambda e: e.tensor_scalar(irow[32:33, :], tmp[32:33, :], NQ - 1, None, ALU.bitwise_and), t)
                a = dve.op(lambda e: e.tensor_tensor(dl[:, :], same[:, 1:JP + 1], same[:, 0:JP], ALU.not_equal), a, m)
                r2 = dve.op(lambda e: e.tensor_copy(irow[64:65, :], dl[64:65, :]), a)
                t1 = dve.op(lambda e: e.tensor_scalar(link[:, :], dl[:, :], -BIG, None, ALU.mult), a)
                t_pre = dve.op(lambda e: e.tensor_scalar(
                    link0[:, :], dl[:, :].rearrange("p (w i) -> p w i", i=W)[:, 0:NW, 0], -BIG, None, ALU.mult), a)
            for q in (pe, dve, act, pool, sp):
                q.waits([r0, r1, r2, t1, t_pre, psfree[0], psfree[1], fgfree[0], fgfree[1]])
            kv = sb(stack, "kv", [P, NK, KVW], F32)
            qb = sb(stack, "qb", [P, NQ, D])
            Ob = sb(stack, "Ob", [P, 2, W, P], BF16)
            Of = sb(stack, "Of", [P, NOF, P])
            OT = sb(stack, "OT2", [P, NT, P])
            prod = sb(stack, "prod", [P, 2, D])
            sims = sb(stack, "sims", [P, 2, NH, W])
            FB = sb(stack, "FB", [P, NH, W])
            FS = sb(stack, "FS", [64, P])
            PM = sb(stack, "PM", [64, P])
            PL = sb(stack, "PL", [P, W, 9])
            absent = sb(stack, "absent", [P, W])
            val = sb(stack, "val", [P, NH, W])
            D0 = sb(stack, "D0", [P, 2, NH, W])
            fw = sb(stack, "fw", [P, NH, W])
            ref = sb(stack, "ref", [P, NH, W])
            carry = sb(stack, "carry", [P, NH])
            alpha = sb(stack, "alpha", [P, 2, NH])
            dd = sb(stack, "dd", [P, NH, W])
            pp = sb(stack, "pp", [P, 2, NH, W])
            pv = sb(stack, "pv", [P, 2, NH * 33])

            t_carry = dve.op(lambda e: e.memset(carry[:, :], -BIG))
            t_d0 = act.op(lambda e: e.activation(D0[:, :, :, :].rearrange("p a b c -> p (a b c)"), iota[:, :],
                                                 ACT.Copy, scale=0.0, bias=-BIG))
            dve.waits([az])
            kvfree = [None] * NK
            ofree = [None] * NOF
            obfree = [None] * 2
            obtok, metok = {}, {}
            prodfree = [None] * 2
            qefree = [None] * 3
            ufree = [None] * 2
            qdone = {}
            kvtok, qtok, otok, qetok, simtok, simfree, oftok = {}, {}, {}, {}, {}, {}, {}
            vs, vp, vd = {}, {}, {}
            S = {"carry": t_carry, "d0": t_d0}

            def onehots(w):
                n = min(W, J - w * W)
                j0 = w * W
                obtok[w] = dve.op(lambda e: e.tensor_tensor(
                    Ob[:, w % 2, 0:n, :], bcast(iotab[:, :], n),
                    dloc[:, j0:j0 + n].rearrange("p (j a) -> p j a", a=1).to_broadcast([P, n, P]), ALU.is_equal),
                    obfree[w % 2])

            def columns(j):
                if j >= J:
                    return
                psb = psum[0][:, :].bitcast(BF16)
                w = j // W
                for i in range(4):
                    t = pe.op(lambda e, i=i: e.transpose(psb[:, i * P:(i + 1) * P], Ob[:, w % 2, j % W + i, :],
                                                         identb[:, :]), obtok[w], S.get("otp"))
                S["otp"] = otok[j // 4] = act.op(lambda e: e.copy(
                    OT[:, j % NT:j % NT + 4, :], psb[:, 0:4 * P].rearrange("p (j n) -> p j n", n=P)), t,
                    metok.get((j - NT) // W))

            def gather(j):
                if j < J:
                    kvtok[j] = sl["kv"][j % NK].dma(pool, lambda e: e.indirect_dma_start(
                        kv[:, j % NK, :], None, kvt, bass.IndirectOffsetOnAxis(ap=sI[:, j:j + 1], axis=0)),
                        kvfree[j % NK])

            def queries(j):
                if j >= J:
                    return
                if j % 4 == 0:
                    m = min(4, J - j)

                    def lds(e):
                        r = four(vs, e, "l1s")
                        e.load(r[:m], irow[0:1, j:j + m])
                        vs["b"] = [e.snap(x, min_val=0, max_val=NB - 1) for x in r[:m]]
                        r = four(vs.setdefault("B", {}), e, "l1t")
                        e.load(r[:m], irow[32:33, j:j + m])
                        vs["s"] = [e.snap(x, min_val=0, max_val=NQ - 1) for x in r[:m]]
                        r = four(vs.setdefault("C", {}), e, "l1u")
                        e.load(r[:m], irow[64:65, j:j + m])
                        vs["n"] = [e.snap(x, min_val=0, max_val=1) for x in r[:m]]
                    sp.do(lds)
                qtok[j] = sl["q"][j % NQ].dma(sp, lambda e: e.dma_start(
                    qb[:, bass.ds(vs["s"][j % 4], 1), :].rearrange("p a d -> p (a d)"),
                    qt[bass.ds(vs["b"][j % 4] * P, P), :], cond=vs["n"][j % 4],
                    bounds_check="skip_entire_dma"), qdone.get(j - NQ))

            def expand(j):
                if j >= J:
                    return
                if j % 4 == 0:
                    m = min(4, J - j)

                    def ldp(e):
                        r = four(vp, e, "l1p")
                        e.load(r[:m], irow[32:33, j:j + m])
                        vp["s"] = [e.snap(x, min_val=0, max_val=NQ - 1) for x in r[:m]]
                    pe.do(ldp)
                qetok[j] = qdone[j] = pe.op(lambda e: e.matmul(
                    psum[1 + j % 3][:, 0:D], lhsT=OT[:, j % NT, :],
                    rhs=qb[:, bass.ds(vp["s"][j % 4], 1), :].rearrange("p a d -> p (a d)"), start=True, stop=True),
                    otok[j // 4], qtok[j], qefree[j % 3])

            def scores(w):
                n = min(W, J - w * W)
                for i in range(n):
                    j = w * W + i
                    gather(j + 4)
                    queries(j + 3)
                    if i == 2 and w + 1 < NW:
                        onehots(w + 1)
                        columns(j + 6)
                    if i == 5:
                        columns(j + 7)
                    expand(j + 2)
                    pr = dve.op(lambda e, j=j: e.tensor_tensor(
                        prod[:, j % 2, :], psum[1 + j % 3][:, 0:D],
                        kv[:, j % NK, 0:D], ALU.mult), qetok.pop(j), kvtok[j], prodfree[j % 2])
                    qefree[j % 3] = pr
                    yield
                    r = prodfree[j % 2] = dve.op(lambda e, j=j, w=w, i=i: e.tensor_reduce(
                        sims[:, w % 2, :, i], prod[:, j % 2, :].rearrange("p (h d) -> p h d", h=NH), AX.X,
                        ALU.add), pr, simfree.get(w - 2))
                    if n < W and i == n - 1:
                        r = dve.op(lambda e, w=w, n=n: e.memset(sims[:, w % 2, :, n:W], 0.0), r)
                    simtok[w] = r
                    yield

            def softmax(w):
                n = min(W, J - w * W)
                j0 = w * W
                fb = act.op(lambda e: e.copy(FB[:, :, :], bcast(FT[:, j0:j0 + W], NH)), S.get("tf"))
                d1 = act.op(lambda e: e.copy(D0[:, 0, :, 1:W], bcast(link[:, j0 + 1:j0 + W], NH)), S.get("scan"),
                            S["d0"])
                d2 = act.op(lambda e: e.copy(D0[:, 1, :, 0:W - 1], bcast(link[:, j0 + 1:j0 + W], NH)))
                tf = S["tf"] = pe.op(lambda e: e.transpose(psum[4][0:64, P:2 * P],
                                                           FB[:, :, :].rearrange("p a b -> p (a b)"), ident[:, :]),
                                     fb, S.get("b4"))
                for k in range(0, n, 4):
                    m = min(4, n - k)
                    for i in range(k, k + m):
                        act.waits([ofree[(j0 + i) % NOF]])
                        oftok[j0 + i] = None
                    o = act.op(lambda e, k=k, m=m: e.copy(Of[:, (j0 + k) % NOF:(j0 + k) % NOF + m, :],
                                                          Ob[:, w % 2, k:k + m, :]), obtok[w])
                    for i in range(k, k + m):
                        oftok[j0 + i] = o
                obfree[w % 2] = o
                ts = pe.op(lambda e: e.transpose(psum[4][0:64, 0:P],
                                                 sims[:, w % 2, :, :].rearrange("p a b -> p (a b)"), ident[:, :]),
                           simtok[w])
                fs = act.op(lambda e: e.copy(FS[:, :], psum[4][0:64, P:2 * P]), tf, ts, S.get("pm"))
                yield
                pm = S["pm"] = dve.op(lambda e: e.tensor_tensor_scan(PM[:, :], FS[:, :], psum[4][0:64, 0:P], 0.0,
                                                                     ALU.add, ALU.max), fs, ts, S.get("tb"))
                tb = S["tb"] = pe.op(lambda e: e.transpose(psum[4][:, 2 * P:2 * P + 64], PM[:, :],
                                                           ident[0:64, 0:64]), pm)
                l2 = act.op(lambda e: e.copy(PL[:, :, NH], LT[:, j0:j0 + W]), S.get("m9"))
                yield
                pl = S["b4"] = dve.op(lambda e: e.tensor_tensor(
                    PL[:, :, 0:NH].rearrange("p j h -> p h j"),
                    psum[4][:, 2 * P:2 * P + 64].rearrange("p (h j) -> p h j", h=NH),
                    bcast(LT[:, j0:j0 + W], NH), ALU.mult), tb, S.get("m9"))
                for i in range(n):
                    m9 = pe.op(lambda e, i=i: e.matmul(psum[5][:, i * 9:(i + 1) * 9], lhsT=Of[:, (j0 + i) % NOF, :],
                                                       rhs=PL[:, i, :], start=True, stop=True),
                               pl, l2, oftok[j0 + i], S.get("d"))
                S["m9"] = m9
                yield
                yield
                v9 = psum[5][:, 0:W * 9].rearrange("p (j k) -> p j k", k=9)
                ab = dve.op(lambda e: e.tensor_scalar(absent[:, 0:n], v9[:, 0:n, NH], BIG, -BIG, ALU.mult, ALU.add),
                            m9)
                if n < W:
                    ab = dve.op(lambda e: e.memset(val[:, :, :], 0.0), ab)
                yield
                v = dve.op(lambda e: e.tensor_tensor(
                    val[:, :, 0:n], v9[:, 0:n, 0:NH].rearrange("p j h -> p h j"), bcast(absent[:, 0:n], NH),
                    ALU.add), ab, S.get("scan"))
                S["val"] = v
                yield
                v = dve.op(lambda e: e.scalar_tensor_tensor(
                    out=val[:, :, 0], in0=carry[:, :], scalar=link0[:, w:w + 1], in1=val[:, :, 0], op0=ALU.add,
                    op1=ALU.max), v, S["carry"])
                yield
                f = dve.op(lambda e: e.tensor_tensor_scan(
                    fw[:, :, :].rearrange("p a b -> p (a b)"), D0[:, 0, :, :].rearrange("p a b -> p (a b)"),
                    val[:, :, :].rearrange("p a b -> p (a b)"), 0.0, ALU.add, ALU.max), v, d1)
                yield
                r = S["scan"] = dve.op(lambda e: e.tensor_tensor_scan(
                    ref[:, :, :].rearrange("p a b -> p (a b)")[:, ::-1],
                    D0[:, 1, :, :].rearrange("p a b -> p (a b)")[:, ::-1],
                    fw[:, :, :].rearrange("p a b -> p (a b)")[:, ::-1], 0.0, ALU.add, ALU.max), f, d2, S.get("me"))
                for i in range(n):
                    me = pe.op(lambda e, i=i: e.matmul(psum[5][:, 128 + i * NH:128 + (i + 1) * NH],
                                                       lhsT=OT[:, (j0 + i) % NT, :], rhs=ref[:, :, i], start=True,
                                                       stop=True), r, S.get("d"))
                metok[w] = S["me"] = me
                yield
                al = dve.op(lambda e: e.scalar_tensor_tensor(
                    out=alpha[:, 0, :], in0=carry[:, :], scalar=link0[:, w:w + 1], in1=ref[:, :, 0], op0=ALU.add,
                    op1=ALU.subtract), r, S.get("ex"))
                ex = S["ex"] = act.op(lambda e: e.activation(alpha[:, 1, :], alpha[:, 0, :], ACT.Exp, scale=SCALE),
                                      al, S.get("resc"))
                S["carry"] = dve.op(lambda e: e.tensor_copy(carry[:, :], ref[:, :, n - 1]), al)
                yield
                d = S["d"] = simfree[w] = dve.op(lambda e: e.tensor_tensor(
                    dd[:, :, 0:n], sims[:, w % 2, :, 0:n],
                    psum[5][:, 128:128 + n * NH].rearrange("p (j h) -> p h j", h=NH), ALU.subtract), me,
                    S.get("pp"))
                S["pp"] = act.op(lambda e: e.activation(pp[:, w % 2, :, 0:n], dd[:, :, 0:n], ACT.Exp, scale=SCALE),
                                 d, S.get(f"ppf{w % 2}"))
                yield

                def rescale(e):
                    r = four(vd, e, "l1d")
                    e.load(r[:1], irow[0:1, j0:j0 + 1])
                    b = e.snap(r[0], min_val=0, max_val=NB - 1)
                    t = acc[:, bass.ds(b, 1), :, :].rearrange("p a h d -> p (a h) d")
                    return e.tensor_tensor(t, t, alpha[:, 1, :].rearrange("p (h a) -> p h a", a=1)
                                           .to_broadcast([P, NH, 33]), ALU.mult)
                S["acc"] = S["resc"] = dve.op(rescale, ex, S.get("acc"))
                yield

            def sums(w):
                n = min(W, J - w * W)
                utok = {}

                def weigh(i):
                    j = w * W + i
                    p = kvfree[j % NK] = dve.op(lambda e: e.tensor_tensor(
                        pv[:, j % 2, :].rearrange("p (h d) -> p h d", h=NH),
                        kv[:, j % NK, D:KVW].rearrange("p (h d) -> p h d", h=NH),
                        pp[:, w % 2, :, i:i + 1].to_broadcast([P, NH, 33]), ALU.mult),
                        S["pp"], S.get(f"pv{j % 2}"), kvtok.pop(j))
                    utok[i] = S[f"pv{j % 2}"] = ofree[j % NOF] = pe.op(lambda e: e.matmul(
                        psum[6 + j % 2][:, 0:NH * 33], lhsT=Of[:, j % NOF, :], rhs=pv[:, j % 2, :], start=True,
                        stop=True), p, ufree[j % 2])
                    S[f"ppf{w % 2}"] = p

                def add(i):
                    j = w * W + i
                    if i % 4 == 0:
                        m = min(4, n - i)

                        def ld(e):
                            r = four(vd, e, "l1d")
                            e.load(r[:m], irow[0:1, j:j + m])
                            vd["v"] = [e.snap(x, min_val=0, max_val=NB - 1) for x in r[:m]]
                        dve.do(ld)

                    def fn(e):
                        t = acc[:, bass.ds(vd["v"][i % 4], 1), :, :].rearrange("p a h d -> p (a h d)")
                        return e.tensor_tensor(t, t, psum[6 + j % 2][:, 0:NH * 33], ALU.add)
                    S["acc"] = ufree[j % 2] = dve.op(fn, utok.pop(i), S["acc"])

                weigh(0)
                yield
                for i in range(1, n):
                    weigh(i)
                    yield
                    add(i - 1)
                    yield
                add(n - 1)
                yield

            for j in range(4):
                gather(j)
            for j in range(3):
                queries(j)
            onehots(0)
            columns(0)
            columns(4)
            expand(0)
            expand(1)
            for w in range(NW + 1):
                one = scores(w) if w < NW else iter(())
                two = softmax(w - 1) if w >= 1 else iter(())
                three = sums(w - 1) if w >= 1 else iter(())
                turns = 0
                live = True
                while live:
                    live = next(one, 1) is None
                    if next(two, 1) is None:
                        live = True
                    else:
                        for _ in range(4):
                            live = (next(three, 1) is None) or live
                    turns += 1
            S_acc = S["acc"]

            w = sl["w"]
            wraw = kv[:, 0:1, 0:2 * D].rearrange("p a (b d) -> p (a b) d", b=2)
            wot = kv[:, 1:2, 0:2 * D].rearrange("p a (b d) -> p (a b) d", b=2)
            bias = kv[:, 2, 0:D]
            l = w[0].dma(sp, lambda e: e.dma_start(wraw, Wo.rearrange("(a p) d -> p a d", p=P)), *kvfree)
            bt = w[1].dma(sp, lambda e: e.dma_start(
                bias, bo.rearrange("(a d) -> a d", a=1).to_broadcast([P, D])))
            c = None
            for a in range(2):
                for b in range(2):
                    t = pe.op(lambda e, a=a, b=b: e.transpose(psum[0][:, 0:P], wraw[:, a, b * P:(b + 1) * P],
                                                              ident[:, :]), l, c, S["otp"])
                    c = act.op(lambda e, a=a, b=b: e.copy(wot[:, b, a * P:(a + 1) * P], psum[0][:, 0:P]), t,
                               *kvfree)
            t_wo = c
            rs = sb(stack, "rs", [P, 2, NH])
            ofr = [None] * 2
            xf = [None] * 2
            p1 = p2 = None
            dve.waits([S_acc])
            for b in range(NB):
                s = b % 2
                n = P if b < NB - 1 else NLAST
                ot = kv[:, 4 + s, 0:D]
                oT = kv[:, 6 + s, 0:D]
                xt = kv[:, 8 + s, 0:D]
                l = sl["x"][s].dma(sp, lambda e, b=b, xt=xt: e.dma_start(xt, x1t[b * P:(b + 1) * P, :]), xf[s])
                a = dve.op(lambda e, b=b, s=s: e.tensor_scalar(rs[:, s, :], acc[:, b, :, 32], 1e-30, None, ALU.max))
                a = dve.op(lambda e, s=s: e.reciprocal(rs[:, s, :], rs[:, s, :]), a)
                a = dve.op(lambda e, b=b, s=s, ot=ot: e.tensor_tensor(
                    ot.rearrange("p (h d) -> p h d", h=NH), acc[:, b, :, 0:32],
                    rs[:, s, :].rearrange("p (h a) -> p h a", a=1).to_broadcast([P, NH, 32]), ALU.mult),
                    a, ofr[s], *kvfree)
                for f in range(2):
                    t = pe.op(lambda e, f=f, ot=ot, s=s: e.transpose(psum[1][:, f * P:(f + 1) * P],
                                                                     ot[:, f * P:(f + 1) * P], ident[:, :]),
                              a, p1)
                ofr[s] = t
                p1 = act.op(lambda e, oT=oT: e.copy(oT, psum[1][:, 0:D]), t, *kvfree)
                for f in range(2):
                    m = pe.op(lambda e, f=f, oT=oT: e.matmul(psum[2][:, 0:D], lhsT=oT[:, f * P:(f + 1) * P],
                                                             rhs=wot[:, f, :], start=(f == 0), stop=(f == 1)),
                              p1, t_wo, p2, *qefree)
                a = dve.op(lambda e, xt=xt: e.tensor_tensor(xt, xt, bias, ALU.add), l, bt)
                a = p2 = dve.op(lambda e, xt=xt: e.tensor_tensor(xt, xt, psum[2][:, 0:D], ALU.add), a, m)
                xf[s] = sl["o"][s].dma(sp, lambda e, b=b, n=n, xt=xt: e.dma_start(out[b * P:b * P + n, :],
                                                                                  xt[0:n, :]), a)
            sp.waits(xf)

        phase("l1", l1, {"gen": 1, "fg": 2, "kv": 20, "q": 4, "w": 2, "x": 2, "o": 2})


_INS = ["x", "src", "dst", "edge_weight", "L0_gnn_weight", "L1_gnn_Wq", "L1_gnn_bq", "L1_gnn_Wk", "L1_gnn_bk",
        "L1_gnn_Wv", "L1_gnn_bv", "L1_gnn_Wo", "L1_gnn_bo"]


def kernel(**inputs):
    import numpy as _np
    import concourse.bacc as _bacc
    from concourse import mybir as _mybir
    from concourse.bass_utils import run_bass_kernel_spmd as _run

    nc = _bacc.Bacc("TRN2", target_bir_lowering=False, num_devices=1)
    arrays, args = {}, []
    for name in _INS:
        a = _np.ascontiguousarray(inputs[name])
        arrays[f"in_{name}"] = a
        args.append(nc.dram_tensor(f"in_{name}", a.shape, _mybir.dt.from_np(a.dtype), kind="ExternalInput").ap())
    out = nc.dram_tensor("out_0", (N, D), F32, kind="ExternalOutput").ap()
    build(nc, *args, out)
    r = _run(nc, [arrays], core_ids=[0])
    return r.results[0]["out_0"]
```

```python
from contextlib import ExitStack

import numpy as np

import concourse.bass as bass
from concourse import mybir

P = 128
N = 12500
E = 200000
D = 256
NH = 8
NB = 98
NLAST = N - (NB - 1) * P
T = 1563
J = T + NB - 1
JP = 13 * P
W = 8
NW = -(-J // W)
NQ2 = J // 2
PERIOD = ("prod0 u0 x u1 red0 a0 x e0 p2 a1 v3 a2 prod1 u2 e1 a3 x red1 x oh u3 x k0 prod2 x a4 "
          "x e2 red2 x a5 prod3 x new of a6 red3 x e3 k4 a7 p0 v1 R").split()
KVW = 256 + NH * 33
ROW = 257
BIG = 1.0e30
SCALE = float(np.float32(1.0) / np.sqrt(np.float32(32.0)))

F32 = mybir.dt.float32
I32 = mybir.dt.int32
U8 = mybir.dt.uint8
BF16 = mybir.dt.bfloat16
ALU = mybir.AluOpType
ACT = mybir.ActivationFunctionType
AX = mybir.AxisListType


class Engine:

    def __init__(self, sem):
        self.sem = sem
        self.count = 0
        self.todo = []
        self.seen = {}

    def waits(self, tokens):
        for t in tokens:
            if t is None:
                continue
            sem, value = t
            if self.seen.get(id(sem), 0) < value:
                self.seen[id(sem)] = value
                self.todo.append(lambda e, sem=sem, value=value: e.wait_ge(sem, value))

    def op(self, fn, *tokens):
        self.waits(tokens)
        self.count += 1
        sem = self.sem
        self.todo.append(lambda e: fn(e).then_inc(sem, 1))
        return (sem, self.count)

    def do(self, fn, *tokens):
        self.waits(tokens)
        self.todo.append(fn)


class Slot:

    def __init__(self, sem):
        self.sem = sem
        self.count = 0

    def dma(self, eng, fn, *tokens):
        eng.waits(tokens)
        self.count += 16
        sem = self.sem
        eng.todo.append(lambda e: fn(e).then_inc(sem, 16))
        return (sem, self.count)

    @property
    def token(self):
        return (self.sem, self.count)


def build(nc, x, src, dst, edge_weight, weight, Wq, bq, Wk, bk, Wv, bv, Wo, bo, out):
    def dram(name, shape, dt=F32):
        return nc.dram_tensor(name, shape, dt, kind="Internal").ap()

    fields = dram("fields", (JP, 5 * P))
    starts = dram("starts", (JP, P))
    dvec = dram("dvec", (8, JP))
    ivec = dram("ivec", (8, JP), I32)
    bvec = dram("bvec", (1, P))
    msgs = dram("msgs", (T * P, ROW))
    srcs = dram("srcs", (E,), I32)
    dsts = dram("dsts", (E,), I32)
    ws = dram("ws", (E,))
    recs = [dram(f"recs{k}", (T * P, 4)) for k in range(2)]
    kvt = dram("kvt", (NB * P, KVW))
    qt = dram("qt", (NB * P, D))
    x1t = dram("x1t", (NB * P, D))

    with ExitStack() as top:
        top.enter_context(nc.allow_non_contiguous_dma(reason="vectors of one element per partition"))

        def mksem(name):
            return top.enter_context(nc.semaphore(name))

        def sb(stack, name, shape, dt=F32):
            return stack.enter_context(nc.sbuf_tensor(name, shape, dt))

        psum = [top.enter_context(nc.psum_tensor(f"ps{i}", [P, 512], F32)) for i in range(8)]
        iota = sb(top, "iota", [P, P])
        ident = sb(top, "ident", [P, P])
        tri = sb(top, "tri", [P, P])
        trib = sb(top, "trib", [P, P], BF16)
        onesb = sb(top, "onesb", [P, 2], BF16)
        iotab = sb(top, "iotab", [P, P], BF16)
        identb = sb(top, "identb", [P, P], BF16)
        unsorted = sb(top, "unsorted", [1, 1], I32)

        always, unless_sorted = ([], []), ([], [])
        by_pool = ("fg", "cg", "kv", "ms", "sc")

        def phase(name, program, slots, kept=always):
            with ExitStack() as stack:
                eng = {k: Engine(mksem(f"{name}_{k}")) for k in ("pe", "dve", "act", "pool", "sp")}
                slot = {}
                used = [0, 0]
                for k, n in slots.items():
                    q = k in by_pool
                    while len(kept[q]) < used[q] + n:
                        kept[q].append(Slot(mksem(f"{name}_dma{int(q)}_{len(kept[q])}")))
                    slot[k] = kept[q][used[q]:used[q] + n]
                    used[q] += n
                program(stack, eng, slot)
                block = stack.enter_context(nc.Block())
                for key, deco in (("pe", block.tensor), ("dve", block.vector), ("act", block.scalar),
                                  ("pool", block.gpsimd), ("sp", block.sync)):
                    def run(e, todo=eng[key].todo):
                        for fn in todo:
                            fn(e)
                    deco(run)

        def four(kept, e, name):
            if "regs" not in kept:
                kept["regs"] = [e.alloc_register(f"{name}{i}") for i in range(4)]
            return kept["regs"]

        def bcast(ap, n):
            return ap.rearrange("p (a b) -> p a b", a=1).to_broadcast([P, n, ap.shape[-1]])

        def rows_of(ap, n=P):
            return ap.rearrange("p (j a) -> p j a", a=1).to_broadcast([P, ap.shape[-1], n])

        def pipeline(stages, n):
            for t in range(n + len(stages) - 1):
                for k in reversed(range(len(stages))):
                    if 0 <= t - k < n:
                        stages[k](t - k)

        def histogram(stack, en, keyT, ready, name, more=None):
            pe, dve = en["pe"], en["dve"]
            hot = sb(stack, f"hot{name}", [P, 3, W, P], BF16)
            C = sb(stack, f"C{name}", [P, JP])
            Cs = sb(stack, f"Cs{name}", [P, T])
            base = sb(stack, f"base{name}", [P, 1])
            free = [None] * 3
            t_one = dve.op(lambda e: e.memset(C[:, :], 1.0))
            hist = None
            for k, t0 in enumerate(range(0, T, W)):
                n = min(W, T - t0)
                o = dve.op(lambda e, k=k, t0=t0, n=n: e.tensor_tensor(
                    hot[:, k % 3, 0:n, :], bcast(iotab[:, :], n), rows_of(keyT[:, t0:t0 + n]), ALU.is_equal),
                    free[k % 3], *ready)
                for t in range(t0, t0 + n):
                    hist = free[k % 3] = pe.op(
                        lambda e, t=t, k=k, t0=t0: e.matmul(
                            psum[2 + t // 512][:, t % 512:t % 512 + 1], lhsT=hot[:, k % 3, t - t0, :],
                            rhs=onesb[:, 0:1], start=True, stop=True), o)
            if more:
                more()
            scan = None
            for k in range(4):
                n = min(512, T - 512 * k)
                first = scan is None
                scan = dve.op(lambda e, k=k, n=n, first=first: e.tensor_tensor_scan(
                    Cs[:, 512 * k:512 * k + n], C[:, 512 * k:512 * k + n], psum[2 + k][:, 0:n],
                    0.0 if first else Cs[:, 512 * k - 1:512 * k], ALU.mult, ALU.add), hist, t_one, scan)
            a = pe.op(lambda e: e.matmul(psum[6][:, 0:1], lhsT=tri[:, :], rhs=Cs[:, T - 1:T], start=True, stop=True),
                      scan)
            t_base = dve.op(lambda e: e.tensor_copy(base[:, :], psum[6][:, 0:1]), a)
            for k in range(4):
                n = min(512, T - 512 * k)
                a = dve.op(lambda e, k=k, n=n: e.tensor_tensor(
                    C[:, 512 * k:512 * k + n], Cs[:, 512 * k:512 * k + n], psum[2 + k][:, 0:n], ALU.subtract), scan)
            t_C = dve.op(lambda e: e.tensor_scalar(C[:, :], C[:, :], base[:, 0:1], None, ALU.add), a, t_base)
            return C, base, t_base, t_C

        def rank(en, hot, C, t, bank, *tokens):
            pe = en["pe"]
            pe.op(lambda e: e.matmul(psum[bank][:, 0:P], lhsT=trib[:, :], rhs=hot, start=True, stop=False), *tokens)
            return pe.op(lambda e: e.matmul(psum[bank][:, 0:P], lhsT=C[:, t:t + 1].to_broadcast([P, P]),
                                            rhs=ident[:, :], start=False, stop=True))

        def ranks(stack, en, keyT, ready, name):
            dve = en["dve"]
            C, _, _, t_C = histogram(stack, en, keyT, ready, name)
            hot = sb(stack, f"hot1{name}", [P, 4, P], BF16)
            keyf = sb(stack, f"keyf{name}", [P, T])
            scr = sb(stack, f"scr{name}", [P, 2, P])
            pos = sb(stack, f"pos{name}", [P, T])
            kf = dve.op(lambda e: e.tensor_copy(keyf[:, :], keyT[:, 0:T]), *ready)
            free = [None] * 4
            bank = [None] * 2
            r = None

            def one(t):
                o = dve.op(lambda e: e.tensor_scalar(hot[:, t % 4, :], iota[:, :], keyf[:, t:t + 1], None,
                                                     ALU.is_equal), free[t % 4], kf)
                held[t] = rank(en, hot[:, t % 4, :], C, t, t % 2, o, bank[t % 2], t_C)

            def two(t):
                nonlocal r
                r = bank[t % 2] = free[t % 4] = dve.op(lambda e: e.tensor_tensor_reduce(
                    scr[:, t % 2, :], hot[:, t % 4, :], psum[t % 2][:, 0:P], 1.0, 0.0, ALU.mult, ALU.add,
                    pos[:, t:t + 1]), held.pop(t))
            held = {}
            pipeline([one, two], T)
            return pos, r

        def pairs(stack, en, slot, k, cv, ready):
            dve, pool, sp = en["dve"], en["pool"], en["sp"]
            ji = sb(stack, f"ji{k}", [P, 13], I32)
            jcol = sb(stack, f"jcol{k}", [P, 13])
            cbc = sb(stack, f"cbc{k}", [P, JP])
            junk = sb(stack, f"junk{k}", [P, T], BF16)
            cnt = sb(stack, f"cnt{k}", [P, 13])
            tj = sb(stack, f"tj{k}", [P, 2, 13])
            tji = sb(stack, f"tji{k}", [P, 2, 13], I32)
            a = pool.op(lambda e: e.iota(ji[:, :], pattern=[[P, 13]], base=0, channel_multiplier=1))
            t_j = dve.op(lambda e: e.tensor_copy(jcol[:, :], ji[:, :]), a)
            a = dve.op(lambda e: e.tensor_tensor(cv, cv, jcol[:, :], ALU.add), t_j, *ready)
            d = slot.dma(sp, lambda e: e.dma_start(dvec[k:k + 1, :].rearrange("a (c p) -> p (a c)", p=P), cv), a,
                         slot.token)
            d = slot.dma(sp, lambda e: e.dma_start(cbc[:, :], dvec[k:k + 1, :].to_broadcast([P, JP])), d)

            def rest():
                tok = None
                for c in range(13):
                    tok = dve.op(lambda e, c=c: e.tensor_scalar(junk[:, :], cbc[:, 0:T], jcol[:, c:c + 1], 0.0,
                                                                ALU.is_le, ALU.add, accum_out=cnt[:, c:c + 1]),
                                 d, tok)
                tok = dve.op(lambda e: e.tensor_scalar(tj[:, 0, :], cnt[:, :], -1.0, 0.0, ALU.add, ALU.max), tok)
                tok = dve.op(lambda e: e.tensor_tensor(tj[:, 1, :], jcol[:, :], tj[:, 0, :], ALU.subtract), tok)
                tok = dve.op(lambda e: e.tensor_copy(tji[:, :, :], tj[:, :, :]), tok)
                dt = d
                for i in range(2):
                    dt = slot.dma(sp, lambda e, i=i: e.dma_start(
                        dvec[2 + 2 * k + i:3 + 2 * k + i, :].rearrange("a (c p) -> p (a c)", p=P), tj[:, i, :]),
                        tok, dt)
                    dt = slot.dma(sp, lambda e, i=i: e.dma_start(
                        ivec[2 * k + i:1 + 2 * k + i, :].rearrange("a (c p) -> p (a c)", p=P), tji[:, i, :]),
                        tok, dt)
                return dt
            return rest

        def start(stack, en, sl):
            pe, dve, act, pool, sp = (en[k] for k in ("pe", "dve", "act", "pool", "sp"))
            inti = sb(stack, "inti", [P, P], I32)
            da = sb(stack, "da", [125, 1600], I32)
            db = sb(stack, "db", [125, 1600], I32)
            df = sb(stack, "df", [125, 1600])
            ds = sb(stack, "ds", [P, 1])
            a = pool.op(lambda e: e.iota(inti[:, :], pattern=[[1, P]], base=0, channel_multiplier=0))
            t_iota = dve.op(lambda e: e.tensor_copy(iota[:, :], inti[:, :]), a)
            a = pool.op(lambda e: e.iota(inti[:, :], pattern=[[1, P]], base=0, channel_multiplier=-1), t_iota)
            t1 = dve.op(lambda e: e.tensor_scalar(ident[:, :], inti[:, :], 0.0, None, ALU.is_equal), a)
            t2 = dve.op(lambda e: e.tensor_scalar(tri[:, :], inti[:, :], 0.0, None, ALU.is_gt), a)
            t_tri = dve.op(lambda e: e.tensor_copy(trib[:, :], tri[:, :]), t2)
            t_onesb = dve.op(lambda e: e.memset(onesb[:, :], 1.0))

            dve.op(lambda e: e.tensor_copy(iotab[:, :], iota[:, :]), t_iota)
            dve.op(lambda e: e.tensor_copy(identb[:, :], ident[:, :]), t1)
            for i, (to, vec) in enumerate(((srcs, src), (dsts, dst), (ws, edge_weight))):
                sl["cp"][i].dma(sp, lambda e, to=to, vec=vec: e.dma_start(
                    to.rearrange("(p e) -> p e", e=3125), vec.rearrange("(p e) -> p e", e=3125)))
            z = dve.op(lambda e: e.memset(db[:, :], 1 << 20))
            z2 = dve.op(lambda e: e.memset(ds[:, :], 0.0))
            la = sl["ld"][0].dma(sp, lambda e: e.dma_start(da[:, :], dst.rearrange("(p e) -> p e", e=1600)))
            lb = sl["ld"][1].dma(sp, lambda e: e.dma_start(db[0:124, :],
                                                           dst[1:1 + 124 * 1600].rearrange("(p e) -> p e", e=1600)), z)
            lc = sl["ld"][2].dma(sp, lambda e: e.dma_start(db[124:125, 0:1599],
                                                           dst[1 + 124 * 1600:E].rearrange("(p e) -> p e", e=1599)))
            a = dve.op(lambda e: e.tensor_tensor(df[:, :], da[:, :], db[:, :], ALU.is_gt), la, lb, lc)
            a = dve.op(lambda e: e.tensor_reduce(ds[0:125, :], df[:, :], AX.X, ALU.add), a, z2)
            onef = sb(stack, "onef", [P, 1])
            o = dve.op(lambda e: e.memset(onef[:, :], 1.0))
            a = pe.op(lambda e: e.matmul(psum[0][0:1, 0:1], lhsT=ds[:, :], rhs=onef[:, :], start=True, stop=True), a, o)
            dve.op(lambda e: e.tensor_copy(unsorted[:, :], psum[0][0:1, 0:1]), a)
            sp.waits([c.token for c in sl["cp"]])

        phase("start", start, {"cp": 3, "ld": 3})

        def sort_pass(k):
            def program(stack, en, sl):
                pe, dve, act, pool, sp = (en[x] for x in ("pe", "dve", "act", "pool", "sp"))
                (ld,) = sl["ld"]
                rec = sb(stack, f"rec{k}", [P, T, 4])
                ri = sb(stack, f"ri{k}", [P, 2, T], I32)
                keyT = sb(stack, f"keyT{k}", [P, T], BF16)
                posI = sb(stack, f"posI{k}", [P, T], I32)
                z = dve.op(lambda e: e.memset(ri[:, :, :], 16383))
                z1 = dve.op(lambda e: e.memset(rec[:, :, :], 0.0))
                full = (T - 1) * P
                if k == 0:
                    for i, vec in enumerate((srcs, dsts)):
                        l = ld.dma(sp, lambda e, i=i, vec=vec: e.dma_start(
                            ri[:, i, 0:T - 1], vec[0:full].rearrange("(t p) -> p t", p=P)), z, ld.token)
                        l = ld.dma(sp, lambda e, i=i, vec=vec: e.dma_start(
                            ri[0:64, i, T - 1:T], vec[full:E].rearrange("(t p) -> p t", p=64)), l)
                    l = ld.dma(sp, lambda e: e.dma_start(
                        rec[:, 0:T - 1, 2], ws[0:full].rearrange("(t p) -> p t", p=P)), z1, l)
                    l = ld.dma(sp, lambda e: e.dma_start(
                        rec[0:64, T - 1, 2:3], ws[full:E].rearrange("(t p) -> p t", p=64)), l)
                    for i in range(2):
                        l = dve.op(lambda e, i=i: e.tensor_copy(rec[:, :, i], ri[:, i, :]), ld.token)
                else:
                    l = ld.dma(sp, lambda e: e.dma_start(rec[:, :, :], recs[0].rearrange("(t p) f -> p t f", p=P)),
                               z1)
                    l = dve.op(lambda e: e.tensor_copy(ri[:, 1, :], rec[:, :, 1]), l, z)
                if k == 0:
                    a = dve.op(lambda e: e.tensor_scalar(ri[:, 0, :], ri[:, 1, :], 127, None, ALU.bitwise_and), l)
                else:
                    a = dve.op(lambda e: e.tensor_scalar(ri[:, 0, :], ri[:, 1, :], 7, None,
                                                         ALU.logical_shift_right), l)
                a = dve.op(lambda e: e.tensor_copy(keyT[:, 0:T], ri[:, 0, :]), a)
                pos, r = ranks(stack, en, keyT, [a], f"s{k}")
                a = dve.op(lambda e: e.tensor_copy(posI[:, :], pos[:, 0:T]), r)
                for t in range(T):
                    s = sl["sc"][t % 8]
                    s.dma(pool, lambda e, t=t: e.indirect_dma_start(
                        recs[k], bass.IndirectOffsetOnAxis(ap=posI[:, t:t + 1], axis=0), rec[:, t, :], None),
                        a, s.token)
                done = [s.token for s in sl["sc"]]
                if k == 1:
                    l = ld.dma(sp, lambda e: e.dma_start(rec[:, :, :], recs[1].rearrange("(t p) f -> p t f", p=P)),
                               *done)
                    for i in range(2):
                        a = dve.op(lambda e, i=i: e.tensor_copy(ri[:, i, :], rec[:, :, i]), l)
                    dve_done = a
                    for i, (vec, t) in enumerate(((srcs, ri[:, 0, :]), (dsts, ri[:, 1, :]), (ws, rec[:, :, 2]))):
                        l = ld.dma(sp, lambda e, vec=vec, t=t: e.dma_start(
                            vec[0:full].rearrange("(t p) -> p t", p=P), t[:, 0:T - 1]), dve_done, l)
                        l = ld.dma(sp, lambda e, vec=vec, t=t: e.dma_start(
                            vec[full:E].rearrange("(t p) -> p t", p=64), t[0:64, T - 1:T]), l)
                    done.append(l)
                sp.waits(done)
            return program

        with nc.If(nc.values_load(unsorted[0:1, 0:1], min_val=0, max_val=E) > 0):
            phase("sort0", sort_pass(0), {"ld": 1, "sc": 8}, unless_sorted)
            phase("sort1", sort_pass(1), {"ld": 1, "sc": 8}, unless_sorted)

        def prep(stack, en, sl):
            pe, dve, act, pool, sp = (en[k] for k in ("pe", "dve", "act", "pool", "sp"))
            (gen,), (gen2,) = sl["gen"], sl["gen2"]
            (ld0,), (ld1,), (ld2,) = sl["ld0"], sl["ld1"], sl["ld2"]
            sbT = sb(stack, "sbT", [P, T], BF16)
            cvec = sb(stack, "cvec", [P, 13])
            epst = sb(stack, "epst", [P, 1])
            stt = sb(stack, "stt", [P, 4, 6])
            mv = sb(stack, "mv", [P, NB, 2])
            sc = sb(stack, "sc", [P, 3, NB])
            first = stack.enter_context(ExitStack())
            ints = sb(first, "ints", [P, 2, 13, P], I32)
            blk = sb(first, "blk", [P, 13, P], I32)
            fr = sb(first, "fr", [P, 13, 5, P])
            sblkf = sb(first, "sblkf", [P, 13, P])
            cblk = sb(first, "cblk", [P, 13])

            m0 = dve.op(lambda e: e.memset(ints[:, :, :, :], 16383))
            m1 = dve.op(lambda e: e.memset(fr[:, 12, 2, :], 0.0))
            mh = dve.op(lambda e: e.memset(h[:, NB - 1, :], 0.0))
            t_eps = dve.op(lambda e: e.memset(epst[:, :], 1e-5))
            full = 12 * P * P
            rest = full + 26 * P

            def load_rows(slot, dst_ap, vec, *tok):
                slot.dma(sp, lambda e: e.dma_start(dst_ap(slice(0, P), slice(0, 12), P),
                                                   vec[0:full].rearrange("(c p e) -> p c e", p=P, e=P)), *tok)
                slot.dma(sp, lambda e: e.dma_start(dst_ap(slice(0, 26), 12, P),
                                                   vec[full:rest].rearrange("(p e) -> p e", e=P)))
                slot.dma(sp, lambda e: e.dma_start(dst_ap(slice(26, 27), 12, 64),
                                                   vec[rest:E].rearrange("(p e) -> p e", e=64)))
            load_rows(ld0, lambda p, c, n: ints[p, 0, c, 0:n], srcs, m0)
            load_rows(ld1, lambda p, c, n: ints[p, 1, c, 0:n], dsts, m0)
            load_rows(ld2, lambda p, c, n: fr[p, c, 2, 0:n], ws, m1)
            xl = []
            for i, (b0, b1) in enumerate(((0, 25), (25, 50), (50, 75), (75, NB - 1))):
                xl += [sl["x"][i].dma(act, lambda e, b0=b0, b1=b1: e.dma_start(
                    h[:, b0:b1, :], x[b0 * P:b1 * P, :].rearrange("(b p) d -> p b d", p=P)))] * (b1 - b0)
            xl.append(sl["x"][4].dma(act, lambda e: e.dma_start(h[0:NLAST, NB - 1, :], x[(NB - 1) * P:N, :]), mh))

            a = dve.op(lambda e: e.tensor_scalar(blk[:, :, :], ints[:, 0, :, :], 7, None, ALU.logical_shift_right),
                       ld0.token)
            t_sblk = dve.op(lambda e: e.tensor_copy(sblkf[:, :, :], blk[:, :, :]), a)
            f_src = dve.op(lambda e: e.tensor_copy(fr[:, :, 0, :], ints[:, 0, :, :]))
            f_dst = dve.op(lambda e: e.tensor_copy(fr[:, :, 1, :], ints[:, 1, :, :]), ld1.token)
            a = dve.op(lambda e: e.tensor_scalar(blk[:, :, 0], ints[:, 1, :, 0], 7, None, ALU.logical_shift_right),
                       t_sblk)
            a = dve.op(lambda e: e.tensor_copy(cvec[:, :], blk[:, :, 0]), a)
            finish_pairs = pairs(first, en, gen, 0, cvec[:, :], [a])
            k1 = dve.op(lambda e: e.memset(fr[:, :, 3, 0:1], 1.0))
            k2 = dve.op(lambda e: e.memset(fr[:, :, 4, P - 1:P], 1.0))
            k3 = dve.op(lambda e: e.tensor_tensor(fr[:, :, 3, 1:P], fr[:, :, 1, 1:P], fr[:, :, 1, 0:P - 1],
                                                  ALU.not_equal), f_dst)
            k4 = dve.op(lambda e: e.tensor_copy(fr[:, :, 4, 0:P - 1], fr[:, :, 3, 1:P]), k3)
            t_fields = gen2.dma(sp, lambda e: e.dma_start(
                fields.rearrange("(c p) f -> p c f", p=P), fr[:, :, :, :].rearrange("p c a b -> p c (a b)")),
                k1, k2, k4, f_src, ld2.token)

            prev = [None, None]
            for c in range(13):
                b = psum[c % 2]
                a = pe.op(lambda e, c=c, b=b: e.transpose(b[:, 0:P], sblkf[:, c, :], ident[:, :]),
                          t_sblk, prev[c % 2])
                n = min(P, T - c * P)
                prev[c % 2] = act.op(lambda e, c=c, b=b, n=n: e.copy(sbT[:, c * P:c * P + n], b[:, 0:n]), a)

            dt = finish_pairs()
            for q in (pe, dve, act, pool, sp):
                q.waits([dt, t_fields, prev[0], prev[1]])
            first.close()
            crow = sb(stack, "crow", [P, 13, P])

            def stats():
                free = [None] * 4
                last = None
                for b in range(NB):
                    a = dve.op(lambda e, b=b: e.bn_stats(stt[:, b % 4, :], h[:, b, :]), xl[b], free[b % 4])
                    last = free[b % 4] = dve.op(lambda e, b=b: e.bn_aggr(mv[:, b, :], stt[:, b % 4, :]), a)
                norm_all(dve, act, mv, sc, epst, last, t_eps)
                for b in range(NB):
                    act.op(lambda e, b=b: e.activation(h[:, b, :], h[:, b, :], ACT.Relu, bias=sc[:, 2, b:b + 1],
                                                       scale=sc[:, 1, b:b + 1]), (dve.sem, dve.count))

            C, base, t_base, t_C = histogram(stack, en, sbT, [prev[0], prev[1]], "a", stats)
            gen.dma(sp, lambda e: e.dma_start(bvec.rearrange("a b -> b a"), base[:, :]), t_base, dt)
            z = dve.op(lambda e: e.memset(C[:, T:JP], 0.0), t_C)
            prev = [None] * 2
            for c in range(13):
                b = psum[c % 2]
                a = pe.op(lambda e, c=c, b=b: e.transpose(b[:, 0:P], C[:, c * P:(c + 1) * P], ident[:, :]),
                          z, prev[c % 2])
                prev[c % 2] = dve.op(lambda e, c=c, b=b: e.tensor_copy(crow[:, c, :], b[:, 0:P]), a)
            dt = gen2.dma(sp, lambda e: e.dma_start(starts.rearrange("(c p) e -> p c e", p=P), crow[:, :, :]),
                          prev[0], prev[1], t_fields)
            sp.waits([dt, gen.token])

        def norm_all(dve, act, mv, sc, epst, *tok):
            a = act.op(lambda e: e.activation(sc[:, 0, :], mv[:, :, 1], ACT.Sqrt, bias=epst[:, :], scale=1.0), *tok)
            a = dve.op(lambda e: e.reciprocal(sc[:, 1, :], sc[:, 0, :]), a)
            return dve.op(lambda e: e.scalar_tensor_tensor(out=sc[:, 2, :], in0=mv[:, :, 0], scalar=-1.0,
                                                           in1=sc[:, 1, :], op0=ALU.mult, op1=ALU.mult), a)

        hstack = top.enter_context(ExitStack())
        h = sb(hstack, "h", [P, NB, D])
        phase("prep", prep, {"gen": 1, "gen2": 1, "ld0": 1, "ld1": 1, "ld2": 1, "x": 5})

        def l0a(stack, en, sl):
            pe, dve, act, pool, sp = (en[k] for k in ("pe", "dve", "act", "pool", "sp"))
            (gen,), (gen2,) = sl["gen"], sl["gen2"]
            NM = 3 * W
            NT = 20
            brow = sb(stack, "brow", [1, JP], I32)
            dloc = sb(stack, "dloc", [P, JP], BF16)
            sdig = sb(stack, "sdig", [P, JP], BF16)
            wT = sb(stack, "wT", [P, JP])
            sT = sb(stack, "sT", [P, JP])
            msk = sb(stack, "msk", [P, JP])
            Cp = sb(stack, "Cp", [P, JP])
            with ExitStack() as pre:
                tidx = sb(pre, "tidx", [P, 13], I32)
                bbc = sb(pre, "bbc", [P, JP])
                dl = sb(pre, "dl0", [P, JP])
                si = sb(pre, "si", [P, JP], I32)
                fg = sb(pre, "fg", [P, 2, 5 * P])
                cg = sb(pre, "cg", [P, 2, P])
                g = gen.dma(sp, lambda e: e.dma_start(tidx[:, :], ivec[0:1, :].rearrange("a (c p) -> p (a c)", p=P)))
                g = gen.dma(sp, lambda e: e.dma_start(brow[:, :], ivec[1:2, :]))
                g = gen.dma(sp, lambda e: e.dma_start(bbc[:, :], dvec[3:4, :].to_broadcast([P, JP])))
                fgfree = [None] * 2
                psfree = [None] * 4
                for c in range(13):
                    s = c % 2
                    lf = sl["fg"][s].dma(pool, lambda e, c=c, s=s: e.indirect_dma_start(
                        fg[:, s, :], None, fields, bass.IndirectOffsetOnAxis(ap=tidx[:, c:c + 1], axis=0)),
                        g, fgfree[s])
                    lc = sl["cg"][s].dma(pool, lambda e, c=c, s=s: e.indirect_dma_start(
                        cg[:, s, :], None, starts, bass.IndirectOffsetOnAxis(ap=tidx[:, c:c + 1], axis=0)))
                    for i, (dstt, view) in enumerate(((dl, fg[:, s, P:2 * P]), (wT, fg[:, s, 2 * P:3 * P]),
                                                      (sT, fg[:, s, 0:P]), (Cp, cg[:, s, :]))):
                        a = pe.op(lambda e, i=i, view=view: e.transpose(psum[i][:, 0:P], view, ident[:, :]),
                                  lf, lc, psfree[i])
                        if i % 2:
                            psfree[i] = act.op(lambda e, i=i, c=c, dstt=dstt: e.copy(
                                dstt[:, c * P:(c + 1) * P], psum[i][:, 0:P]), a)
                        else:
                            psfree[i] = dve.op(lambda e, i=i, c=c, dstt=dstt: e.tensor_copy(
                                dstt[:, c * P:(c + 1) * P], psum[i][:, 0:P]), a)
                    fgfree[s] = a
                a = dve.op(lambda e: e.scalar_tensor_tensor(out=dl[:, :], in0=bbc[:, :], scalar=-float(P),
                                                            in1=dl[:, :], op0=ALU.mult, op1=ALU.add), *psfree, g)
                b0 = dve.op(lambda e: e.tensor_copy(dloc[:, :], dl[:, :]), a)
                b1 = dve.op(lambda e: e.tensor_scalar(msk[:, :], dl[:, :], 0.0, 1.0e6, ALU.is_lt, ALU.mult), a)
                b2 = dve.op(lambda e: e.tensor_scalar(dl[:, :], dl[:, :], 127.0, 1.0e6, ALU.is_gt, ALU.mult), a, b0, b1)
                b3 = dve.op(lambda e: e.tensor_tensor(msk[:, :], msk[:, :], dl[:, :], ALU.add), b1, b2)
                b4 = dve.op(lambda e: e.tensor_copy(si[:, :], sT[:, :]), psfree[2])
                b4 = dve.op(lambda e: e.tensor_scalar(si[:, :], si[:, :], 7, None, ALU.logical_shift_right), b4)
                b5 = dve.op(lambda e: e.tensor_copy(sdig[:, :], si[:, :]), b4)
            for q in (pe, dve, act, pool, sp):
                q.waits([b3, b5, *psfree, *fgfree, g])
            Ob = sb(stack, "Ob0", [P, 2, W, P], BF16)
            Os = sb(stack, "Os0", [P, 2, W, P], BF16)
            OT = sb(stack, "OT0", [P, NT, P])
            mt = sb(stack, "mtw", [P, NM, ROW])
            scr = sb(stack, "scr0", [P, 2, P])
            pos = sb(stack, "pos0", [P, 2, W])
            posI = sb(stack, "posIw", [P, 3, W], I32)
            zrow = sb(stack, "zrow", [64, ROW])
            basebc = sb(stack, "basebc", [P, P])
            cv = sb(stack, "cv", [P, 13])
            cr = sb(stack, "cr", [P, 13])
            cri = sb(stack, "cri", [P, 13], I32)

            z = dve.op(lambda e: e.memset(zrow[:, :], 0.0))
            z = dve.op(lambda e: e.memset(zrow[:, D:D + 1], 16383.0), z)
            t_z = gen2.dma(sp, lambda e: e.dma_start(msgs[E:T * P, :], zrow[:, :]), z)

            tb = gen.dma(sp, lambda e: e.dma_start(basebc[:, :], bvec.to_broadcast([P, P])), g)
            a = pool.op(lambda e: e.iota(cri[:, :], pattern=[[P * P, 13]], base=0, channel_multiplier=P))
            a = dve.op(lambda e: e.tensor_copy(cr[:, :], cri[:, :]), a)
            last = None
            for c in range(13):
                last = dve.op(lambda e, c=c: e.tensor_scalar(scr[:, c % 2, 1:P], basebc[:, 1:P], cr[:, c:c + 1], 0.0,
                                                             ALU.is_le, ALU.add, accum_out=cv[:, c:c + 1]),
                              tb, a, last)
            finish_pairs = pairs(stack, en, gen, 1, cv[:, :], [last])

            vals = {}
            obtok, ostok, otok, hetok, hedone, rktok, scaled, ranked = ({} for _ in range(8))
            bank = {k: None for k in range(8)}
            mfree = [None] * NM
            pos_free = [None] * 2
            scrfree = [last, last]

            def onehots(w):
                n = min(W, J - w * W)
                j0 = w * W
                obtok[w] = dve.op(lambda e: e.tensor_tensor(
                    Ob[:, w % 2, 0:n, :], bcast(iotab[:, :], n), rows_of(dloc[:, j0:j0 + n]), ALU.is_equal),
                    otok.get((j0 - W) // 4 - 1))
                ostok[w] = dve.op(lambda e: e.tensor_tensor(
                    Os[:, w % 2, 0:n, :], bcast(iotab[:, :], n), rows_of(sdig[:, j0:j0 + n]), ALU.is_equal),
                    ranked.get(j0 - W - 1))

            def columns(j):
                if j >= J:
                    return
                psb = psum[0][:, :].bitcast(BF16)
                w = j // W
                for i in range(4):
                    t = pe.op(lambda e, i=i: e.transpose(psb[:, i * P:(i + 1) * P], Ob[:, w % 2, j % W + i, :],
                                                         identb[:, :]), obtok[w], bank[0])
                bank[0] = otok[j // 4] = act.op(lambda e: e.copy(
                    OT[:, j % NT:j % NT + 4, :], psb[:, 0:4 * P].rearrange("p (j n) -> p j n", n=P)), t,
                    hedone.get(j - NT + 3))

            def products(j):
                if j % 4 == 0:
                    m = min(4, J - j)

                    def ld(e):
                        r = four(vals, e, "l0a")
                        e.load(r[:m], brow[0:1, j:j + m])
                        vals["v"] = [e.snap(x, min_val=0, max_val=NB - 1) for x in r[:m]]
                    pe.do(ld)
                k = 1 + j % 3
                hetok[j] = hedone[j] = pe.op(lambda e: e.matmul(
                    psum[k][:, 0:D], lhsT=OT[:, j % NT, :],
                    rhs=h[:, bass.ds(vals["v"][j % 4], 1), :].rearrange("p a b -> p (a b)"), start=True, stop=True),
                    otok[j // 4], bank[k])
                k2 = 4 + j % 3
                rktok[j] = rank(en, Os[:, j // W % 2, j % W, :], Cp, j, k2, ostok[j // W], bank[k2])

            def weigh(j):
                k = 1 + j % 3
                scaled[j] = bank[k] = act.op(lambda e: e.activation(mt[:, j % NM, 0:D], psum[k][:, 0:D], ACT.Copy,
                                                                    scale=wT[:, j:j + 1]),
                                             hetok.pop(j), mfree[j % NM])
                k2 = 4 + j % 3
                r = ranked[j] = bank[k2] = scrfree[j % 2] = dve.op(lambda e: e.tensor_tensor_reduce(
                    scr[:, j % 2, :], Os[:, j // W % 2, j % W, :], psum[k2][:, 0:P], 1.0, 0.0, ALU.mult, ALU.add,
                    pos[:, j // W % 2, j % W:j % W + 1]), rktok.pop(j), pos_free[j // W % 2], scrfree[j % 2])
                if j % W == W - 1 or j == J - 1:
                    w = j // W
                    n = j % W + 1
                    j0 = w * W
                    s0 = j0 % NM
                    c = dve.op(lambda e: e.tensor_copy(mt[:, s0:s0 + n, D], sT[:, j0:j0 + n]), *mfree[s0:s0 + n])
                    a = pos_free[w % 2] = dve.op(lambda e: e.tensor_tensor(
                        posI[:, w % 3, 0:n], pos[:, w % 2, 0:n], msk[:, j0:j0 + n], ALU.add), r, *mfree[s0:s0 + n])
                    for i in range(n):
                        mfree[s0 + i] = sl["ms"][s0 + i].dma(pool, lambda e, i=i: e.indirect_dma_start(
                            msgs, bass.IndirectOffsetOnAxis(ap=posI[:, w % 3, i:i + 1], axis=0),
                            mt[:, s0 + i, :], None, bounds_check=E - 1, oob_is_err=False), scaled[j0 + i], c, a)

            onehots(0)
            columns(0)
            columns(4)

            def step(j):
                if j % W == 2 and j // W + 1 < NW:
                    onehots(j // W + 1)
                    columns(j + 6)
                if j % W == 5:
                    columns(j + 7)
                products(j)
            pipeline([step, lambda j: None, weigh], J)
            dt = finish_pairs()
            pool.waits(mfree)
            sp.waits([dt, t_z])

        phase("l0a", l0a, {"gen": 1, "gen2": 1, "fg": 2, "cg": 2, "ms": 3 * W})
        hstack.close()

        def l0b(stack, en, sl):
            pe, dve, act, pool, sp = (en[k] for k in ("pe", "dve", "act", "pool", "sp"))
            (gen,) = sl["gen"]
            acc = sb(stack, "acc0", [P, NB, D])
            az = pool.op(lambda e: e.memset(acc[:, :, :], 0.0))
            wts = sb(stack, "wts", [P, 2, D])
            wt = sb(stack, "wt", [P, 2, 3, D])
            bias = sb(stack, "bias", [P, 3, D])
            epst = sb(stack, "epst1", [P, 1])
            t_eps = dve.op(lambda e: e.memset(epst[:, :], 1e-5))
            w = sl["w"]
            t_w = w[0].dma(act, lambda e: e.dma_start(wts[:, :, :], weight.rearrange("(a p) d -> p a d", p=P)))
            for i, bb in enumerate((bq, bk, bv)):
                bt = w[1].dma(act, lambda e, i=i, bb=bb: e.dma_start(
                    bias[:, i, :], bb.rearrange("(a d) -> a d", a=1).to_broadcast([P, D])))
            part = stack.enter_context(ExitStack())
            NM = 3 * W
            wraw = sb(part, "wraw", [P, 3, 2, D])
            bbc = sb(part, "bbc1", [P, JP])
            rows = sb(part, "rows1", [1, 2, JP], I32)
            mt = sb(part, "mt1", [P, NM, ROW])
            O = sb(part, "O1", [P, 2, W, P])
            sl8 = sb(part, "sl8", [P, 2, W])
            for i, ww in enumerate((Wq, Wk, Wv)):
                lw = w[2].dma(act, lambda e, ww=ww, i=i: e.dma_start(wraw[:, i, :, :],
                                                                     ww.rearrange("(a p) d -> p a d", p=P)))
            g = gen.dma(sp, lambda e: e.dma_start(rows[:, 0, :], ivec[2:3, :]))
            g = gen.dma(sp, lambda e: e.dma_start(rows[:, 1, :], ivec[3:4, :]))
            g = gen.dma(sp, lambda e: e.dma_start(bbc[:, :], dvec[5:6, :].to_broadcast([P, JP])))
            k = dve.op(lambda e: e.tensor_scalar(bbc[:, :], bbc[:, :], float(P), None, ALU.mult), g)
            c = [None] * 2
            for i in range(3):
                for a in range(2):
                    for b in range(2):
                        q = (a + b) % 2
                        t = pe.op(lambda e, a=a, b=b, i=i, q=q: e.transpose(
                            psum[6 + q][:, 0:P], wraw[:, i, a, b * P:(b + 1) * P], ident[:, :]), lw, c[q])
                        c[q] = act.op(lambda e, a=a, b=b, i=i, q=q: e.copy(
                            wt[:, b, i, a * P:(a + 1) * P], psum[6 + q][:, 0:P]), t)
            t_wt = c

            mfree = [None] * NM
            bank = [None] * 4
            ofree = [None] * 2
            vs, vd = {}, {}
            mtok, otok, ptok = {}, {}, {}
            S = {"acc": None}
            sp.waits([g])
            dve.waits([az, k])

            def load(w):
                for j in range(w * W, min(J, (w + 1) * W)):
                    if j % 4 == 0:
                        n = min(4, J - j)

                        def lds(e, j=j, n=n):
                            r = four(vs, e, "l0s")
                            e.load(r[:n], rows[0:1, 0, j:j + n])
                            vs["v"] = [e.snap(x, min_val=0, max_val=T - 1) for x in r[:n]]
                        sp.do(lds)
                    mtok[j] = sl["m"][j % NM].dma(sp, lambda e, j=j: e.dma_start(
                        mt[:, j % NM, :], msgs[bass.ds(vs["v"][j % 4] * P, P), :]), mfree[j % NM])

            def onehots(w):
                if w >= NW:
                    return
                j0 = w * W
                n = min(W, J - j0)
                s0 = j0 % NM
                a = dve.op(lambda e: e.tensor_tensor(sl8[:, w % 2, 0:n], mt[:, s0:s0 + n, D], bbc[:, j0:j0 + n],
                                                     ALU.subtract), *[mtok[j] for j in range(j0, j0 + n)])
                otok[w] = dve.op(lambda e: e.tensor_tensor(
                    O[:, w % 2, 0:n, :], bcast(iota[:, :], n), rows_of(sl8[:, w % 2, 0:n]), ALU.is_equal),
                    a, ofree[w % 2])

            def product(j):
                w = j // W
                for f in range(2):
                    m = pe.op(lambda e, f=f: e.matmul(
                        psum[j % 4][:, f * P:(f + 1) * P], lhsT=mt[:, j % NM, f * P:(f + 1) * P],
                        rhs=O[:, w % 2, j % W, :], start=True, stop=True), mtok[j], otok[w], bank[j % 4])
                ptok[j] = mfree[j % NM] = ofree[w % 2] = m

            def add(j):
                if j % 4 == 0:
                    n = min(4, J - j)

                    def ld(e):
                        r = four(vd, e, "l0d")
                        e.load(r[:n], rows[0:1, 1, j:j + n])
                        vd["v"] = [e.snap(x, min_val=0, max_val=NB - 1) for x in r[:n]]
                    dve.do(ld)

                def fn(e):
                    t = acc[:, bass.ds(vd["v"][j % 4], 1), :].rearrange("p a b -> p (a b)")
                    return e.tensor_tensor(t, t, psum[j % 4][:, 0:D], ALU.add)
                S["acc"] = bank[j % 4] = dve.op(fn, ptok.pop(j), S["acc"])

            load(0)
            load(1)
            onehots(0)

            def step(j):
                if j % W == 0 and j // W + 2 < NW:
                    load(j // W + 2)
                if j % W == 4:
                    onehots(j // W + 1)
                product(j)
            pipeline([step, lambda j: None, add], J)
            last = S["acc"]
            for q in (pe, dve, act, pool, sp):
                q.waits([last, t_w, bt, *t_wt, *mfree])
            part.close()

            NX = 6
            xt = sb(stack, "xt1", [P, NX, D])
            stt = sb(stack, "stt1", [P, 4, 6])
            mv = sb(stack, "mv1", [P, NB, 2])
            sc = sb(stack, "sc1", [P, 3, NB])
            z = dve.op(lambda e: e.memset(xt[:, (NB - 1) % NX, :], 0.0))
            xfree = [None] * NX
            bank = [last] * 4
            sfree = [None] * 4
            l, m, a = {}, {}, {}

            def x_load(b):
                s = b % NX
                n = P if b < NB - 1 else NLAST
                zz = dve.op(lambda e: e.memset(xt[:, s, :], 0.0), xfree[s]) if b == NB - 1 else None
                l[b] = sl["x"][s].dma(sp, lambda e: e.dma_start(xt[0:n, s, :], x[b * P:b * P + n, :]), xfree[s], zz, z)

            def x_product(b):
                for f in range(2):
                    m[b] = pe.op(lambda e, f=f: e.matmul(psum[b % 4][:, 0:D], lhsT=acc[:, b, f * P:(f + 1) * P],
                                                         rhs=wts[:, f, :], start=(f == 0), stop=(f == 1)), bank[b % 4])

            def x_add(b):
                a[b] = bank[b % 4] = xfree[b % NX] = dve.op(lambda e: e.tensor_tensor(
                    acc[:, b, :], xt[:, b % NX, :], psum[b % 4][:, 0:D], ALU.add), m[b], l[b])

            def x_stats(b):
                sfree[b % 4] = dve.op(lambda e: e.bn_stats(stt[:, b % 4, :], acc[:, b, :]), a[b], sfree[b % 4])
                sl["st"][b % 4].dma(sp, lambda e: e.dma_start(x1t[b * P:(b + 1) * P, :], acc[:, b, :]), a[b],
                                    sl["st"][b % 4].token)

            def x_aggr(b):
                sfree[b % 4] = dve.op(lambda e: e.bn_aggr(mv[:, b, :], stt[:, b % 4, :]), sfree[b % 4])
            pipeline([x_load, lambda b: None, lambda b: None, x_product, x_add, x_stats, x_aggr], NB)
            nrm = norm_all(dve, act, mv, sc, epst, *sfree, t_eps)

            NY = 3
            ht = sb(stack, "ht1", [P, NY, D])
            hT = sb(stack, "hT1", [P, NY, D])
            qo = sb(stack, "qo", [P, NY, D])
            kvo = sb(stack, "kvo", [P, NY, KVW])
            t_one = dve.op(lambda e: e.memset(kvo[:, :, :], 1.0))
            hd, tr, cp, qm, km = {}, {}, {}, {}, {}
            bank = [None] * 8
            hfree = [None] * NY
            hTfree = [None] * NY
            ofree = [None] * NY

            def h_norm(b):
                s = b % NY
                hd[b] = act.op(lambda e: e.activation(ht[:, s, :], acc[:, b, :], ACT.Relu, bias=sc[:, 2, b:b + 1],
                                                      scale=sc[:, 1, b:b + 1]), nrm, hfree[s])

            def h_turn(b):
                k = b % 2
                for f in range(2):
                    tr[b] = pe.op(lambda e, f=f: e.transpose(psum[k][:, f * P:(f + 1) * P],
                                                             ht[:, b % NY, f * P:(f + 1) * P], ident[:, :]),
                                  hd[b], bank[k])
                hfree[b % NY] = tr[b]
                cp[b] = bank[k] = act.op(lambda e: e.copy(hT[:, b % NY, :], psum[k][:, 0:D]), tr[b], hTfree[b % NY])

            def h_products(b):
                k = 2 + b % 2
                for f in range(2):
                    qm[b] = pe.op(lambda e, f=f: e.matmul(psum[k][:, 0:D], lhsT=hT[:, b % NY, f * P:(f + 1) * P],
                                                          rhs=wt[:, f, 0, :], start=(f == 0), stop=(f == 1)),
                                  cp[b], bank[k])
                k2 = 4 + b % 3
                for f in range(2):
                    km[b] = pe.op(lambda e, f=f: e.matmul(
                        psum[k2][:, :], lhsT=hT[:, b % NY, f * P:(f + 1) * P],
                        rhs=wt[:, f, 1:3, :].rearrange("p a b -> p (a b)"), start=(f == 0), stop=(f == 1)), bank[k2])
                hTfree[b % NY] = km[b]

            def h_out(b):
                s = b % NY
                k, k2 = 2 + b % 2, 4 + b % 3
                a1 = bank[k] = dve.op(lambda e: e.tensor_tensor(qo[:, s, :], psum[k][:, 0:D], bias[:, 0, :], ALU.add),
                                      qm[b], ofree[s])
                dve.op(lambda e: e.tensor_tensor(kvo[:, s, 0:D], psum[k2][:, 0:D], bias[:, 1, :], ALU.add),
                       km[b], t_one)
                a3 = bank[k2] = dve.op(lambda e: e.tensor_tensor(
                    kvo[:, s, D:KVW].rearrange("p (h d) -> p h d", h=NH)[:, :, 0:32],
                    psum[k2][:, D:2 * D].rearrange("p (h d) -> p h d", h=NH),
                    bias[:, 2, :].rearrange("p (h d) -> p h d", h=NH), ALU.add))
                o = sl["qo"][s]
                o.dma(sp, lambda e: e.dma_start(qt[b * P:(b + 1) * P, :], qo[:, s, :]), a1)
                ofree[s] = o.dma(sp, lambda e: e.dma_start(kvt[b * P:(b + 1) * P, :], kvo[:, s, :]), a3)
            pipeline([h_norm, h_turn, h_products, h_out], NB)
            sp.waits(ofree + [q.token for q in sl["st"]])

        phase("l0b", l0b, {"gen": 1, "m": 3 * W, "w": 3, "x": 6, "st": 4, "qo": 3})

        def l1(stack, en, sl):
            pe, dve, act, pool, sp = (en[k] for k in ("pe", "dve", "act", "pool", "sp"))
            (gen,) = sl["gen"]
            acc = sb(stack, "acc2", [P, NB, NH, 33])
            irow = sb(stack, "irow", [P, JP], I32)
            sI = sb(stack, "sI", [P, JP], I32)
            dloc = sb(stack, "dloc2", [P, JP], BF16)
            FT = sb(stack, "FT", [P, JP], U8)
            LT = sb(stack, "LT", [P, JP], U8)
            link = sb(stack, "link", [P, JP], U8)
            NK = 22
            AHEAD = 6
            NQ = 4
            NOF = 16
            NT = 20

            az = pool.op(lambda e: e.memset(acc[:, :, :, :], 0.0))
            with ExitStack() as pre:
                tidx = sb(pre, "tidx2", [P, 13], I32)
                same = sb(pre, "same", [P, JP + 1])
                tmp = sb(pre, "tmpI", [P, JP], I32)
                dl = sb(pre, "dl", [P, JP])
                fg = sb(pre, "fg2", [P, 2, 5 * P])
                g = gen.dma(sp, lambda e: e.dma_start(tidx[:, :], ivec[0:1, :].rearrange("a (c p) -> p (a c)", p=P)))
                g = gen.dma(sp, lambda e: e.dma_start(same[:, 1:JP + 1], dvec[3:4, :].to_broadcast([P, JP])))
                fgfree = [None] * 2
                psfree = [None] * 2
                for c in range(13):
                    s = c % 2
                    lf = sl["fg"][s].dma(pool, lambda e, c=c, s=s: e.indirect_dma_start(
                        fg[:, s, :], None, fields, bass.IndirectOffsetOnAxis(ap=tidx[:, c:c + 1], axis=0)),
                        g, fgfree[s])
                    for i, (dstt, k) in enumerate(((dl, 1), (sI, 0), (FT, 3), (LT, 4))):
                        a = pe.op(lambda e, i=i, s=s, k=k: e.transpose(psum[i % 2][:, 0:P],
                                                                       fg[:, s, k * P:(k + 1) * P], ident[:, :]),
                                  lf, psfree[i % 2])
                        if k == 0:
                            psfree[i % 2] = dve.op(lambda e, i=i, c=c, dstt=dstt: e.tensor_scalar(
                                dstt[:, c * P:(c + 1) * P], psum[i % 2][:, 0:P], float(N - 1), None, ALU.min), a)
                        else:
                            psfree[i % 2] = act.op(lambda e, i=i, c=c, dstt=dstt: e.copy(
                                dstt[:, c * P:(c + 1) * P], psum[i % 2][:, 0:P]), a)
                    fgfree[s] = a
                a = dve.op(lambda e: e.scalar_tensor_tensor(
                    out=dloc[:, :], in0=same[:, 1:JP + 1], scalar=-float(P), in1=dl[:, :], op0=ALU.mult,
                    op1=ALU.add), psfree[0], psfree[1], g)
                m = dve.op(lambda e: e.memset(same[:, 0:1], -1.0), g)
                t = dve.op(lambda e: e.tensor_copy(tmp[:, :], same[:, 1:JP + 1]), g)
                r0 = dve.op(lambda e: e.tensor_copy(irow[0:1, :], tmp[0:1, :]), t)
                r1 = dve.op(lambda e: e.tensor_scalar(irow[32:33, :], tmp[32:33, :], NQ - 1, None, ALU.bitwise_and), t)
                a = dve.op(lambda e: e.tensor_tensor(dl[:, :], same[:, 1:JP + 1], same[:, 0:JP], ALU.not_equal), a, m)
                r2 = dve.op(lambda e: e.tensor_copy(irow[64:65, :], dl[64:65, :]), a)
                t1 = dve.op(lambda e: e.tensor_copy(link[:, :], dl[:, :]), a)
            for q in (pe, dve, act, pool, sp):
                q.waits([r0, r1, r2, t1, psfree[0], psfree[1], fgfree[0], fgfree[1]])
            kv = sb(stack, "kv", [P, NK, KVW], F32)
            qb = sb(stack, "qb", [P, NQ, D])
            Ob = sb(stack, "Ob", [P, 2, W, P], BF16)
            Of = sb(stack, "Of", [P, NOF, P])
            OT = sb(stack, "OT2", [P, NT, P])
            prod = sb(stack, "prod", [P, 2, 2, D])
            sims = sb(stack, "sims", [P, 2, NH, W])
            FB = sb(stack, "FB", [P, NH, W])
            FS = sb(stack, "FS", [64, P])
            PM = sb(stack, "PM", [64, P])
            PL = sb(stack, "PL", [P, W, 9])
            absent = sb(stack, "absent", [P, W])
            val = sb(stack, "val", [P, NH, W])
            D0 = sb(stack, "D0", [P, 2, NH, W])
            fw = sb(stack, "fw", [P, NH, W])
            ref = sb(stack, "ref", [P, NH, W])
            carry = sb(stack, "carry", [P, NH])
            cut = sb(stack, "cut", [P, 1])
            alpha = sb(stack, "alpha", [P, 2, NH])
            dd = sb(stack, "dd", [P, NH, W])
            pp = sb(stack, "pp", [P, 2, NH, W])
            pv = sb(stack, "pv", [P, 4, NH * 33])

            t_carry = dve.op(lambda e: e.memset(carry[:, :], -BIG))
            t_d0 = act.op(lambda e: e.activation(D0[:, :, :, :].rearrange("p a b c -> p (a b c)"), iota[:, :],
                                                 ACT.Copy, scale=0.0, bias=-BIG))
            dve.waits([az])
            kvfree = [None] * NK
            ofree = [None] * NOF
            obfree = [None] * 2
            obtok, metok = {}, {}
            prodfree = [None] * 2
            qefree = [None] * 2
            ufree = [None] * 4
            ufull = [None] * 4
            qdone = {}
            kvtok, qtok, otok, qetok, simtok, simfree, oftok = {}, {}, {}, {}, {}, {}, {}
            vs, vp, vd = {}, {}, {}
            S = {"carry": t_carry, "d0": t_d0}

            def onehots(w):
                n = min(W, J - w * W)
                j0 = w * W
                obtok[w] = dve.op(lambda e: e.tensor_tensor(
                    Ob[:, w % 2, 0:n, :], bcast(iotab[:, :], n),
                    dloc[:, j0:j0 + n].rearrange("p (j a) -> p j a", a=1).to_broadcast([P, n, P]), ALU.is_equal),
                    obfree[w % 2])

            def columns(j):
                if j >= J:
                    return
                psb = psum[0][:, :].bitcast(BF16)
                w = j // W
                for i in range(4):
                    t = pe.op(lambda e, i=i: e.transpose(psb[:, i * P:(i + 1) * P], Ob[:, w % 2, j % W + i, :],
                                                         identb[:, :]), obtok[w], S.get("otp"))
                S["otp"] = otok[j // 4] = act.op(lambda e: e.copy(
                    OT[:, j % NT:j % NT + 4, :], psb[:, 0:4 * P].rearrange("p (j n) -> p j n", n=P)), t,
                    metok.get((j - NT) // W))

            def gather(j):
                if j < J:
                    assert j - NK not in kvtok
                    kvtok[j] = sl["kv"][j % NK].dma(pool, lambda e: e.indirect_dma_start(
                        kv[:, j % NK, :], None, kvt, bass.IndirectOffsetOnAxis(ap=sI[:, j:j + 1], axis=0)),
                        kvfree[j % NK])

            def queries(j):
                if j >= J:
                    return
                if j % 4 == 0:
                    m = min(4, J - j)

                    def lds(e):
                        r = four(vs, e, "l1s")
                        e.load(r[:m], irow[0:1, j:j + m])
                        vs["b"] = [e.snap(x, min_val=0, max_val=NB - 1) for x in r[:m]]
                        r = four(vs.setdefault("B", {}), e, "l1t")
                        e.load(r[:m], irow[32:33, j:j + m])
                        vs["s"] = [e.snap(x, min_val=0, max_val=NQ - 1) for x in r[:m]]
                        r = four(vs.setdefault("C", {}), e, "l1u")
                        e.load(r[:m], irow[64:65, j:j + m])
                        vs["n"] = [e.snap(x, min_val=0, max_val=1) for x in r[:m]]
                    sp.do(lds)
                qtok[j] = sl["q"][j % NQ].dma(sp, lambda e: e.dma_start(
                    qb[:, bass.ds(vs["s"][j % 4], 1), :].rearrange("p a d -> p (a d)"),
                    qt[bass.ds(vs["b"][j % 4] * P, P), :], cond=vs["n"][j % 4],
                    bounds_check="skip_entire_dma"), qdone.get(j - NQ))

            def expand(q):
                if q >= NQ2:
                    return
                if q % 2 == 0:
                    def ldp(e):
                        r = four(vp, e, "l1p")
                        e.load(r[:4], irow[32:33, 2 * q:2 * q + 4])
                        vp["s"] = [e.snap(x, min_val=0, max_val=NQ - 1) for x in r[:4]]
                    pe.do(ldp)
                for j in (2 * q, 2 * q + 1):
                    qetok[q] = qdone[j] = pe.op(lambda e, j=j: e.matmul(
                        psum[1 + q % 2][:, j % 2 * D:j % 2 * D + D], lhsT=OT[:, j % NT, :],
                        rhs=qb[:, bass.ds(vp["s"][j % 4], 1), :].rearrange("p a d -> p (a d)"), start=True,
                        stop=True), otok[j // 4], qtok[j], qefree[q % 2])

            def product(w, c):
                q = w * W // 2 + c
                j = 2 * q
                if j >= J:
                    return
                for k in range(j + AHEAD, j + AHEAD + 2):
                    gather(k)
                s = j % NK
                S["prod"] = qefree[q % 2] = dve.op(lambda e: e.tensor_tensor(
                    prod[:, q % 2, :, :], psum[1 + q % 2][:, :].rearrange("p (a d) -> p a d", a=2),
                    kv[:, s:s + 2, 0:D], ALU.mult), qetok.pop(q), kvtok[j], kvtok[j + 1], prodfree[q % 2])

            def reduce(w, c):
                q = w * W // 2 + c
                if 2 * q >= J:
                    return
                r = prodfree[q % 2] = dve.op(lambda e: e.tensor_reduce(
                    sims[:, w % 2, :, 2 * c:2 * c + 2].rearrange("p h i -> p i h"),
                    prod[:, q % 2, :, :].rearrange("p a (h d) -> p a h d", h=NH), AX.X,
                    ALU.add), S["prod"], simfree.get(w - 2))
                if 2 * q + 2 == J and J % W:
                    r = dve.op(lambda e: e.memset(sims[:, w % 2, :, J % W:W], 0.0), r)
                simtok[w] = r

            def rows(w):
                n = min(W, J - w * W)
                for k in range(0, n, 4):
                    js = range(w * W + k, w * W + k + 4)
                    o = act.op(lambda e, k=k: e.copy(Of[:, (w * W + k) % NOF:(w * W + k) % NOF + 4, :],
                                                     Ob[:, w % 2, k:k + 4, :]), obtok[w], *(ofree[j % NOF] for j in js))
                    for j in js:
                        oftok[j] = o
                obfree[w % 2] = o

            def softmax(w):
                n = min(W, J - w * W)
                j0 = w * W
                fb = act.op(lambda e: e.activation(FB[:, :, :], bcast(FT[:, j0:j0 + W], NH), ACT.Copy,
                                                     scale=-BIG), S.get("tf"))
                d1 = act.op(lambda e: e.activation(D0[:, 0, :, 1:W], bcast(link[:, j0 + 1:j0 + W], NH), ACT.Copy,
                                                     scale=-BIG), S.get("scan"), S["d0"])
                d2 = act.op(lambda e: e.activation(D0[:, 1, :, 0:W - 1], bcast(link[:, j0 + 1:j0 + W], NH),
                                                     ACT.Copy, scale=-BIG))
                d3 = act.op(lambda e: e.activation(cut[:, :], link[:, j0:j0 + 1], ACT.Copy, scale=-BIG), S.get("al"))
                tf = S["tf"] = pe.op(lambda e: e.transpose(psum[3][0:64, P:2 * P],
                                                           FB[:, :, :].rearrange("p a b -> p (a b)"), ident[:, :]),
                                     fb, S.get("d"))
                yield
                ts = pe.op(lambda e: e.transpose(psum[3][0:64, 0:P],
                                                 sims[:, w % 2, :, :].rearrange("p a b -> p (a b)"), ident[:, :]),
                           simtok[w])
                fs = act.op(lambda e: e.copy(FS[:, :], psum[3][0:64, P:2 * P]), tf, ts, S.get("pm"))
                yield
                pm = S["pm"] = dve.op(lambda e: e.tensor_tensor_scan(PM[:, :], FS[:, :], psum[3][0:64, 0:P], 0.0,
                                                                     ALU.add, ALU.max), fs, ts, S.get("tb"))
                tb = S["tb"] = pe.op(lambda e: e.transpose(psum[3][:, 2 * P:2 * P + 64], PM[:, :],
                                                           ident[0:64, 0:64]), pm)
                l2 = act.op(lambda e: e.copy(PL[:, :, NH], LT[:, j0:j0 + W]), S.get("m9"))
                yield
                pl = dve.op(lambda e: e.tensor_tensor(
                    PL[:, :, 0:NH].rearrange("p j h -> p h j"),
                    psum[3][:, 2 * P:2 * P + 64].rearrange("p (h j) -> p h j", h=NH),
                    bcast(LT[:, j0:j0 + W], NH), ALU.mult), tb, S.get("m9"))
                for i in range(n):
                    m9 = pe.op(lambda e, i=i: e.matmul(psum[3][:, 320 + i * 9:320 + (i + 1) * 9], lhsT=Of[:, (j0 + i) % NOF, :],
                                                       rhs=PL[:, i, :], start=True, stop=True),
                               pl, l2, oftok[j0 + i], S.get("d"))
                S["m9"] = m9
                yield
                v9 = psum[3][:, 320:320 + W * 9].rearrange("p (j k) -> p j k", k=9)
                ab = dve.op(lambda e: e.tensor_scalar(absent[:, 0:n], v9[:, 0:n, NH], BIG, -BIG, ALU.mult, ALU.add),
                            m9)
                if n < W:
                    ab = dve.op(lambda e: e.memset(val[:, :, :], 0.0), ab)
                yield
                v = dve.op(lambda e: e.tensor_tensor(
                    val[:, :, 0:n], v9[:, 0:n, 0:NH].rearrange("p j h -> p h j"), bcast(absent[:, 0:n], NH),
                    ALU.add), ab, S.get("scan"))
                S["val"] = v
                yield
                v = dve.op(lambda e: e.scalar_tensor_tensor(
                    out=val[:, :, 0], in0=carry[:, :], scalar=cut[:, :], in1=val[:, :, 0], op0=ALU.add,
                    op1=ALU.max), v, S["carry"], d3)
                yield
                f = dve.op(lambda e: e.tensor_tensor_scan(
                    fw[:, :, :].rearrange("p a b -> p (a b)"), D0[:, 0, :, :].rearrange("p a b -> p (a b)"),
                    val[:, :, :].rearrange("p a b -> p (a b)"), 0.0, ALU.add, ALU.max), v, d1)
                yield
                r = S["scan"] = dve.op(lambda e: e.tensor_tensor_scan(
                    ref[:, :, :].rearrange("p a b -> p (a b)")[:, ::-1],
                    D0[:, 1, :, :].rearrange("p a b -> p (a b)")[:, ::-1],
                    fw[:, :, :].rearrange("p a b -> p (a b)")[:, ::-1], 0.0, ALU.add, ALU.max), f, d2, S.get("me"))
                for i in range(n):
                    me = pe.op(lambda e, i=i: e.matmul(psum[3][:, 392 + i * NH:392 + (i + 1) * NH],
                                                       lhsT=OT[:, (j0 + i) % NT, :], rhs=ref[:, :, i], start=True,
                                                       stop=True), r, S.get("d"))
                metok[w] = S["me"] = me
                yield
                al = S["al"] = dve.op(lambda e: e.scalar_tensor_tensor(
                    out=alpha[:, 0, :], in0=carry[:, :], scalar=cut[:, :], in1=ref[:, :, 0], op0=ALU.add,
                    op1=ALU.subtract), r, S.get("ex"))
                ex = S["ex"] = act.op(lambda e: e.activation(alpha[:, 1, :], alpha[:, 0, :], ACT.Exp, scale=SCALE),
                                      al, S.get("resc"))
                S["carry"] = dve.op(lambda e: e.tensor_copy(carry[:, :], ref[:, :, n - 1]), al)
                yield
                d = S["d"] = simfree[w] = dve.op(lambda e: e.tensor_tensor(
                    dd[:, :, 0:n], sims[:, w % 2, :, 0:n],
                    psum[3][:, 392:392 + n * NH].rearrange("p (j h) -> p h j", h=NH), ALU.subtract), me,
                    S.get("pp"))
                S["pp"] = act.op(lambda e: e.activation(pp[:, w % 2, :, 0:n], dd[:, :, 0:n], ACT.Exp, scale=SCALE),
                                 d, S.get(f"ppf{w % 2}"), S.get(f"ppd{w % 2}"))
                yield

            def sums(w):
                n = min(W, J - w * W)
                utok, weighed = {}, {}

                def load(i):
                    def ld(e):
                        r = four(vd, e, "l1d")
                        e.load(r[:4], irow[0:1, w * W + i:w * W + i + 4])
                        vd["v"] = [e.snap(x, min_val=0, max_val=NB - 1) for x in r[:4]]
                    dve.do(ld)

                def rescale(e):
                    t = acc[:, bass.ds(vd["v"][0], 1), :, :].rearrange("p a h d -> p (a h) d")
                    return e.tensor_tensor(t, t, alpha[:, 1, :].rearrange("p (h a) -> p h a", a=1)
                                           .to_broadcast([P, NH, 33]), ALU.mult)

                def weigh(c):
                    i = 2 * c
                    j = w * W + i
                    if c % 2 == 0:
                        for k in range(2):
                            p = kvfree[(j + k) % NK] = pool.op(lambda e, k=k: e.tensor_tensor(
                                pv[:, (j + k) % 4, :].rearrange("p (h d) -> p h d", h=NH),
                                kv[:, (j + k) % NK, D:KVW].rearrange("p (h d) -> p h d", h=NH),
                                pp[:, w % 2, :, i + k:i + k + 1].to_broadcast([P, NH, 33]), ALU.mult),
                                S["pp"], ufull[(j + k) % 4], kvtok.pop(j + k))
                            weighed[i + k] = p
                        S[f"ppf{w % 2}"] = p
                    elif c == 3:
                        for k in range(2):
                            t = kvtok.pop(j + k)
                            for h in range(NH):
                                p = act.op(lambda e, k=k, h=h: e.activation(
                                    pv[:, (j + k) % 4, h * 33:h * 33 + 33],
                                    kv[:, (j + k) % NK, D + h * 33:D + h * 33 + 33], ACT.Copy,
                                    scale=pp[:, w % 2, h, i + k:i + k + 1]), S["pp"], ufull[(j + k) % 4], t)
                            weighed[i + k] = kvfree[(j + k) % NK] = p
                        S[f"ppd{w % 2}"] = p
                    else:
                        p = kvfree[j % NK] = kvfree[(j + 1) % NK] = dve.op(lambda e: e.tensor_tensor(
                            pv[:, j % 4:j % 4 + 2, :].rearrange("p a (h d) -> p a h d", h=NH),
                            kv[:, j % NK:j % NK + 2, D:KVW].rearrange("p a (h d) -> p a h d", h=NH),
                            pp[:, w % 2, :, i:i + 2].rearrange("p h (a b) -> p a h b", b=1)
                            .to_broadcast([P, 2, NH, 33]), ALU.mult),
                            S["pp"], ufull[j % 4], ufull[(j + 1) % 4], kvtok.pop(j), kvtok.pop(j + 1))
                        for k in range(2):
                            weighed[i + k] = p
                        S[f"ppd{w % 2}"] = p

                def product(c):
                    for i in (2 * c, 2 * c + 1):
                        j = w * W + i
                        utok[i] = ufull[j % 4] = ofree[j % NOF] = pe.op(lambda e, j=j: e.matmul(
                            psum[4 + j % 4][:, 0:NH * 33], lhsT=Of[:, j % NOF, :], rhs=pv[:, j % 4, :], start=True,
                            stop=True), weighed.pop(i), ufree[j % 4])

                def add(i):
                    j = w * W + i
                    if i == 4:
                        load(4)

                    def fn(e):
                        t = acc[:, bass.ds(vd["v"][i % 4], 1), :, :].rearrange("p a h d -> p (a h d)")
                        return e.tensor_tensor(t, t, psum[4 + j % 4][:, 0:NH * 33], ALU.add)
                    S["acc"] = ufree[j % 4] = dve.op(fn, utok.pop(i), S["acc"])

                def begin():
                    load(0)
                    S["acc"] = S["resc"] = dve.op(rescale, S["ex"], S.get("acc"))

                def step(k):
                    c = int(k[1:] or 0)
                    if k == "R":
                        begin()
                    elif 2 * c < n and k[0] in "pv":
                        weigh(c)
                    elif 2 * c < n and k[0] == "u":
                        product(c)
                    elif c < n and k[0] == "a":
                        add(c)
                return step

            for j in range(AHEAD):
                gather(j)
            for j in range(4):
                queries(j)
            onehots(0)
            columns(0)
            columns(4)
            expand(0)
            expand(1)
            for j in range(4, 8):
                queries(j)
            soft = iter(())
            two = None
            for w in range(NW + 2):
                for k in PERIOD:
                    c = int(k[-1]) if k[-1].isdigit() else 0
                    if k == "x":
                        next(soft, None)
                    elif k == "new":
                        assert next(soft, 1) == 1
                        soft = softmax(w) if w < NW else iter(())
                        next(soft, None)
                    elif k[0] in "ua" or k in ("p2", "v3"):
                        if two:
                            two(k)
                    elif k in ("R", "p0", "v1"):
                        if k == "p0":
                            two = sums(w - 1) if 1 <= w <= NW else None
                        if two:
                            two(k)
                    elif w < NW:
                        if k[:4] == "prod":
                            product(w, c)
                        elif k[:3] == "red":
                            reduce(w, c)
                        elif k[0] == "e":
                            q = w * W // 2 + c + 2
                            expand(q)
                            queries(2 * q + 4)
                            queries(2 * q + 5)
                        elif k == "of":
                            rows(w)
                        elif w + 1 < NW:
                            if k == "oh":
                                onehots(w + 1)
                            elif k[0] == "k":
                                columns(w * W + W + c)
            assert next(soft, 1) == 1
            S_acc = S["acc"]

            w = sl["w"]
            wraw = kv[:, 0:1, 0:2 * D].rearrange("p a (b d) -> p (a b) d", b=2)
            wot = kv[:, 1:2, 0:2 * D].rearrange("p a (b d) -> p (a b) d", b=2)
            bias = kv[:, 2, 0:D]
            l = w[0].dma(sp, lambda e: e.dma_start(wraw, Wo.rearrange("(a p) d -> p a d", p=P)), *kvfree)
            bt = w[1].dma(sp, lambda e: e.dma_start(
                bias, bo.rearrange("(a d) -> a d", a=1).to_broadcast([P, D])))
            c = None
            for a in range(2):
                for b in range(2):
                    t = pe.op(lambda e, a=a, b=b: e.transpose(psum[0][:, 0:P], wraw[:, a, b * P:(b + 1) * P],
                                                              ident[:, :]), l, c, S["otp"])
                    c = act.op(lambda e, a=a, b=b: e.copy(wot[:, b, a * P:(a + 1) * P], psum[0][:, 0:P]), t,
                               *kvfree)
            t_wo = c
            rs = sI[:, 0:NB * NH].bitcast(F32).rearrange("p (b h) -> p b h", h=NH)
            a = dve.op(lambda e: e.tensor_scalar(rs, acc[:, :, :, 32], 1e-30, None, ALU.max), S_acc)
            t_rs = dve.op(lambda e: e.reciprocal(rs, rs), a)
            for q in (dve, act, sp):
                q.waits(kvfree)
            UB = (3, 6, 7)
            pe.waits([*qefree, *ufree, S["d"]])
            bank = {k: None for k in range(1, 8)}
            otfr, oTfr, xf = [None] * 3, [None] * 3, [None] * 6
            l, a, t, c, m, a2 = ({} for _ in range(6))
            ot = lambda b: kv[:, 3 + b % 3, 0:D]
            oT = lambda b: kv[:, 6 + b % 3, 0:D]
            xt = lambda b: kv[:, 9 + b % 6, 0:D]

            def o_load(b):
                l[b] = sl["x"][b % 6].dma(sp, lambda e: e.dma_start(xt(b), x1t[b * P:(b + 1) * P, :]), xf[b % 6])

            def o_scale(b):
                a[b] = dve.op(lambda e: e.tensor_tensor(
                    ot(b).rearrange("p (h d) -> p h d", h=NH), acc[:, b, :, 0:32],
                    rs[:, b, :].rearrange("p (h a) -> p h a", a=1).to_broadcast([P, NH, 32]), ALU.mult),
                    t_rs, otfr[b % 3])

            def o_turn(b):
                k = 1 + b % 2
                for f in range(2):
                    t[b] = otfr[b % 3] = pe.op(lambda e, f=f: e.transpose(
                        psum[k][:, f * P:(f + 1) * P], ot(b)[:, f * P:(f + 1) * P], ident[:, :]), a[b], bank[k])
                c[b] = bank[k] = act.op(lambda e: e.copy(oT(b), psum[k][:, 0:D]), t[b], oTfr[b % 3])

            def o_product(b):
                k = UB[b % 3]
                for f in range(2):
                    m[b] = oTfr[b % 3] = pe.op(lambda e, f=f: e.matmul(
                        psum[k][:, 0:D], lhsT=oT(b)[:, f * P:(f + 1) * P], rhs=wot[:, f, :], start=(f == 0),
                        stop=(f == 1)), c[b], t_wo, bank[k])
                a2[b] = dve.op(lambda e: e.tensor_tensor(xt(b), xt(b), bias, ALU.add), l[b], bt)

            def o_out(b):
                k = UB[b % 3]
                n = P if b < NB - 1 else NLAST
                z = bank[k] = dve.op(lambda e: e.tensor_tensor(xt(b), xt(b), psum[k][:, 0:D], ALU.add), a2[b], m[b])
                xf[b % 6] = sl["o"][b % 6].dma(sp, lambda e: e.dma_start(out[b * P:b * P + n, :], xt(b)[0:n, :]), z)
            pipeline([o_load, lambda b: None, o_scale, o_turn, o_product, o_out], NB)
            sp.waits(xf)

        phase("l1", l1, {"gen": 1, "fg": 2, "kv": 22, "q": 4, "w": 2, "x": 6, "o": 6})


_INS = ["x", "src", "dst", "edge_weight", "L0_gnn_weight", "L1_gnn_Wq", "L1_gnn_bq", "L1_gnn_Wk", "L1_gnn_bk",
        "L1_gnn_Wv", "L1_gnn_bv", "L1_gnn_Wo", "L1_gnn_bo"]


def kernel(**inputs):
    import numpy as _np
    import concourse.bacc as _bacc
    from concourse import mybir as _mybir
    from concourse.bass_utils import run_bass_kernel_spmd as _run

    nc = _bacc.Bacc("TRN2", target_bir_lowering=False, num_devices=1)
    arrays, args = {}, []
    for name in _INS:
        a = _np.ascontiguousarray(inputs[name])
        arrays[f"in_{name}"] = a
        args.append(nc.dram_tensor(f"in_{name}", a.shape, _mybir.dt.from_np(a.dtype), kind="ExternalInput").ap())
    out = nc.dram_tensor("out_0", (N, D), F32, kind="ExternalOutput").ap()
    build(nc, *args, out)
    r = _run(nc, [arrays], core_ids=[0])
    return r.results[0]["out_0"]
```
